# Optimizing a Trainium2 kernel written in Bass

```python
import numpy as np
import jax
import jax.numpy as jnp

def _softmax(x, axis=-1):
    return jax.nn.softmax(x, axis=axis)

def _gelu(x):
    return jax.nn.gelu(x, approximate=True)

def _silu(x):
    return jax.nn.silu(x)

def _sigmoid(x):
    return jax.nn.sigmoid(x)

def _layernorm(x, axis=-1, eps=1e-05):
    m = jnp.mean(x, axis=axis, keepdims=True)
    v = jnp.var(x, axis=axis, keepdims=True)
    return (x - m) / jnp.sqrt(v + eps)

def _scatter_add(tgt, idx, src, axis=0):
    return tgt.at[idx].add(src)

def _segment_sum(src, seg, n):
    return jax.ops.segment_sum(src, seg, n)
kernel_name = 'mk_hybrid_d2_jaxref_r4_c755e7'

def setup_inputs(seed: int=0):
    np.random.seed(seed)
    _w = jnp.asarray

    def _L0_attn_a_setup():
        import jax, jax.numpy as jnp
        import numpy as np
        from jax import lax
        D_MODEL = 256
        D_STATE = 16
        D_CONV = 4
        EXPAND = 2
        D_INNER = EXPAND * D_MODEL
        DT_RANK = (D_MODEL + 15) // 16
        LN_EPS = 1e-05

        def _mamba_block(x, ln_g, ln_b, W_in, conv_w, conv_b, W_xproj, W_dt, b_dt, A_log, D, W_out):
            B, L, _ = x.shape
            mu = jnp.mean(x, axis=-1, keepdims=True)
            var = jnp.var(x, axis=-1, keepdims=True)
            h = (x - mu) * lax.rsqrt(var + LN_EPS) * ln_g + ln_b
            xz = jnp.einsum('bld,de->ble', h, W_in)
            u, z = jnp.split(xz, 2, axis=-1)
            u_t = jnp.transpose(u, (0, 2, 1))
            u_t = lax.conv_general_dilated(u_t, conv_w, window_strides=(1,), padding=[(D_CONV - 1, 0)], feature_group_count=D_INNER, dimension_numbers=('NCH', 'OIH', 'NCH'))
            u_t = u_t + conv_b[None, :, None]
            u = jax.nn.silu(jnp.transpose(u_t, (0, 2, 1)))
            x_dbl = jnp.einsum('bld,de->ble', u, W_xproj)
            dt, Bm, Cm = jnp.split(x_dbl, [DT_RANK, DT_RANK + D_STATE], axis=-1)
            dt = jax.nn.softplus(jnp.einsum('blr,rd->bld', dt, W_dt) + b_dt)
            A = -jnp.exp(A_log)
            dA = jnp.exp(jnp.einsum('bld,dn->bldn', dt, A))
            dBu = jnp.einsum('bld,bln->bldn', dt * u, Bm)

            def step(hc, inp):
                dA_t, dBu_t, C_t = inp
                hc = dA_t * hc + dBu_t
                y_t = jnp.einsum('bdn,bn->bd', hc, C_t)
                return (hc, y_t)
            h0 = jnp.zeros((B, D_INNER, D_STATE), x.dtype)
            xs = (jnp.transpose(dA, (1, 0, 2, 3)), jnp.transpose(dBu, (1, 0, 2, 3)), jnp.transpose(Cm, (1, 0, 2)))
            _, ys = lax.scan(step, h0, xs)
            y = jnp.transpose(ys, (1, 0, 2)) + u * D
            y = y * jax.nn.silu(z)
            out = jnp.einsum('bld,dm->blm', y, W_out)
            return x + out
        key = jax.random.key(seed)
        ks = jax.random.split(key, 12)
        s = 0.02
        x = jax.random.normal(ks[0], (2, 512, D_MODEL), dtype=jnp.float32)
        params = {'x': x, 'ln_g': jnp.ones((D_MODEL,), jnp.float32), 'ln_b': jnp.zeros((D_MODEL,), jnp.float32), 'W_in': jax.random.normal(ks[1], (D_MODEL, 2 * D_INNER), jnp.float32) * s, 'conv_w': jax.random.normal(ks[2], (D_INNER, 1, D_CONV), jnp.float32) * 0.2, 'conv_b': jnp.zeros((D_INNER,), jnp.float32), 'W_xproj': jax.random.normal(ks[3], (D_INNER, DT_RANK + 2 * D_STATE), jnp.float32) * s, 'W_dt': jax.random.normal(ks[4], (DT_RANK, D_INNER), jnp.float32) * 0.1, 'b_dt': jax.random.normal(ks[5], (D_INNER,), jnp.float32) * 0.1, 'A_log': jnp.log(jnp.tile(jnp.arange(1.0, D_STATE + 1.0, dtype=jnp.float32), (D_INNER, 1))), 'D': jnp.ones((D_INNER,), jnp.float32), 'W_out': jax.random.normal(ks[6], (D_INNER, D_MODEL), jnp.float32) * s}
        return params
    _L0_attn_a_in = _L0_attn_a_setup()

    def _L0_attn_b_setup():
        import jax, jax.numpy as jnp
        import numpy as np
        B, T, C = (8, 1024, 256)
        LN_EPS = 1e-05
        NEG_INF = -1e+38

        def _ln(x, g, b):
            mu = jnp.mean(x, axis=-1, keepdims=True)
            var = jnp.mean(jnp.square(x - mu), axis=-1, keepdims=True)
            return (x - mu) * jax.lax.rsqrt(var + LN_EPS) * g + b

        def _shift(x):
            return jnp.concatenate([jnp.zeros_like(x[:, :1]), x[:, :-1]], axis=1)

        def _wkv(w, u, k, v):
            kt = jnp.moveaxis(k, 1, 0)
            vt = jnp.moveaxis(v, 1, 0)
            aa = jnp.zeros(k.shape[::2], k.dtype)
            bb = jnp.zeros(k.shape[::2], k.dtype)
            pp = jnp.full(k.shape[::2], NEG_INF, k.dtype)

            def step(carry, kv):
                aa, bb, pp = carry
                kk, vv = kv
                p = jnp.maximum(pp, u + kk)
                e1 = jnp.exp(pp - p)
                e2 = jnp.exp(u + kk - p)
                y = (e1 * aa + e2 * vv) / (e1 + e2)
                p2 = jnp.maximum(pp + w, w + kk)
                e1u = jnp.exp(pp + w - p2)
                e2u = jnp.exp(w + kk - p2)
                aa = e1u * aa + e2u * vv
                bb = e1u + e2u
                pp = p2 + jnp.log(bb)
                return ((aa, bb, pp), y)
            _, ys = jax.lax.scan(step, (aa, bb, pp), (kt, vt))
            return jnp.moveaxis(ys, 0, 1)
        key = jax.random.key(seed)
        ks = jax.random.split(key, 20)
        n = lambda i, sh, s=1.0: jax.random.normal(ks[i], sh, jnp.float32) * s
        un = lambda i, sh: jax.random.uniform(ks[i], sh, jnp.float32)
        return {'x': n(0, (B, T, C)), 'w': n(1, (C,), 0.01), 'u': n(2, (C,), 0.01), 'rk': un(3, (C,)), 'rv': un(4, (C,)), 'rr': un(5, (C,)), 'crk': un(6, (C,)), 'crr': un(7, (C,)), 'Wk': n(8, (C, C), 0.02), 'Wv': n(9, (C, C), 0.02), 'Wr': n(10, (C, C), 0.02), 'Wck': n(11, (4 * C, C), 0.02), 'Wcv': n(12, (C, 4 * C), 0.02), 'Wcr': n(13, (C, C), 0.02), 'ln1_g': jnp.ones((C,)), 'ln1_b': jnp.zeros((C,)), 'ln2_g': jnp.ones((C,)), 'ln2_b': jnp.zeros((C,))}
    _L0_attn_b_in = _L0_attn_b_setup()

    def _L0_ffn_setup():
        import jax, jax.numpy as jnp
        import numpy as np
        import math
        B, S, H, I, E = (4, 512, 256, 1024, 8)
        TOP_K = 2
        CAPACITY_FACTOR = 1.25
        key = jax.random.key(seed)
        k1, k2, k3, k4, k5 = jax.random.split(key, 5)
        x = jax.random.normal(k1, (B, S, H), dtype=jnp.float32)
        W_router = jax.random.normal(k2, (E, H), dtype=jnp.float32) * (1.0 / math.sqrt(H))
        b_router = jnp.zeros((E,), dtype=jnp.float32)
        experts_inter = jax.random.normal(k3, (E, H, I), dtype=jnp.float32) * 0.02
        experts_out = jax.random.normal(k4, (E, I, H), dtype=jnp.float32) * 0.02
        return {'x': x, 'W_router': W_router, 'b_router': b_router, 'experts_inter': experts_inter, 'experts_out': experts_out}
    _L0_ffn_in = _L0_ffn_setup()

    def _L1_attn_a_setup():
        import jax, jax.numpy as jnp
        import numpy as np
        EPS = 1e-06

        def rmsnorm(x, w):
            rms = jnp.sqrt(jnp.mean(x * x, axis=-1, keepdims=True) + EPS)
            return w * x / rms
        key = jax.random.key(seed)
        ks = jax.random.split(key, 12)
        B, L, D, S, E, H = (2, 512, 256, 16, 4, 512)
        x = jax.random.normal(ks[0], (B, L, D), jnp.float32)
        A_log = jnp.log(jax.random.uniform(ks[1], (D, S), jnp.float32) * 0.5 + 0.5)
        D_param = jnp.ones((D,), jnp.float32)
        W_delta = jax.random.normal(ks[2], (D, D), jnp.float32) * 0.02
        b_delta = jnp.zeros((D,), jnp.float32)
        W_B = jax.random.normal(ks[3], (D, S), jnp.float32) * 0.02
        W_C = jax.random.normal(ks[4], (D, S), jnp.float32) * 0.02
        W_router = jax.random.normal(ks[5], (D, E), jnp.float32) * 0.02
        Wg = jax.random.normal(ks[6], (E, D, H), jnp.float32) * 0.02
        Wu = jax.random.normal(ks[7], (E, D, H), jnp.float32) * 0.02
        Wd = jax.random.normal(ks[8], (E, H, D), jnp.float32) * 0.02
        wn_exp = jnp.ones((E, H), jnp.float32)
        norm_w = jnp.ones((D,), jnp.float32)
        return dict(x=x, A_log=A_log, D_param=D_param, W_delta=W_delta, b_delta=b_delta, W_B=W_B, W_C=W_C, W_router=W_router, Wg=Wg, Wu=Wu, Wd=Wd, wn_exp=wn_exp, norm_w=norm_w)
    _L1_attn_a_in = _L1_attn_a_setup()

    def _L1_attn_b_setup():
        import jax, jax.numpy as jnp
        import numpy as np
        import math
        B, S, E = (2, 512, 256)
        H, DC, DR = (16, 64, 128)
        HD = E // H

        def _linear_params(key, din, dout):
            k1, k2 = jax.random.split(key)
            bound = 1.0 / math.sqrt(din)
            w = jax.random.uniform(k1, (din, dout), minval=-bound, maxval=bound, dtype=jnp.float32)
            b = jax.random.uniform(k2, (dout,), minval=-bound, maxval=bound, dtype=jnp.float32)
            return (w, b)

        def _gelu(x):
            return jax.nn.gelu(x, approximate=False)

        def _rope_cos_sin(seq_len, d_rope):
            inv_freq = 1.0 / 10000.0 ** (jnp.arange(0, d_rope, 2, dtype=jnp.float32) / d_rope)
            t = jnp.arange(seq_len, dtype=jnp.float32)
            freqs = t[:, None] * inv_freq[None, :]
            emb = jnp.concatenate([freqs, freqs], axis=-1)
            return (jnp.cos(emb), jnp.sin(emb))

        def _apply_rope(x, cos, sin):
            d = x.shape[-1]
            x1, x2 = (x[..., :d // 2], x[..., d // 2:])
            rot = jnp.concatenate([-x2, x1], axis=-1)
            return x * cos + rot * sin
        key = jax.random.key(seed)
        ks = jax.random.split(key, 10)
        x = jax.random.normal(ks[0], (B, S, E), dtype=jnp.float32)
        wq, bq = _linear_params(ks[1], E, DC)
        wqc, bqc = _linear_params(ks[2], DC, E - DR)
        wqr, bqr = _linear_params(ks[3], E, DR)
        wkv, bkv = _linear_params(ks[4], E, DC)
        wkr, bkr = _linear_params(ks[5], E, DR)
        wkc, bkc = _linear_params(ks[6], DC, E - DR)
        wv, bv = _linear_params(ks[7], DC, E)
        wo, bo = _linear_params(ks[8], E, E)
        return dict(x=x, wq=wq, bq=bq, wqc=wqc, bqc=bqc, wqr=wqr, bqr=bqr, wkv=wkv, bkv=bkv, wkr=wkr, bkr=bkr, wkc=wkc, bkc=bkc, wv=wv, bv=bv, wo=wo, bo=bo)
    _L1_attn_b_in = _L1_attn_b_setup()

    def _L1_ffn_setup():
        import jax, jax.numpy as jnp
        import numpy as np
        B, S, D = (2, 512, 256)
        E, K, F = (16, 2, 128)
        FS = 256
        key = jax.random.key(seed)
        ks = jax.random.split(key, 8)

        def w(k, shape, fan_in):
            return jax.random.normal(k, shape, jnp.float32) / np.sqrt(fan_in).astype(np.float32)
        return {'x': jax.random.normal(ks[0], (B, S, D), jnp.float32), 'Wr': w(ks[1], (D, E), D), 'Wg': w(ks[2], (E, D, F), D), 'Wu': w(ks[3], (E, D, F), D), 'Wd': w(ks[4], (E, F, D), F), 'Sg': w(ks[5], (D, FS), D), 'Su': w(ks[6], (D, FS), D), 'Sd': w(ks[7], (FS, D), FS)}
    _L1_ffn_in = _L1_ffn_setup()
    _d = {'L0_attn_a_x': _L0_attn_a_in['x'], 'L0_attn_a_ln_g': _L0_attn_a_in['ln_g'], 'L0_attn_a_ln_b': _L0_attn_a_in['ln_b'], 'L0_attn_a_W_in': _L0_attn_a_in['W_in'], 'L0_attn_a_conv_w': _L0_attn_a_in['conv_w'], 'L0_attn_a_conv_b': _L0_attn_a_in['conv_b'], 'L0_attn_a_W_xproj': _L0_attn_a_in['W_xproj'], 'L0_attn_a_W_dt': _L0_attn_a_in['W_dt'], 'L0_attn_a_b_dt': _L0_attn_a_in['b_dt'], 'L0_attn_a_A_log': _L0_attn_a_in['A_log'], 'L0_attn_a_D': _L0_attn_a_in['D'], 'L0_attn_a_W_out': _L0_attn_a_in['W_out'], 'L0_attn_b_w': _L0_attn_b_in['w'], 'L0_attn_b_u': _L0_attn_b_in['u'], 'L0_attn_b_rk': _L0_attn_b_in['rk'], 'L0_attn_b_rv': _L0_attn_b_in['rv'], 'L0_attn_b_rr': _L0_attn_b_in['rr'], 'L0_attn_b_crk': _L0_attn_b_in['crk'], 'L0_attn_b_crr': _L0_attn_b_in['crr'], 'L0_attn_b_Wk': _L0_attn_b_in['Wk'], 'L0_attn_b_Wv': _L0_attn_b_in['Wv'], 'L0_attn_b_Wr': _L0_attn_b_in['Wr'], 'L0_attn_b_Wck': _L0_attn_b_in['Wck'], 'L0_attn_b_Wcv': _L0_attn_b_in['Wcv'], 'L0_attn_b_Wcr': _L0_attn_b_in['Wcr'], 'L0_attn_b_ln1_g': _L0_attn_b_in['ln1_g'], 'L0_attn_b_ln1_b': _L0_attn_b_in['ln1_b'], 'L0_attn_b_ln2_g': _L0_attn_b_in['ln2_g'], 'L0_attn_b_ln2_b': _L0_attn_b_in['ln2_b'], 'L0_ffn_W_router': _L0_ffn_in['W_router'], 'L0_ffn_b_router': _L0_ffn_in['b_router'], 'L0_ffn_experts_inter': _L0_ffn_in['experts_inter'], 'L0_ffn_experts_out': _L0_ffn_in['experts_out'], 'L1_attn_a_A_log': _L1_attn_a_in['A_log'], 'L1_attn_a_D_param': _L1_attn_a_in['D_param'], 'L1_attn_a_W_delta': _L1_attn_a_in['W_delta'], 'L1_attn_a_b_delta': _L1_attn_a_in['b_delta'], 'L1_attn_a_W_B': _L1_attn_a_in['W_B'], 'L1_attn_a_W_C': _L1_attn_a_in['W_C'], 'L1_attn_a_W_router': _L1_attn_a_in['W_router'], 'L1_attn_a_Wg': _L1_attn_a_in['Wg'], 'L1_attn_a_Wu': _L1_attn_a_in['Wu'], 'L1_attn_a_Wd': _L1_attn_a_in['Wd'], 'L1_attn_a_wn_exp': _L1_attn_a_in['wn_exp'], 'L1_attn_a_norm_w': _L1_attn_a_in['norm_w'], 'L1_attn_b_wq': _L1_attn_b_in['wq'], 'L1_attn_b_bq': _L1_attn_b_in['bq'], 'L1_attn_b_wqc': _L1_attn_b_in['wqc'], 'L1_attn_b_bqc': _L1_attn_b_in['bqc'], 'L1_attn_b_wqr': _L1_attn_b_in['wqr'], 'L1_attn_b_bqr': _L1_attn_b_in['bqr'], 'L1_attn_b_wkv': _L1_attn_b_in['wkv'], 'L1_attn_b_bkv': _L1_attn_b_in['bkv'], 'L1_attn_b_wkr': _L1_attn_b_in['wkr'], 'L1_attn_b_bkr': _L1_attn_b_in['bkr'], 'L1_attn_b_wkc': _L1_attn_b_in['wkc'], 'L1_attn_b_bkc': _L1_attn_b_in['bkc'], 'L1_attn_b_wv': _L1_attn_b_in['wv'], 'L1_attn_b_bv': _L1_attn_b_in['bv'], 'L1_attn_b_wo': _L1_attn_b_in['wo'], 'L1_attn_b_bo': _L1_attn_b_in['bo'], 'L1_ffn_Wr': _L1_ffn_in['Wr'], 'L1_ffn_Wg': _L1_ffn_in['Wg'], 'L1_ffn_Wu': _L1_ffn_in['Wu'], 'L1_ffn_Wd': _L1_ffn_in['Wd'], 'L1_ffn_Sg': _L1_ffn_in['Sg'], 'L1_ffn_Su': _L1_ffn_in['Su'], 'L1_ffn_Sd': _L1_ffn_in['Sd']}
    _x0 = _d['L0_attn_a_x']
    _d['L0_attn_a_x'] = jax.random.normal(jax.random.fold_in(jax.random.key(seed), 1), (4, 1024, 256), dtype=_x0.dtype)
    del _x0
    return _d

def reference(L0_attn_a_x, L0_attn_a_ln_g, L0_attn_a_ln_b, L0_attn_a_W_in, L0_attn_a_conv_w, L0_attn_a_conv_b, L0_attn_a_W_xproj, L0_attn_a_W_dt, L0_attn_a_b_dt, L0_attn_a_A_log, L0_attn_a_D, L0_attn_a_W_out, L0_attn_b_w, L0_attn_b_u, L0_attn_b_rk, L0_attn_b_rv, L0_attn_b_rr, L0_attn_b_crk, L0_attn_b_crr, L0_attn_b_Wk, L0_attn_b_Wv, L0_attn_b_Wr, L0_attn_b_Wck, L0_attn_b_Wcv, L0_attn_b_Wcr, L0_attn_b_ln1_g, L0_attn_b_ln1_b, L0_attn_b_ln2_g, L0_attn_b_ln2_b, L0_ffn_W_router, L0_ffn_b_router, L0_ffn_experts_inter, L0_ffn_experts_out, L1_attn_a_A_log, L1_attn_a_D_param, L1_attn_a_W_delta, L1_attn_a_b_delta, L1_attn_a_W_B, L1_attn_a_W_C, L1_attn_a_W_router, L1_attn_a_Wg, L1_attn_a_Wu, L1_attn_a_Wd, L1_attn_a_wn_exp, L1_attn_a_norm_w, L1_attn_b_wq, L1_attn_b_bq, L1_attn_b_wqc, L1_attn_b_bqc, L1_attn_b_wqr, L1_attn_b_bqr, L1_attn_b_wkv, L1_attn_b_bkv, L1_attn_b_wkr, L1_attn_b_bkr, L1_attn_b_wkc, L1_attn_b_bkc, L1_attn_b_wv, L1_attn_b_bv, L1_attn_b_wo, L1_attn_b_bo, L1_ffn_Wr, L1_ffn_Wg, L1_ffn_Wu, L1_ffn_Wd, L1_ffn_Sg, L1_ffn_Su, L1_ffn_Sd):

    def _L0_attn_a_ref(x, ln_g, ln_b, W_in, conv_w, conv_b, W_xproj, W_dt, b_dt, A_log, D, W_out):
        import jax, jax.numpy as jnp
        import numpy as np
        from jax import lax
        D_MODEL = 256
        D_STATE = 16
        D_CONV = 4
        EXPAND = 2
        D_INNER = EXPAND * D_MODEL
        DT_RANK = (D_MODEL + 15) // 16
        LN_EPS = 1e-05

        def _mamba_block(x, ln_g, ln_b, W_in, conv_w, conv_b, W_xproj, W_dt, b_dt, A_log, D, W_out):
            B, L, _ = x.shape
            mu = jnp.mean(x, axis=-1, keepdims=True)
            var = jnp.var(x, axis=-1, keepdims=True)
            h = (x - mu) * lax.rsqrt(var + LN_EPS) * ln_g + ln_b
            xz = jnp.einsum('bld,de->ble', h, W_in)
            u, z = jnp.split(xz, 2, axis=-1)
            u_t = jnp.transpose(u, (0, 2, 1))
            u_t = lax.conv_general_dilated(u_t, conv_w, window_strides=(1,), padding=[(D_CONV - 1, 0)], feature_group_count=D_INNER, dimension_numbers=('NCH', 'OIH', 'NCH'))
            u_t = u_t + conv_b[None, :, None]
            u = jax.nn.silu(jnp.transpose(u_t, (0, 2, 1)))
            x_dbl = jnp.einsum('bld,de->ble', u, W_xproj)
            dt, Bm, Cm = jnp.split(x_dbl, [DT_RANK, DT_RANK + D_STATE], axis=-1)
            dt = jax.nn.softplus(jnp.einsum('blr,rd->bld', dt, W_dt) + b_dt)
            A = -jnp.exp(A_log)
            dA = jnp.exp(jnp.einsum('bld,dn->bldn', dt, A))
            dBu = jnp.einsum('bld,bln->bldn', dt * u, Bm)

            def step(hc, inp):
                dA_t, dBu_t, C_t = inp
                hc = dA_t * hc + dBu_t
                y_t = jnp.einsum('bdn,bn->bd', hc, C_t)
                return (hc, y_t)
            h0 = jnp.zeros((B, D_INNER, D_STATE), x.dtype)
            xs = (jnp.transpose(dA, (1, 0, 2, 3)), jnp.transpose(dBu, (1, 0, 2, 3)), jnp.transpose(Cm, (1, 0, 2)))
            _, ys = lax.scan(step, h0, xs)
            y = jnp.transpose(ys, (1, 0, 2)) + u * D
            y = y * jax.nn.silu(z)
            out = jnp.einsum('bld,dm->blm', y, W_out)
            return x + out
        return _mamba_block(x, ln_g, ln_b, W_in, conv_w, conv_b, W_xproj, W_dt, b_dt, A_log, D, W_out)

    def _L0_attn_b_ref(x, w, u, rk, rv, rr, crk, crr, Wk, Wv, Wr, Wck, Wcv, Wcr, ln1_g, ln1_b, ln2_g, ln2_b):
        import jax, jax.numpy as jnp
        import numpy as np
        B, T, C = (8, 1024, 256)
        LN_EPS = 1e-05
        NEG_INF = -1e+38

        def _ln(x, g, b):
            mu = jnp.mean(x, axis=-1, keepdims=True)
            var = jnp.mean(jnp.square(x - mu), axis=-1, keepdims=True)
            return (x - mu) * jax.lax.rsqrt(var + LN_EPS) * g + b

        def _shift(x):
            return jnp.concatenate([jnp.zeros_like(x[:, :1]), x[:, :-1]], axis=1)

        def _wkv(w, u, k, v):
            kt = jnp.moveaxis(k, 1, 0)
            vt = jnp.moveaxis(v, 1, 0)
            aa = jnp.zeros(k.shape[::2], k.dtype)
            bb = jnp.zeros(k.shape[::2], k.dtype)
            pp = jnp.full(k.shape[::2], NEG_INF, k.dtype)

            def step(carry, kv):
                aa, bb, pp = carry
                kk, vv = kv
                p = jnp.maximum(pp, u + kk)
                e1 = jnp.exp(pp - p)
                e2 = jnp.exp(u + kk - p)
                y = (e1 * aa + e2 * vv) / (e1 + e2)
                p2 = jnp.maximum(pp + w, w + kk)
                e1u = jnp.exp(pp + w - p2)
                e2u = jnp.exp(w + kk - p2)
                aa = e1u * aa + e2u * vv
                bb = e1u + e2u
                pp = p2 + jnp.log(bb)
                return ((aa, bb, pp), y)
            _, ys = jax.lax.scan(step, (aa, bb, pp), (kt, vt))
            return jnp.moveaxis(ys, 0, 1)
        xa = _ln(x, ln1_g, ln1_b)
        xp = _shift(xa)
        xk = xa * rk + xp * (1.0 - rk)
        xv = xa * rv + xp * (1.0 - rv)
        xr = xa * rr + xp * (1.0 - rr)
        k = jnp.einsum('btc,dc->btd', xk, Wk)
        v = jnp.einsum('btc,dc->btd', xv, Wv)
        r = jnp.einsum('btc,dc->btd', xr, Wr)
        wkv = _wkv(w, u, k, v)
        x1 = x + jax.nn.sigmoid(r) * wkv
        xb = _ln(x1, ln2_g, ln2_b)
        xpb = _shift(xb)
        xck = xb * crk + xpb * (1.0 - crk)
        xcr = xb * crr + xpb * (1.0 - crr)
        kc = jnp.square(jax.nn.relu(jnp.einsum('btc,dc->btd', xck, Wck)))
        vc = jnp.einsum('bth,dh->btd', kc, Wcv)
        out = x1 + jax.nn.sigmoid(jnp.einsum('btc,dc->btd', xcr, Wcr)) * vc
        return out

    def _L0_ffn_ref(x, W_router, b_router, experts_inter, experts_out):
        import jax, jax.numpy as jnp
        import numpy as np
        import math
        B, S, H, I, E = (4, 512, 256, 1024, 8)
        TOP_K = 2
        CAPACITY_FACTOR = 1.25
        b, s, h = x.shape
        e = experts_inter.shape[0]
        T = b * s
        capacity = math.ceil(T / e * CAPACITY_FACTOR)
        x_flat = x.reshape(T, h)
        logits = x_flat @ W_router.T + b_router
        weights_flat = jax.nn.softmax(logits, axis=-1)
        top_vals, top_idx = jax.lax.top_k(weights_flat, TOP_K)
        topk_flat = jnp.zeros_like(weights_flat).at[jnp.arange(T)[:, None], top_idx].set(top_vals)
        routing_mask = (topk_flat > 0).astype(jnp.int32)
        order = jnp.argsort(-routing_mask, axis=0, stable=True)
        sorted_mask = jnp.take_along_axis(routing_mask, order, axis=0)
        sorted_mask = sorted_mask[:capacity]
        sorted_idx = order[:capacity]
        used_tokens = (sorted_idx * sorted_mask).reshape(-1)
        mask_flat = sorted_mask.reshape(-1).astype(x.dtype)
        inputs_tokens = x_flat[used_tokens] * mask_flat[:, None]
        inputs_tokens = inputs_tokens.reshape(capacity, e, h)
        inputs_weights = jnp.take_along_axis(topk_flat, sorted_idx, axis=0)
        hmid = jnp.einsum('ceh,ehi->cei', inputs_tokens, experts_inter)
        hmid = jax.nn.relu(hmid)
        out = jnp.einsum('cei,eih->ceh', hmid, experts_out)
        out = out * inputs_weights[:, :, None]
        combined = jnp.zeros((T, h), dtype=x.dtype).at[used_tokens].add(out.reshape(-1, h))
        return combined.reshape(b, s, h)

    def _L1_attn_a_ref(x, A_log, D_param, W_delta, b_delta, W_B, W_C, W_router, Wg, Wu, Wd, wn_exp, norm_w):
        import jax, jax.numpy as jnp
        import numpy as np
        EPS = 1e-06

        def rmsnorm(x, w):
            rms = jnp.sqrt(jnp.mean(x * x, axis=-1, keepdims=True) + EPS)
            return w * x / rms
        B, L, D = x.shape
        delta = jax.nn.softplus(x @ W_delta + b_delta)
        Bm = x @ W_B
        Cm = x @ W_C
        A = -jnp.exp(A_log)
        S = A.shape[1]
        h0 = jnp.zeros((B, D, S), x.dtype)
        xs = (jnp.moveaxis(x, 1, 0), jnp.moveaxis(delta, 1, 0), jnp.moveaxis(Bm, 1, 0), jnp.moveaxis(Cm, 1, 0))

        def step(h, inp):
            x_t, d_t, B_t, C_t = inp
            bar_A = jnp.exp(jnp.minimum(d_t[..., None] * A, 10.0))
            bar_B = jnp.clip(d_t[..., None] * B_t[:, None, :], -10.0, 10.0)
            h = jnp.clip(bar_A * h + bar_B * x_t[..., None], -10000.0, 10000.0)
            y_t = jnp.sum(h * C_t[:, None, :], axis=-1) + x_t * D_param
            return (h, y_t)
        _, ys = jax.lax.scan(step, h0, xs)
        ssm_out = jnp.moveaxis(ys, 0, 1)
        flat = ssm_out.reshape(-1, D)
        probs = jax.nn.softmax(flat @ W_router, axis=-1)
        w2, idx2 = jax.lax.top_k(probs, 2)
        w2 = w2 / (jnp.sum(w2, axis=-1, keepdims=True) + 1e-09)

        def expert(xf, wg, wu, wd, wn):
            g = jax.nn.silu(xf @ wg) * (xf @ wu)
            g = rmsnorm(g, wn)
            return g @ wd
        all_out = jax.vmap(expert, in_axes=(None, 0, 0, 0, 0))(flat, Wg, Wu, Wd, wn_exp)
        tok = jnp.arange(flat.shape[0])
        moe = w2[:, 0, None] * all_out[idx2[:, 0], tok] + w2[:, 1, None] * all_out[idx2[:, 1], tok]
        out = rmsnorm(ssm_out + moe.reshape(B, L, D), norm_w)
        return out

    def _L1_attn_b_ref(x, wq, bq, wqc, bqc, wqr, bqr, wkv, bkv, wkr, bkr, wkc, bkc, wv, bv, wo, bo):
        import jax, jax.numpy as jnp
        import numpy as np
        import math
        B, S, E = (2, 512, 256)
        H, DC, DR = (16, 64, 128)
        HD = E // H

        def _linear_params(key, din, dout):
            k1, k2 = jax.random.split(key)
            bound = 1.0 / math.sqrt(din)
            w = jax.random.uniform(k1, (din, dout), minval=-bound, maxval=bound, dtype=jnp.float32)
            b = jax.random.uniform(k2, (dout,), minval=-bound, maxval=bound, dtype=jnp.float32)
            return (w, b)

        def _gelu(x):
            return jax.nn.gelu(x, approximate=False)

        def _rope_cos_sin(seq_len, d_rope):
            inv_freq = 1.0 / 10000.0 ** (jnp.arange(0, d_rope, 2, dtype=jnp.float32) / d_rope)
            t = jnp.arange(seq_len, dtype=jnp.float32)
            freqs = t[:, None] * inv_freq[None, :]
            emb = jnp.concatenate([freqs, freqs], axis=-1)
            return (jnp.cos(emb), jnp.sin(emb))

        def _apply_rope(x, cos, sin):
            d = x.shape[-1]
            x1, x2 = (x[..., :d // 2], x[..., d // 2:])
            rot = jnp.concatenate([-x2, x1], axis=-1)
            return x * cos + rot * sin
        b, s, _ = x.shape
        cq = _gelu(x @ wq + bq)
        q_c = cq @ wqc + bqc
        q_r = x @ wqr + bqr
        ckv = _gelu(x @ wkv + bkv)
        k_r = x @ wkr + bkr
        k_c = ckv @ wkc + bkc
        v = (ckv @ wv + bv).reshape(b, s, H, HD).transpose(0, 2, 1, 3)
        cos, sin = _rope_cos_sin(s, DR)
        q_r = _apply_rope(q_r, cos, sin)
        k_r = _apply_rope(k_r, cos, sin)
        q = _gelu(jnp.concatenate([q_c, q_r], axis=-1)).reshape(b, s, H, HD).transpose(0, 2, 1, 3)
        k = _gelu(jnp.concatenate([k_c, k_r], axis=-1)).reshape(b, s, H, HD).transpose(0, 2, 1, 3)
        scale = 1.0 / math.sqrt(HD)
        scores = jnp.einsum('bhqd,bhkd->bhqk', q, k) * scale
        causal = jnp.triu(jnp.ones((s, s), dtype=bool), k=1)
        scores = jnp.where(causal[None, None], -jnp.inf, scores)
        attn = jax.nn.softmax(scores, axis=-1)
        out = jnp.einsum('bhqk,bhkd->bhqd', attn, v)
        out = out.transpose(0, 2, 1, 3).reshape(b, s, E)
        return out @ wo + bo

    def _L1_ffn_ref(x, Wr, Wg, Wu, Wd, Sg, Su, Sd):
        import jax, jax.numpy as jnp
        import numpy as np
        B, S, D = (2, 512, 256)
        E, K, F = (16, 2, 128)
        FS = 256
        b, s, d = x.shape
        T = b * s
        xf = x.reshape(T, d)
        shared = jax.nn.silu(xf @ Sg) * (xf @ Su) @ Sd
        probs = jax.nn.softmax(xf @ Wr, axis=-1)
        topk_p, topk_i = jax.lax.top_k(probs, K)
        n_exp = Wr.shape[1]
        cw = jnp.zeros((T, n_exp), x.dtype).at[jnp.arange(T)[:, None], topk_i].add(topk_p)

        def step(acc, ew):
            wg, wu, wd, c = ew
            y = jax.nn.silu(xf @ wg) * (xf @ wu) @ wd
            return (acc + y * c[:, None], None)
        routed, _ = jax.lax.scan(step, jnp.zeros_like(xf), (Wg, Wu, Wd, cw.T))
        return (routed + shared).reshape(b, s, d)
    x = L0_attn_a_x
    x = x + _L0_attn_a_ref(_layernorm(x, axis=-1), L0_attn_a_ln_g, L0_attn_a_ln_b, L0_attn_a_W_in, L0_attn_a_conv_w, L0_attn_a_conv_b, L0_attn_a_W_xproj, L0_attn_a_W_dt, L0_attn_a_b_dt, L0_attn_a_A_log, L0_attn_a_D, L0_attn_a_W_out)
    x = x + _L0_ffn_ref(_layernorm(x, axis=-1), L0_ffn_W_router, L0_ffn_b_router, L0_ffn_experts_inter, L0_ffn_experts_out)
    x = x + _L0_attn_b_ref(_layernorm(x, axis=-1), L0_attn_b_w, L0_attn_b_u, L0_attn_b_rk, L0_attn_b_rv, L0_attn_b_rr, L0_attn_b_crk, L0_attn_b_crr, L0_attn_b_Wk, L0_attn_b_Wv, L0_attn_b_Wr, L0_attn_b_Wck, L0_attn_b_Wcv, L0_attn_b_Wcr, L0_attn_b_ln1_g, L0_attn_b_ln1_b, L0_attn_b_ln2_g, L0_attn_b_ln2_b)
    x = x + _L0_ffn_ref(_layernorm(x, axis=-1), L0_ffn_W_router, L0_ffn_b_router, L0_ffn_experts_inter, L0_ffn_experts_out)
    x = x + _L1_attn_a_ref(_layernorm(x, axis=-1), L1_attn_a_A_log, L1_attn_a_D_param, L1_attn_a_W_delta, L1_attn_a_b_delta, L1_attn_a_W_B, L1_attn_a_W_C, L1_attn_a_W_router, L1_attn_a_Wg, L1_attn_a_Wu, L1_attn_a_Wd, L1_attn_a_wn_exp, L1_attn_a_norm_w)
    x = x + _L1_ffn_ref(_layernorm(x, axis=-1), L1_ffn_Wr, L1_ffn_Wg, L1_ffn_Wu, L1_ffn_Wd, L1_ffn_Sg, L1_ffn_Su, L1_ffn_Sd)
    x = x + _L1_attn_b_ref(_layernorm(x, axis=-1), L1_attn_b_wq, L1_attn_b_bq, L1_attn_b_wqc, L1_attn_b_bqc, L1_attn_b_wqr, L1_attn_b_bqr, L1_attn_b_wkv, L1_attn_b_bkv, L1_attn_b_wkr, L1_attn_b_bkr, L1_attn_b_wkc, L1_attn_b_bkc, L1_attn_b_wv, L1_attn_b_bv, L1_attn_b_wo, L1_attn_b_bo)
    x = x + _L1_ffn_ref(_layernorm(x, axis=-1), L1_ffn_Wr, L1_ffn_Wg, L1_ffn_Wu, L1_ffn_Wd, L1_ffn_Sg, L1_ffn_Su, L1_ffn_Sd)
    return x

_drawn_inputs = setup_inputs


def setup_inputs(seed=0):
    import zlib

    import numpy as np

    out = dict(_drawn_inputs(seed))
    spreads = {'L0_attn_a_ln_g': (1.0, 0.2),
     'L0_attn_a_ln_b': (0.0, 0.1),
     'L0_attn_a_conv_b': (0.0, 0.1),
     'L0_attn_a_D': (1.0, 0.2),
     'L0_attn_b_ln1_g': (1.0, 0.2),
     'L0_attn_b_ln1_b': (0.0, 0.1),
     'L0_attn_b_ln2_g': (1.0, 0.2),
     'L0_attn_b_ln2_b': (0.0, 0.1),
     'L0_ffn_b_router': (0.0, 0.1),
     'L1_attn_a_D_param': (1.0, 0.2),
     'L1_attn_a_b_delta': (0.0, 0.1),
     'L1_attn_a_wn_exp': (1.0, 0.2),
     'L1_attn_a_norm_w': (1.0, 0.2)}
    factors = {}
    for name, (base, spread) in spreads.items():
        noise = np.random.default_rng([zlib.crc32(name.encode()), seed]).standard_normal(out[name].shape)
        drawn = base * np.exp(spread * noise) if base else spread * noise
        out[name] = jnp.asarray(drawn.astype(out[name].dtype))
    for name, factor in factors.items():
        out[name] = (out[name] * factor).astype(out[name].dtype)
    return out
```

```python
from contextlib import ExitStack

import numpy as np
import concourse.bass as bass
from concourse import mybir

F32, BF16, I32 = mybir.dt.float32, mybir.dt.bfloat16, mybir.dt.int32
ACT, ALU, AX = mybir.ActivationFunctionType, mybir.AluOpType, mybir.AxisListType

P = 128
NB, L, D = 4, 1024, 256
T_ALL = NB * L
NT = T_ALL // P
DT = D // P
CH = 512
NC = T_ALL // CH
TPC = CH // P
CPB = L // CH
LN_EPS = 1e-5
BAR_B_MAX, H_MAX = 10.0, 10000.0


class Engine:

    def __init__(self, eng, name, stack, nc):
        self.e, self.n, self.seen = eng, 0, {}
        self.sem = stack.enter_context(nc.semaphore("done_" + name))

    def did(self, inst):
        self.n += 1
        inst.then_inc(self.sem, 1)
        return (self.sem, self.n)

    def wait(self, *marks):
        for m in marks:
            if m is None:
                continue
            if type(m) is list:
                self.wait(*m)
                continue
            sem, value = m
            if self.seen.get(sem.name, 0) < value:
                self.e.wait_ge(sem, value)
                self.seen[sem.name] = value

    def own(self):
        return (self.sem, self.n)


class Core:
    def __init__(self, nc, stack):
        self.nc, self.stack = nc, stack
        self.V = Engine(nc.vector, "vector", stack, nc)
        self.S = Engine(nc.scalar, "scalar", stack, nc)
        self.G = Engine(nc.gpsimd, "gpsimd", stack, nc)
        self.T = Engine(nc.tensor, "tensor", stack, nc)
        self.Q = Engine(nc.sync, "sync", stack, nc)
        self.streams, self.stage = {}, 0

    def dma(self, queue, out, in_, stream):
        return self.count(queue.e.dma_start(out, in_), stream)

    def count(self, inst, stream):
        if stream not in self.streams:
            self.streams[stream] = [self.stack.enter_context(self.nc.semaphore("dma_" + stream)), 0]
        s = self.streams[stream]
        s[1] += 16
        inst.then_inc(s[0], 16)
        return (s[0], s[1])

    def barrier(self):
        marks = [e.own() for e in (self.V, self.S, self.G, self.T) if e.n]
        marks += [(s[0], s[1]) for s in self.streams.values()]
        for e in (self.V, self.S, self.G, self.T, self.Q):
            e.wait(*marks)


class Memory:

    def __init__(self, K):
        self.K, self.stack = K, ExitStack()
        K.stage += 1
        self.tag = f"s{K.stage}_"

    def sb(self, name, shape, dt=F32):
        return self.stack.enter_context(self.K.nc.sbuf_tensor(self.tag + name, shape, dt))

    def ps(self, name, shape, dt=F32):
        return self.stack.enter_context(self.K.nc.psum_tensor(self.tag + name, shape, dt))

    def free(self):
        self.K.barrier()
        self.stack.close()


def mid(ap, n):
    p, c = ap.shape
    return ap.unsqueeze(1).to_broadcast([p, n, c])


def last(ap, n):
    p, a = ap.shape
    return ap.unsqueeze(2).to_broadcast([p, a, n])


def layernorm_tiles(K, M, src, dst, n, wait, eps=LN_EPS, tag=""):
    V, G = K.V, K.G
    st, mv, ve, rs = M.ln
    V.wait(wait)
    for i in range(n):
        V.did(V.e.bn_stats(st[:, i, :], src[:, i, :]))
    V.wait(V.own())
    for i in range(n):
        V.did(V.e.bn_aggr(mv[:, i, :], st[:, i, :]))
    V.wait(V.own())
    G.wait(V.did(V.e.tensor_scalar(ve[:, 0:n], mv[:, 0:n, 1], eps, None, ALU.add)))
    V.wait(G.did(G.e.tensor_tensor(rs[:, 0:n], ve[:, 0:n], K.neghalf[:, 0:n], ALU.pow)))
    for i in range(n):
        V.did(V.e.tensor_scalar(dst[:, i, :], src[:, i, :], mv[:, i, 0:1], rs[:, i:i + 1],
                                ALU.subtract, ALU.mult))
    return V.own()


def ln_buffers(M, n):
    M.ln = (M.sb("ln_stats", [P, n, 6]), M.sb("ln_meanvar", [P, n, 2]),
            M.sb("ln_vareps", [P, n]), M.sb("ln_rstd", [P, n]))


class Scan:

    def __init__(self, K, M, nd, ns):
        self.K, self.M, self.nd, self.ns = K, M, nd, ns
        self.dA = [M.sb(f"dA{i}", [P, nd, CH]) for i in range(2)]
        self.dBu = [M.sb(f"dBu{i}", [P, nd, CH]) for i in range(2)]
        self.h = [M.sb(f"h{i}", [P, nd, CH]) for i in range(2)]
        self.Bb = [M.sb(f"Bb{i}", [P, CH]) for i in range(2)]
        self.carry = M.sb("carry", [P, ns, nd])
        self.Bps = M.ps("B_rows", [P, CH])
        self.Cps = [M.ps(f"C_rows{i}", [P, CH]) for i in range(2)]
        self.y = [M.ps(f"y_sum{i}", [P, CH]) for i in range(nd)]
        self.i = 0
        self.b_copied = self.y_free = None
        self.dbu_done = [None, None]
        self.scanned = [None, None]
        self.weighed = [None, None]
        self.c_made, self.decayed = [None, None], [None, None]
        self.summed = [None, None]

    def prepare(self, n, dt, dtu, BC3, A, sel, ready):
        K, nd = self.K, self.nd
        S, G, T = K.S, K.G, K.T
        r = self.i % 2
        self.i += 1
        T.wait(ready, self.b_copied)
        b_made = T.did(T.e.matmul(self.Bps[:], sel[:, n, :], BC3, start=True, stop=True))
        T.wait(self.weighed[r])
        self.c_made[r] = T.did(T.e.matmul(self.Cps[r][:], sel[:, 16 + n, :], BC3, start=True, stop=True))
        S.wait(b_made, self.dbu_done[r])
        self.b_copied = S.did(S.e.activation(self.Bb[r][:], self.Bps[:], ACT.Copy))
        S.wait(ready, self.scanned[r])
        for d in range(nd):
            S.did(S.e.activation(self.dA[r][:, d, :], dt[:, d, :], ACT.Exp, scale=A[:, d, n:n + 1]))
        self.decayed[r] = S.own()
        G.wait(ready, self.b_copied, self.scanned[r])
        self.dbu_done[r] = G.did(G.e.tensor_tensor(self.dBu[r][:], dtu, mid(self.Bb[r][:], nd), ALU.mult))

    def scan(self, c, n, r, general=None):
        nd, V = self.nd, self.K.V
        first_chunk = c % CPB == 0
        V.wait(self.decayed[r], self.dbu_done[r], self.summed[r])
        for d in range(nd):
            V.did(V.e.tensor_tensor_scan(
                self.h[r][:, d, :], self.dA[r][:, d, :], self.dBu[r][:, d, :],
                0.0 if first_chunk else self.carry[:, n, d:d + 1], ALU.mult, ALU.add))
        if general is not None:
            general(self, r, n, c)
        self.scanned[r] = V.own()
        V.wait(self.scanned[r])
        V.did(V.e.tensor_copy(self.carry[:, n, :], self.h[r][:, :, CH - 1]))
        V.wait(self.c_made[r], V.own())
        self.weighed[r] = V.did(V.e.tensor_tensor(
            self.h[r][:], self.h[r][:], mid(self.Cps[r][:], nd), ALU.mult))

    def total(self, n, r):
        T = self.K.T
        T.wait(self.weighed[r])
        if n == 0:
            T.wait(self.y_free)
        for d in range(self.nd):
            T.did(T.e.matmul(self.y[d][:], self.K.ident[:], self.h[r][:, d, :],
                             start=n == 0, stop=n == self.ns - 1))
        self.summed[r] = T.own()


def run_scan(sc, front, back, operands, general=None):
    for _ in front(0):
        pass
    sc.prepare(0, *operands(0))
    for c in range(NC):
        side = front(c + 1) if c + 1 < NC else iter(())
        left = sc.pairs
        for n in range(sc.ns):
            r = (c * sc.ns + n) % 2
            slots = sc.ns - 1 - n
            if n + 1 < sc.ns:
                sc.prepare(n + 1, *operands(c))
            take = -(-left // slots) if slots else 0
            left -= take
            next(side, None) if take else None
            if slots == 0:
                for _ in side:
                    pass
                if c + 1 < NC:
                    sc.prepare(0, *operands(c + 1))
            sc.scan(c, n, r, general)
            sc.total(n, r)
            for _ in range(2 * take - 1):
                next(side, None)
        back(c)


def split3(K, src, dst, rest, ready):
    V = K.V
    V.wait(ready)
    V.wait(V.did(V.e.tensor_copy(dst[0:96, :], src[0:96, :])))
    V.did(V.e.tensor_tensor(rest[32:64, :], src[32:64, :], dst[32:64, :], ALU.subtract))
    V.wait(V.did(V.e.tensor_tensor(rest[64:96, :], src[64:96, :], dst[64:96, :], ALU.subtract)))
    V.did(V.e.tensor_copy(dst[32:64, :], rest[32:64, :]))
    V.wait(V.did(V.e.tensor_copy(dst[64:96, :], rest[64:96, :])))
    V.wait(V.did(V.e.tensor_tensor(rest[64:96, :], rest[64:96, :], dst[64:96, :], ALU.subtract)))
    return V.did(V.e.tensor_copy(dst[64:96, :], rest[64:96, :]))


def mamba_stage(K, W):
    V, S, G, T, Q = K.V, K.S, K.G, K.T, K.Q
    X = K.X
    DI, NS, R = 512, 16, 16
    ND = DI // P
    M = Memory(K)
    ln_buffers(M, TPC)
    w_in = M.sb("w_in", [P, DT, 2 * DI])
    w_bc = M.sb("w_bc", [P, ND, 3, 2 * NS])
    w_dtr = M.sb("w_dtr", [P, ND, R])
    w_dt = M.sb("w_dt", [R, DI])
    w_out = M.sb("w_out", [P, ND, D])
    vec = M.sb("mamba_vectors", [P, ND, 8])
    lnv = M.sb("mamba_ln", [P, DT, 2])
    A = M.sb("A", [P, ND, NS])
    sel = M.sb("selectors", [96, 32, P], BF16)
    loads = [
        K.dma(Q, w_in[:], W["L0_attn_a_W_in"].rearrange("(k p) e -> p k e", p=P), "weights"),
        K.dma(Q, w_out[:], W["L0_attn_a_W_out"].rearrange("(k p) e -> p k e", p=P), "weights"),
        K.dma(Q, w_dt[:], W["L0_attn_a_W_dt"], "weights"),
        K.dma(Q, w_dtr[:], W["L0_attn_a_W_xproj"].rearrange("(k p) e -> p k e", p=P)[:, :, 0:R], "weights"),
        K.dma(Q, vec[:], W["mamba_vectors"], "weights"),
        K.dma(Q, lnv[:], W["mamba_ln"], "weights"),
        K.dma(Q, A[:], W["L0_attn_a_A_log"].rearrange("(k p) n -> p k n", p=P), "weights"),
        K.dma(Q, sel[:], W["const_selectors"], "weights"),
    ]
    for j in range(3):
        loads.append(K.dma(Q, w_bc[:, :, j, :], W["L0_attn_a_W_xproj"].rearrange("(k p) e -> p k e", p=P)[:, :, R:], "weights"))
    loaded = loads[-1]
    S.wait(loaded)
    S.wait(S.did(S.e.activation(A[:], A[:], ACT.Exp)))
    V.wait(S.own())
    a_ready = V.did(V.e.tensor_scalar(A[:], A[:], -1.0, None, ALU.mult))
    for e in (V, S, G, T):
        e.wait(loaded, a_ready)

    sc = Scan(K, M, ND, NS)
    xn = M.sb("xn", [P, TPC, D])
    hT = M.sb("hT", [P, DT, CH])
    uraw = M.sb("uraw", [P, ND, 3 + CH])
    cv = M.sb("conv", [P, ND, CH])
    zs = [M.sb(f"z{i}", [P, ND, CH]) for i in range(2)]
    u = [M.sb(f"u{i}", [P, ND, CH]) for i in range(2)]
    dt = [M.sb(f"dt{i}", [P, ND, CH]) for i in range(2)]
    dtu = [M.sb(f"dtu{i}", [P, ND, CH]) for i in range(2)]
    BC3 = [M.sb(f"BC3_{i}", [96, CH], BF16) for i in range(2)]
    rest = M.sb("bc_rest", [96, CH])
    dtr = M.sb("dt_rank", [R, CH])
    fp = M.ps("front", [P, CH])
    st = {"bank": None, "chunk_done": [None, None], "hT_free": None, "ready": [None, None],
          "hist": None}

    def front(c):
        r = c % 2
        x4 = X[:, TPC * c:TPC * (c + 1), :]
        normed = layernorm_tiles(K, M, x4, xn, TPC, [st["hT_free"], K.x_ready])
        yield
        yield
        V.wait(normed)
        added = V.did(V.e.tensor_tensor(x4, x4, xn[:], ALU.add))
        K.x_written[c] = added
        V.wait(added)
        h_ready = layernorm_tiles(K, M, xn, xn, TPC, None)
        yield
        yield
        for k in range(DT):
            T.wait(h_ready, st["bank"])
            for i in range(TPC):
                T.did(T.e.transpose(fp[:, i * P:(i + 1) * P], xn[:, i, k * P:(k + 1) * P], K.ident[:]))
            made = T.own()
            yield
            S.wait(made, st["hT_free"])
            st["bank"] = S.did(S.e.activation(hT[:, k, :], fp[:], ACT.Identity,
                                              bias=lnv[:, k, 1:2], scale=lnv[:, k, 0:1]))
            yield
        hT_ready = st["bank"]
        V.wait(st["hist"])
        if c % CPB:
            hist = V.did(V.e.tensor_copy(uraw[:, :, 0:3], uraw[:, :, CH:CH + 3]))
        else:
            hist = V.did(V.e.memset(uraw[:, :, 0:3], 0.0))
        for e in range(2 * ND):
            T.wait(hT_ready, st["bank"])
            for k in range(DT):
                T.did(T.e.matmul(fp[:], w_in[:, k, e * P:(e + 1) * P], hT[:, k, :],
                                 start=k == 0, stop=k == DT - 1))
            made = T.own()
            yield
            S.wait(made, hist, st["chunk_done"][r])
            to = uraw[:, e, 3:3 + CH] if e < ND else zs[r][:, e - ND, :]
            st["bank"] = S.did(S.e.activation(to, fp[:], ACT.Copy))
            if e == ND - 1:
                u_ready = st["bank"]
            if e < ND:
                yield
                continue
            d = e - ND
            V.wait(u_ready, st["u_free"] if "u_free" in st else None)
            V.wait(V.did(V.e.tensor_scalar(cv[:, d, :], uraw[:, d, 0:CH], vec[:, d, 0:1], vec[:, d, 4:5],
                                           ALU.mult, ALU.add)))
            for t in range(1, 4):
                V.wait(V.did(V.e.scalar_tensor_tensor(cv[:, d, :], uraw[:, d, t:t + CH], vec[:, d, t:t + 1],
                                                      cv[:, d, :], ALU.mult, ALU.add)))
            yield
        st["hT_free"] = T.own()
        st["hist"] = V.own()
        S.wait(V.own(), S.own())
        S.did(S.e.activation(u[r][:], cv[:], ACT.Silu))
        S.did(S.e.activation(zs[r][:], zs[r][:], ACT.Silu))
        st["u_free"] = S.own()
        yield
        yield
        T.wait(S.own(), st["bank"])
        for k in range(ND):
            T.did(T.e.matmul(fp[0:96, :], w_bc[:, k, :, :].rearrange("p a b -> p (a b)"), u[r][:, k, :],
                             start=k == 0, stop=k == ND - 1))
        made = T.own()
        yield
        split_done = split3(K, fp, BC3[r], rest, [made, st["chunk_done"][r]])
        yield
        T.wait(split_done)
        for k in range(ND):
            T.did(T.e.matmul(fp[0:R, :], w_dtr[:, k, :], u[r][:, k, :], start=k == 0, stop=k == ND - 1))
        made = T.own()
        yield
        S.wait(made)
        st["bank"] = S.did(S.e.activation(dtr[:], fp[0:R, :], ACT.Copy))
        yield
        ab = cv
        for d in range(ND):
            T.wait(st["bank"])
            T.did(T.e.matmul(fp[:], w_dt[:, d * P:(d + 1) * P], dtr[:], start=True, stop=True))
            made = T.own()
            yield
            S.wait(made, st["u_free"])
            S.did(S.e.activation(ab[:, d, :], fp[:], ACT.Abs, bias=vec[:, d, 5:6]))
            V.wait(S.own())
            relu = V.did(V.e.tensor_scalar(dt[r][:, d, :], fp[:], vec[:, d, 5:6], 0.0, ALU.add, ALU.max))
            st["bank"] = [S.own(), relu]
            yield
        S.wait(S.own())
        S.wait(S.did(S.e.activation(ab[:], ab[:], ACT.Exp, scale=-1.0)))
        S.did(S.e.activation(ab[:], ab[:], ACT.Ln, bias=1.0))
        yield
        yield
        V.wait(S.own(), V.own())
        made = V.did(V.e.tensor_tensor(dt[r][:], dt[r][:], ab[:], ALU.add))
        st["u_free"] = made
        G.wait(made)
        st["ready"][r] = [G.did(G.e.tensor_tensor(dtu[r][:], dt[r][:], u[r][:], ALU.mult)), made, split_done]
        yield

    def back(c):
        r = c % 2
        V.wait(sc.summed[0], sc.summed[1])
        for d in range(ND):
            V.did(V.e.scalar_tensor_tensor(u[r][:, d, :], u[r][:, d, :], vec[:, d, 6:7], sc.y[d][:],
                                           ALU.mult, ALU.add))
        sc.y_free = V.own()
        V.wait(V.own())
        gated = V.did(V.e.tensor_tensor(u[r][:], u[r][:], zs[r][:], ALU.mult))
        T.wait(gated)
        for i in range(0, TPC, 2):
            T.wait(st["bank"])
            for j in range(2):
                for k in range(ND):
                    T.did(T.e.matmul(fp[:, j * D:(j + 1) * D], u[r][:, k, (i + j) * P:(i + j + 1) * P],
                                     w_out[:, k, :], start=k == 0, stop=k == ND - 1))
            xt = X[:, TPC * c + i:TPC * c + i + 2, :]
            V.wait(T.own(), K.x_written[c])
            st["bank"] = V.did(V.e.tensor_tensor(xt, xt, fp[:].rearrange("p (a b) -> p a b", a=2), ALU.add))
        st["chunk_done"][r] = [T.own(), V.own()]

    K.x_written = [None] * NC
    sc.pairs = 21
    run_scan(sc, front, back, lambda c: (dt[c % 2], dtu[c % 2][:], BC3[c % 2][:], A, sel, st["ready"][c % 2]))
    K.x_ready = V.own()
    M.free()



SLOT_TILES = 80
SLOTS = SLOT_TILES * P
ZERO_ROW = SLOTS
DROPPED = 1 << 20


def prepare_tiles(K, M, c, xn, xT, bank, wait, have_ln=True):
    V, S, T = K.V, K.S, K.T
    ready = wait
    if have_ln:
        tiles = slice(TPC * c, TPC * (c + 1))
        ready = layernorm_tiles(K, M, K.X[:, tiles, :], xn, TPC, wait)
    marks = []
    for k in range(DT):
        T.wait(ready, bank.free)
        for i in range(TPC):
            T.did(T.e.transpose(bank.ap[:, i * P:(i + 1) * P], xn[:, i, k * P:(k + 1) * P], K.ident[:]))
        S.wait(T.own(), wait)
        bank.free = S.did(S.e.activation(xT[:, k, :], bank.ap[:], ACT.Copy))
        marks.append(bank.free)
    return ready, marks


class Bank:

    def __init__(self, ap):
        self.ap, self.free = ap, None


class Routing:

    def __init__(self, K, M, E, capacity=None):
        self.K, self.M, self.E, self.cap = K, M, E, capacity
        self.logits = M.ps("logits", [P, NT, E])
        n = [P, NT, E]
        self.p, self.a, self.b = M.sb("probs", n), M.sb("route_a", n), M.sb("route_b", n)
        self.oh = [M.sb(f"onehot{i}", n) for i in range(2)]
        self.mask = M.sb("mask", n, BF16)
        self.tot = M.sb("totals", [P, E, NT])
        self.cum = M.sb("cumulated", [P, E, NT])
        self.keep = M.sb("keep", [P, E, NT])
        self.w = [M.sb(f"weight{i}", [P, NT]) for i in range(2)]
        self.red = M.sb("route_red", [P, NT])
        self.fl = M.sb("route_slot", [P, NT])
        self.scatter_to = [M.sb(f"scatter_to{i}", [P, NT], I32) for i in range(2)]
        self.gather_of = [M.sb(f"gather_of{i}", [P, NT], I32) for i in range(2)]
        self.small = M.sb("route_small", [P, E, NT])
        self.nt, self.end = M.sb("n_tiles", [P, E]), M.sb("end_tile", [P, E])
        self.rev = M.sb("reversed_iota", [P, E])
        self.ones = M.sb("route_ones", [P, E])
        if capacity is None:
            self.ej = M.sb("tile_compare", [P, SLOT_TILES, E])
            self.ef = M.sb("tile_expert_f", [P, SLOT_TILES])
            self.tile_expert = M.sb("tile_expert", [P, SLOT_TILES], I32)

    def run(self, made, bias=None, normalise=False):
        K, E = self.K, self.E
        V, S, T = K.V, K.S, K.T
        p, a, b, red, fl = self.p, self.a, self.b, self.red, self.fl
        ranks = ExitStack()
        self.within = ranks.enter_context(K.nc.psum_tensor(self.M.tag + "rank_within_tile", [P, NT, E], F32))
        self.totals = ranks.enter_context(K.nc.psum_tensor(self.M.tag + "tile_totals", [P, NT, E], F32))

        def v(inst):
            V.wait(V.did(inst))

        V.wait(made)
        if bias is not None:
            v(V.e.tensor_tensor(p[:], self.logits[:], mid(bias, NT), ALU.add))
        else:
            v(V.e.tensor_copy(p[:], self.logits[:]))
        v(V.e.tensor_reduce(red[:], p[:], AX.X, ALU.max))
        v(V.e.tensor_tensor(p[:], p[:], last(red[:], E), ALU.subtract))
        S.wait(V.own())
        V.wait(S.did(S.e.activation(p[:], p[:], ACT.Exp)))
        v(V.e.tensor_reduce(red[:], p[:], AX.X, ALU.add))
        v(V.e.reciprocal(red[:], red[:]))
        v(V.e.tensor_tensor(p[:], p[:], last(red[:], E), ALU.mult))
        v(V.e.tensor_scalar(self.rev[:], K.iota[:, 0:E], -1.0, float(E), ALU.mult, ALU.add))
        v(V.e.tensor_copy(a[:], p[:]))
        for i in range(2):
            v(V.e.tensor_reduce(self.w[i][:], a[:], AX.X, ALU.max))
            v(V.e.tensor_tensor(b[:], a[:], last(self.w[i][:], E), ALU.is_equal))
            v(V.e.tensor_tensor(b[:], b[:], mid(self.rev[:], NT), ALU.mult))
            v(V.e.tensor_reduce(red[:], b[:], AX.X, ALU.max))
            v(V.e.tensor_tensor(self.oh[i][:], b[:], last(red[:], E), ALU.is_equal))
            if i == 0:
                v(V.e.scalar_tensor_tensor(a[:], self.oh[0][:], -2.0, a[:], ALU.mult, ALU.add))
        v(V.e.tensor_tensor(b[:], self.oh[0][:], self.oh[1][:], ALU.add))
        if self.cap is not None:
            v(V.e.tensor_scalar(a[:], p[:], 0.0, None, ALU.is_gt))
            v(V.e.tensor_tensor(b[:], b[:], a[:], ALU.mult))
        v(V.e.tensor_copy(self.mask[:], b[:]))
        T.wait(V.own())
        T.did(T.e.matmul(self.within[:].rearrange("p t e -> p (t e)"), K.before[:],
                         self.mask[:].rearrange("p t e -> p (t e)"), start=True, stop=True))
        T.did(T.e.matmul(self.totals[:].rearrange("p t e -> p (t e)"), K.ones_bf[:],
                         self.mask[:].rearrange("p t e -> p (t e)"), start=True, stop=True))
        V.wait(T.own())
        v(V.e.tensor_copy(self.tot[:], self.totals[:].rearrange("p t e -> p e t")))
        v(V.e.memset(self.keep[:], 1.0))
        v(V.e.memset(self.keep[:, :, 0], 0.0))
        flat = lambda t: t[:].rearrange("p e t -> p (e t)")
        v(V.e.tensor_tensor_scan(flat(self.cum), flat(self.keep), flat(self.tot), 0.0, ALU.mult, ALU.add))
        count = self.small
        if self.cap is None:
            v(V.e.tensor_scalar(self.keep[:], mid(K.iota[:, 0:NT], E), float(P), None, ALU.mult))
            v(V.e.tensor_tensor(count[:], last(self.cum[:, :, NT - 1], NT), self.keep[:], ALU.is_gt))
            v(V.e.tensor_reduce(self.nt[:], count[:], AX.X, ALU.add))
            v(V.e.memset(self.ones[:], 1.0))
            v(V.e.tensor_tensor_scan(self.end[:], self.ones[:], self.nt[:], 0.0, ALU.mult, ALU.add))
            v(V.e.tensor_tensor(self.ej[:], last(K.iota[:, 0:SLOT_TILES], E), mid(self.end[:], SLOT_TILES), ALU.is_ge))
            v(V.e.tensor_reduce(self.ef[:], self.ej[:], AX.X, ALU.add))
            v(V.e.tensor_scalar(self.ef[:], self.ef[:], float(E - 1), None, ALU.min))
            v(V.e.tensor_copy(self.tile_expert[:], self.ef[:]))
            v(V.e.tensor_tensor(self.nt[:], self.end[:], self.nt[:], ALU.subtract))
            v(V.e.tensor_scalar(self.nt[:], self.nt[:], float(P), None, ALU.mult))
        else:
            v(V.e.tensor_scalar(self.nt[:], K.iota[:, 0:E], float(self.cap), None, ALU.mult))
        v(V.e.tensor_tensor(self.cum[:], self.cum[:], self.tot[:], ALU.subtract))
        v(V.e.tensor_tensor(a[:], self.within[:], self.cum[:].rearrange("p e t -> p t e"), ALU.add))
        for i in range(2):
            if self.cap is not None:
                v(V.e.tensor_tensor(b[:], self.oh[i][:], a[:], ALU.mult))
                v(V.e.tensor_reduce(red[:], b[:], AX.X, ALU.add))
                v(V.e.tensor_scalar(red[:], red[:], float(self.cap), None, ALU.is_lt))
                v(V.e.tensor_scalar(fl[:], self.w[i][:], 0.0, None, ALU.is_gt))
                v(V.e.tensor_tensor(red[:], red[:], fl[:], ALU.mult))
            v(V.e.tensor_tensor(b[:], a[:], mid(self.nt[:], NT), ALU.add))
            v(V.e.tensor_tensor(b[:], b[:], self.oh[i][:], ALU.mult))
            v(V.e.tensor_reduce(fl[:], b[:], AX.X, ALU.add))
            if self.cap is not None:
                v(V.e.tensor_tensor(fl[:], fl[:], red[:], ALU.mult))
                v(V.e.tensor_scalar(red[:], red[:], -1.0, 1.0, ALU.mult, ALU.add))
                v(V.e.scalar_tensor_tensor(self.small[:, 0, :], red[:], float(DROPPED), fl[:], ALU.mult, ALU.add))
                v(V.e.tensor_copy(self.scatter_to[i][:], self.small[:, 0, :]))
                v(V.e.scalar_tensor_tensor(fl[:], red[:], float(ZERO_ROW), fl[:], ALU.mult, ALU.add))
                v(V.e.tensor_copy(self.gather_of[i][:], fl[:]))
            else:
                v(V.e.tensor_copy(self.scatter_to[i][:], fl[:]))
                v(V.e.tensor_copy(self.gather_of[i][:], fl[:]))
        if normalise:
            v(V.e.tensor_tensor(red[:], self.w[0][:], self.w[1][:], ALU.add))
            v(V.e.tensor_scalar(red[:], red[:], 1e-9, None, ALU.add))
            v(V.e.reciprocal(red[:], red[:]))
            for i in range(2):
                v(V.e.tensor_tensor(self.w[i][:], self.w[i][:], red[:], ALU.mult))
        T.wait(V.own())
        ranks.close()
        return V.own()

    def scatter(self, rows, routed):
        K, G = self.K, self.K.G
        G.wait(routed, K.sorted_read)
        for t in range(NT):
            for i in range(2):
                done = K.count(G.e.indirect_dma_start(
                    K.sorted_in, bass.IndirectOffsetOnAxis(ap=self.scatter_to[i][:, t:t + 1], axis=0),
                    rows[:, t, :], None, bounds_check=SLOTS - 1, oob_is_err=False), "scatter")
        return done

    def combine(self, stored, into, ring=4):
        K, V, G = self.K, self.K.V, self.K.G
        got = [[self.M.sb(f"gathered{i}_{j}", [P, D]) for j in range(2)] for i in range(ring)]
        used = [None] * ring
        G.wait(stored)
        for t in range(NT):
            s = t % ring
            G.wait(used[s])
            for i in range(2):
                arrived = K.count(G.e.indirect_dma_start(
                    got[s][i][:], None, K.sorted_out,
                    bass.IndirectOffsetOnAxis(ap=self.gather_of[i][:, t:t + 1], axis=0),
                    bounds_check=SLOTS, oob_is_err=False), f"gather{s}")
            V.wait(arrived, K.x_ready)
            for i in range(2):
                V.did(V.e.scalar_tensor_tensor(into[:, t, :], got[s][i][:], self.w[i][:, t:t + 1], into[:, t, :],
                                               ALU.mult, ALU.add))
                V.wait(V.own())
            used[s] = V.own()


def moe0_stage(K, W):
    V, S, G, T, Q = K.V, K.S, K.G, K.T, K.Q
    E, I = 8, 1024
    CAP = -(-T_ALL * 5 // (4 * E))
    CT = CAP // P
    KI = I // P
    M = Memory(K)
    ln_buffers(M, TPC)
    R = Routing(K, M, E, CAP)
    wr = M.sb("w_router", [P, DT, E])
    rb = M.sb("b_router", [P, E])
    xn = M.sb("xn", [P, NT, D])
    xT = [M.sb(f"xT{i}", [P, DT, CH]) for i in range(2)]
    tbank = [Bank(M.ps(f"transposed{i}", [P, CH])) for i in range(2)]
    w_in = [M.sb(f"w_inter{i}", [P, DT, I]) for i in range(2)]
    w_out = [M.sb(f"w_exp_out{i}", [P, KI, D]) for i in range(2)]
    rows = [M.sb(f"rows{i}", [P, CT, D]) for i in range(2)]
    K.dma(Q, wr[:], W["L0_router_T"].rearrange("(k p) e -> p k e", p=P), "weights")
    loaded = K.dma(Q, rb[:], W["L0_router_bias"], "weights")
    freed = [None, None]

    def load_expert(e):
        r = e % 2
        Q.wait(freed[r])
        K.dma(Q, w_in[r][:], W["L0_ffn_experts_inter"][e].rearrange("(k p) i -> p k i", p=P), f"expert{r}")
        return K.dma(Q, w_out[r][:], W["L0_ffn_experts_out"][e].rearrange("(k p) i -> p k i", p=P), f"expert{r}")

    expert_here = [load_expert(0), load_expert(1)]
    T.wait(loaded)
    V.wait(loaded)
    used = [None, None]
    for c in range(NC):
        r = c % 2
        _, marks = prepare_tiles(K, M, c, xn[:, TPC * c:TPC * (c + 1), :], xT[r], tbank[r], [used[r], K.x_ready])
        T.wait(marks)
        for i in range(TPC):
            for k in range(DT):
                T.did(T.e.matmul(R.logits[:, TPC * c + i, :], xT[r][:, k, i * P:(i + 1) * P], wr[:, k, :],
                                 start=k == 0, stop=k == DT - 1))
        used[r] = T.own()
    routed = R.run(T.own(), bias=rb[:])
    scattered = R.scatter(xn, routed)

    xsT = [M.sb(f"rowsT{i}", [P, DT, CAP]) for i in range(2)]
    hT = M.sb("hidden", [P, KI, CAP])
    out = [M.sb(f"result{i}", [P, D]) for i in range(4)]
    hb = [Bank(M.ps(f"hidden_sum{i}", [P, 512])) for i in range(2)]
    ob = Bank(M.ps("result_sum", [P, 2, D]))
    HALF = CAP // 2
    rows_here, rows_free, xsT_free, xsT_ready = [None, None], [None, None], [None, None], [None, None]
    out_stored = [None] * 4
    Q.wait(scattered)

    def load_rows(e):
        r = e % 2
        Q.wait(rows_free[r])
        rows_here[r] = K.dma(Q, rows[r][:], K.sorted_in[e * CAP:(e + 1) * CAP, :].rearrange("(t p) c -> p t c", p=P), f"rows{r}")

    def transpose_rows(e):
        r = e % 2
        T.wait(rows_here[r])
        for t in range(CT):
            b = tbank[t % 2]
            T.wait(b.free)
            for k in range(DT):
                T.did(T.e.transpose(b.ap[:, k * P:(k + 1) * P], rows[r][:, t, k * P:(k + 1) * P], K.ident[:]))
            S.wait(T.own(), xsT_free[r])
            b.free = S.did(S.e.activation(xsT[r][:, :, t * P:(t + 1) * P],
                                          b.ap[:, 0:DT * P].rearrange("p (k q) -> p k q", k=DT), ACT.Copy))
        rows_free[r] = T.own()
        xsT_ready[r] = S.own()

    load_rows(0)
    load_rows(1)
    transpose_rows(0)
    h_free, n_out, stored = None, 0, None
    for e in range(E):
        r = e % 2
        T.wait(xsT_ready[r], expert_here[r])
        for i in range(KI):
            for half in range(2):
                b = hb[half]
                T.wait(b.free)
                for k in range(DT):
                    T.did(T.e.matmul(b.ap[:, 0:HALF], w_in[r][:, k, i * P:(i + 1) * P],
                                     xsT[r][:, k, half * HALF:(half + 1) * HALF], start=k == 0, stop=k == DT - 1))
                to = hT[:, i, half * HALF:(half + 1) * HALF]
                if half:
                    S.wait(T.own(), h_free)
                    b.free = S.did(S.e.activation(to, b.ap[:, 0:HALF], ACT.Relu))
                else:
                    V.wait(T.own(), h_free)
                    b.free = V.did(V.e.tensor_scalar(to, b.ap[:, 0:HALF], 0.0, None, ALU.max))
        xsT_free[r] = T.own()
        h_ready = [S.own(), V.own()]
        if e + 1 < E:
            transpose_rows(e + 1)
            if e + 2 < E:
                load_rows(e + 2)
        T.wait(h_ready)
        for t in range(CT):
            half = n_out % 2
            T.wait(ob.free if half == 0 else None)
            for i in range(KI):
                T.did(T.e.matmul(ob.ap[:, half, :], hT[:, i, t * P:(t + 1) * P], w_out[r][:, i, :],
                                 start=i == 0, stop=i == KI - 1))
            T_mark = T.own()
            V.wait(T_mark, out_stored[n_out % 4])
            ob.free = V.did(V.e.tensor_copy(out[n_out % 4][:], ob.ap[:, half, :]))
            S.wait(ob.free)
            row = (e * CT + t) * P
            out_stored[n_out % 4] = stored = K.dma(S, K.sorted_out[row:row + P, :], out[n_out % 4][:], f"store{n_out % 4}")
            T.wait(ob.free)
            n_out += 1
        h_free = T.own()
        freed[r] = T.own()
        if e + 2 < E:
            expert_here[r] = load_expert(e + 2)
    K.sorted_read = [rows_here[0], rows_here[1]]
    R.combine(out_stored, K.X)
    K.x_ready = V.own()
    M.free()


def do(E, issue, *marks):
    E.wait(*marks)
    return E.did(issue())


def run_lanes(chunk, n, skew, lanes=2):
    active, started, since = [], 0, skew
    while active or started < n:
        if started < n and len(active) < lanes and since >= skew:
            active.append(chunk(started))
            started += 1
            since = 0
        since += 1
        for g in list(active):
            if next(g, "end") == "end":
                active.remove(g)


class Lane:

    def __init__(self, ln, xn, hh, xa, mx, pp, aa, m0, k, v, sr, kw, ea, eb, rr, d1, scr):
        self.ln, self.done = ln, None
        self.xn, self.hh, self.xa, self.mx, self.pp, self.aa, self.m0 = xn, hh, xa, mx, pp, aa, m0
        self.k, self.v, self.sr, self.kw, self.ea, self.eb, self.rr = k, v, sr, kw, ea, eb, rr
        self.d1, self.scr = d1, scr


def rwkv_stage(K, W):
    V, S, G, T, Q = K.V, K.S, K.G, K.T, K.Q
    X = K.X
    HID = 4 * D
    KH = HID // P
    NEG = -1e38
    M = Memory(K)
    w = {n: M.sb("w_" + n, [P, DT, D]) for n in ("k", "v", "r", "cr")}
    for n in w:
        K.dma(Q, w[n][:], W[f"rwkv_W{n}_T"].rearrange("(k p) d -> p k d", p=P), "weights")
    w_ck = M.sb("w_ck", [P, DT, HID])
    w_cv = M.sb("w_cv", [P, KH, D])
    vec = M.sb("rwkv_vectors", [P, DT, 12])
    K.dma(Q, w_ck[:], W["rwkv_Wck_T"].rearrange("(k p) d -> p k d", p=P), "weights")
    K.dma(Q, w_cv[:], W["rwkv_Wcv_T"].rearrange("(k p) d -> p k d", p=P), "weights")
    loaded = K.dma(Q, vec[:], W["rwkv_vectors"], "weights")
    for e in (V, S, G, T):
        e.wait(loaded)
    WD, U, G1, B1, G2, B2 = 0, 1, 7, 8, 9, 10
    MIX = {"k": 2, "v": 3, "r": 4, "ck": 5, "cr": 6}
    omr = M.sb("one_minus_mix", [P, DT, 12])
    nu = M.sb("minus_u", [P, DT])
    V.did(V.e.tensor_scalar(omr[:], vec[:], -1.0, 1.0, ALU.mult, ALU.add))
    prep = V.did(V.e.tensor_scalar(nu[:], vec[:, :, U], -1.0, None, ALU.mult))
    for e in (V, S, G):
        e.wait(prep)

    def lane(i):
        shapes = {n: [P, TPC, D] for n in ("xn", "hh")}
        shapes.update({n: [P, DT, 1 + CH] for n in ("xa", "mx", "pp", "aa")})
        shapes.update({n: [P, DT, CH] for n in ("m0", "k", "v", "sr", "kw", "ea", "eb", "rr", "d1")})
        shapes["scr"] = [P, D]
        ln = tuple(M.sb(f"l{i}_{n}", sh) for n, sh in (("st", [P, TPC, 6]), ("mv", [P, TPC, 2]),
                                                       ("ve", [P, TPC]), ("rs", [P, TPC])))
        return Lane(ln, **{n: M.sb(f"l{i}_{n}", sh) for n, sh in shapes.items()})

    lanes = [lane(i) for i in range(2)]
    kc, kc_free = M.sb("kc", [P, KH, CH]), [None]
    banks = [Bank(M.ps(f"bank{i}", [P, CH])) for i in range(8)]
    tb, pb, kb, ob = banks[0:2], banks[2:4], banks[4:6], banks[6:8]
    turn = {"t": 0, "p": 0, "k": 0, "o": 0}

    def bank(kind):
        turn[kind] += 1
        return {"t": tb, "p": pb, "k": kb, "o": ob}[kind][turn[kind] % 2]

    def to_channels(src, dst, gain, bias, ready, free):
        marks = []
        for k in range(DT):
            f = bank("t")
            T.wait(ready, f.free)
            for i in range(TPC):
                T.did(T.e.transpose(f.ap[:, i * P:(i + 1) * P], src[:, i, k * P:(k + 1) * P], K.ident[:]))
            f.free = do(S, lambda: S.e.activation(dst[:, k, 1:], f.ap[:], ACT.Identity,
                                                  bias=vec[:, k, bias:bias + 1], scale=vec[:, k, gain:gain + 1]),
                        T.own(), free)
            marks.append(f.free)
        return marks

    def mixed(xa, dst, kind, ready, free):
        m, marks = MIX[kind], []
        for k in range(DT):
            s1 = do(S, lambda: S.e.activation(dst[:, k, :], xa[:, k, 0:CH], ACT.Copy, scale=omr[:, k, m:m + 1]),
                    ready, free)
            marks.append(do(V, lambda: V.e.scalar_tensor_tensor(
                dst[:, k, :], xa[:, k, 1:], vec[:, k, m:m + 1], dst[:, k, :], ALU.mult, ALU.add), s1, ready))
        return marks

    prev = {}
    carry = {n: [M.sb(f"carry_{n}{i}", [P, DT, 1]) for i in range(2)] for n in ("xa", "mx", "rr", "pp", "aa", "xb")}

    def start_column(name, buf, c, value, free=None):
        if c % CPB == 0:
            return do(V, lambda: V.e.memset(buf[:, :, 0:1], value), free)
        return do(V, lambda: V.e.tensor_copy(buf[:, :, 0:1], carry[name][(c - 1) % 2][:]), prev[name], free)

    def save_column(name, ap, c, ready):
        prev[name] = do(V, lambda: V.e.tensor_copy(carry[name][c % 2][:], ap), ready)

    def chunk(c):
        b = lanes[c % 2]
        x4 = X[:, TPC * c:TPC * (c + 1), :]
        first = c % CPB == 0
        for e in (V, S, G, T):
            e.wait(b.done)
        xn_ready = layernorm_tiles(K, b, x4, b.xn, TPC, K.x_ready)
        yield
        h_ready = layernorm_tiles(K, b, b.xn, b.hh, TPC, xn_ready)
        yield
        col = start_column("xa", b.xa, c, 0.0)
        xa_ready = to_channels(b.hh, b.xa, G1, B1, h_ready, None)
        save_column("xa", b.xa[:, :, CH:], c, list(xa_ready))
        xa_ready.append(col)
        yield
        proj, read = {}, None
        for kind, dst in (("k", b.k), ("v", b.v), ("r", b.sr)):
            m_ready = mixed(b.xa, b.m0, kind, xa_ready, read)
            yield
            marks = []
            for d in range(DT):
                f = bank("p")
                T.wait(m_ready, f.free)
                for k in range(DT):
                    T.did(T.e.matmul(f.ap[:], w[kind][:, k, d * P:(d + 1) * P], b.m0[:, k, :],
                                     start=k == 0, stop=k == DT - 1))
                f.free = do(S, lambda: S.e.activation(dst[:, d, :], f.ap[:], ACT.Copy), T.own())
                marks.append(f.free)
            read = T.own()
            proj[kind] = marks
            yield
        kw_ready = [do(V, lambda: V.e.tensor_scalar(b.kw[:, d, :], b.k[:, d, :], vec[:, d, WD:WD + 1], None, ALU.add),
                       proj["k"]) for d in range(DT)]
        col = start_column("mx", b.mx, c, NEG)
        for d in range(DT):
            mx = do(V, lambda: V.e.tensor_tensor_scan(
                b.mx[:, d, 1:], vec[:, d, WD:WD + 1].to_broadcast([P, CH]), b.kw[:, d, :],
                b.mx[:, d, 0:1], ALU.add, ALU.max), col, kw_ready)
        save_column("mx", b.mx[:, :, CH:], c, mx)
        yield
        d_a = do(V, lambda: V.e.tensor_tensor(b.ea[:], b.mx[:, :, 0:CH], b.mx[:, :, 1:], ALU.subtract), mx)
        d_b = do(V, lambda: V.e.tensor_tensor(b.eb[:], b.kw[:], b.mx[:, :, 1:], ALU.subtract), mx)
        for d in range(DT):
            e_a = do(S, lambda: S.e.activation(b.ea[:, d, :], b.ea[:, d, :], ACT.Exp, bias=vec[:, d, WD:WD + 1]), d_a)
        e_b = do(S, lambda: S.e.activation(b.eb[:], b.eb[:], ACT.Exp), d_b)
        yield
        for d in range(DT):
            r_ready = do(V, lambda: V.e.tensor_tensor_scan(
                b.rr[:, d, :], b.ea[:, d, :], b.eb[:, d, :],
                0.0 if first else carry["rr"][(c - 1) % 2][:, d, :], ALU.mult, ALU.add),
                e_a, e_b, prev.get("rr"))
        save_column("rr", b.rr[:, :, CH - 1:CH], c, r_ready)
        ln_r = do(S, lambda: S.e.activation(b.eb[:], b.rr[:], ACT.Ln), r_ready)
        yield
        col = start_column("pp", b.pp, c, NEG)
        pp = do(V, lambda: V.e.tensor_tensor(b.pp[:, :, 1:], b.eb[:], b.mx[:, :, 1:], ALU.add), ln_r, col)
        save_column("pp", b.pp[:, :, CH:], c, pp)
        d1 = do(V, lambda: V.e.tensor_tensor(b.d1[:], b.pp[:, :, 0:CH], b.k[:], ALU.subtract), pp)
        neg = do(V, lambda: V.e.tensor_scalar(b.ea[:], b.d1[:], 0.0, None, ALU.min), d1)
        pos = do(V, lambda: V.e.tensor_scalar(b.kw[:], b.d1[:], 0.0, None, ALU.max), d1)
        e1u = do(S, lambda: S.e.activation(b.ea[:], b.ea[:], ACT.Exp), neg)
        e2u = do(S, lambda: S.e.activation(b.kw[:], b.kw[:], ACT.Exp, scale=-1.0), pos)
        yield
        bv = do(G, lambda: G.e.tensor_tensor(b.kw[:], b.kw[:], b.v[:], ALU.mult), e2u, proj["v"])
        col = start_column("aa", b.aa, c, 0.0)
        for d in range(DT):
            aa = do(V, lambda: V.e.tensor_tensor_scan(
                b.aa[:, d, 1:], b.ea[:, d, :], b.kw[:, d, :], b.aa[:, d, 0:1], ALU.mult, ALU.add), e1u, bv, col)
        save_column("aa", b.aa[:, :, CH:], c, aa)
        yield
        for d in range(DT):
            S.wait(ln_r, d1)
            g1 = S.did(S.e.activation(b.eb[:, d, :], b.d1[:, d, :], ACT.Sigmoid, bias=nu[:, d:d + 1]))
            g2 = do(S, lambda: S.e.activation(b.rr[:, d, :], b.d1[:, d, :], ACT.Sigmoid,
                                              bias=vec[:, d, U:U + 1], scale=-1.0), prev["rr"])
        sr = do(S, lambda: S.e.activation(b.sr[:], b.sr[:], ACT.Sigmoid), proj["r"])
        ya = do(G, lambda: G.e.tensor_tensor(b.eb[:], b.eb[:], b.aa[:, :, 0:CH], ALU.mult), g1, aa)
        yb = do(V, lambda: V.e.tensor_tensor(b.rr[:], b.rr[:], b.v[:], ALU.mult), g2)
        y = do(V, lambda: V.e.tensor_tensor(b.rr[:], b.rr[:], b.eb[:], ALU.add), ya, yb)
        gated = do(V, lambda: V.e.tensor_tensor(b.rr[:], b.rr[:], b.sr[:], ALU.mult), y, sr)
        yield
        for i in range(0, TPC, 2):
            f = bank("t")
            T.wait(gated, f.free)
            for j in range(2):
                for k in range(DT):
                    T.did(T.e.transpose(f.ap[:, j * D + k * P:j * D + (k + 1) * P],
                                        b.rr[:, k, (i + j) * P:(i + j + 1) * P], K.ident[:]))
            x1 = f.free = do(V, lambda: V.e.tensor_tensor(
                b.xn[:, i:i + 2, :], b.xn[:, i:i + 2, :], f.ap[:].rearrange("p (a c) -> p a c", a=2), ALU.add), T.own())
        yield
        grown = do(V, lambda: V.e.tensor_tensor(x4, x4, b.xn[:], ALU.add), x1)
        h_ready = layernorm_tiles(K, b, b.xn, b.hh, TPC, x1)
        yield
        col = start_column("xb", b.mx, c, 0.0, [pp, d_a, d_b, prev["mx"]])
        xb_ready = to_channels(b.hh, b.mx, G2, B2, h_ready, [pp, d_a, d_b, prev["mx"]])
        save_column("xb", b.mx[:, :, CH:], c, list(xb_ready))
        xb_ready.append(col)
        mk = mixed(b.mx, b.m0, "ck", xb_ready, read)
        mr = mixed(b.mx, b.k, "cr", xb_ready, d1)
        yield
        for h in range(KH):
            f = bank("k")
            T.wait(mk, f.free)
            for k in range(DT):
                T.did(T.e.matmul(f.ap[:], w_ck[:, k, h * P:(h + 1) * P], b.m0[:, k, :],
                                 start=k == 0, stop=k == DT - 1))
            relu = f.free = do(S, lambda: S.e.activation(kc[:, h, :], f.ap[:], ACT.Relu), T.own(), kc_free[0])
            sq = do(V, lambda: V.e.tensor_tensor(kc[:, h, :], kc[:, h, :], kc[:, h, :], ALU.mult), relu)
            if h % 2:
                yield
        for i in range(TPC):
            f = bank("o")
            T.wait(mr, sq, f.free)
            for k in range(DT):
                T.did(T.e.matmul(f.ap[:, 0:D], b.k[:, k, i * P:(i + 1) * P], w["cr"][:, k, :],
                                 start=k == 0, stop=k == DT - 1))
            c_made = T.own()
            for h in range(KH):
                T.did(T.e.matmul(f.ap[:, D:2 * D], kc[:, h, i * P:(i + 1) * P], w_cv[:, h, :],
                                 start=h == 0, stop=h == KH - 1))
            scr = do(S, lambda: S.e.activation(b.scr[:], f.ap[:, 0:D], ACT.Sigmoid), T.own(), V.own())
            prod = f.free = do(V, lambda: V.e.tensor_tensor(b.scr[:], b.scr[:], f.ap[:, D:2 * D], ALU.mult), scr)
            do(V, lambda: V.e.tensor_tensor(x4[:, i, :], x4[:, i, :], b.scr[:], ALU.add), prod, grown)
            if i % 2:
                yield
        kc_free[0] = T.own()
        b.done = [V.own(), S.own(), G.own(), T.own()]

    run_lanes(chunk, NC, 14)
    K.x_ready = V.own()
    M.free()


def expert_tiles(K, M, R, E, F, w_gu, w_d, routed, scattered, rms=False):
    V, S, G, T, Q = K.V, K.S, K.G, K.T, K.Q
    FK = F // P
    n_tiles = 2 * NT + E
    wide = 2 * F > CH
    RING = 4
    rows = [M.sb(f"rows{i}", [P, D]) for i in range(RING)]
    xT = [M.sb(f"rowsT{i}", [P, DT, P]) for i in range(2)]
    act = [M.sb(f"act{i}", [P, F]) for i in range(2)]
    mid_ = [M.sb(f"mid{i}", [P, F]) for i in range(2)]
    midT = [M.sb(f"midT{i}", [P, FK, P]) for i in range(2)]
    out = [M.sb(f"result{i}", [P, D]) for i in range(RING)]
    sq = M.sb("squares", [P, F])
    ss = [M.sb(f"sum_squares{i}", [P, 1]) for i in range(4)]
    rs = [M.sb(f"inverse_rms{i}", [P, 1]) for i in range(4)]
    if wide:
        tb = [Bank(M.ps("transposed", [P, CH]))]
        gb = [Bank(M.ps(f"gate_up{i}", [P, 2 * CH])) for i in range(2)]
        hb = [Bank(M.ps("mid_transposed", [P, CH]))]
        ob = [Bank(M.ps("result_sum", [P, CH]))]
    else:
        tb, gb, hb, ob = ([Bank(M.ps(f"{n}{i}", [P, CH])) for i in range(n_b)]
                          for n, n_b in (("transposed", 1), ("gate_up", 2), ("mid_transposed", 1), ("result_sum", 1)))
    gu_flat = w_gu[:].rearrange("p e k f -> p (e k f)")
    d_flat = w_d[:].rearrange("p e k c -> p (e k c)")
    rows_here, rows_free = {}, [None] * RING
    xT_ready, xT_free, mid_ready, mid_free, midT_ready, midT_free = {}, [None] * 2, {}, [None] * 2, {}, [None] * 2
    rs_ready, stored, expert = {}, [None] * RING, {}
    Q.wait(scattered)
    T.wait(routed)

    def load(j):
        Q.wait(rows_free[j % RING])
        rows_here[j] = K.dma(Q, rows[j % RING][:], K.sorted_in[j * P:(j + 1) * P, :], f"rows{j % RING}")

    def transpose(j):
        b = tb[j % len(tb)]
        T.wait(rows_here[j], b.free)
        for k in range(DT):
            T.did(T.e.transpose(b.ap[:, k * P:(k + 1) * P], rows[j % RING][:, k * P:(k + 1) * P], K.ident[:]))
        rows_free[j % RING] = T.own()
        b.free = xT_ready[j] = do(S, lambda: S.e.activation(
            xT[j % 2][:], b.ap[:, 0:DT * P].rearrange("p (k q) -> p k q", k=DT), ACT.Copy), T.own(), xT_free[j % 2])

    def up(j):
        b = gb[j % len(gb)]
        expert[j] = T.e.value_load(R.tile_expert[0:1, j:j + 1], min_val=0, max_val=E - 1)
        T.wait(xT_ready[j], b.free)
        for at in range(0, 2 * F, CH):
            n = min(CH, 2 * F)
            for k in range(DT):
                T.did(T.e.matmul(b.ap[:, at:at + n], xT[j % 2][:, k, :],
                                 gu_flat[:, bass.ds(expert[j] * (DT * 2 * F) + (k * 2 * F + at), n)],
                                 start=k == 0, stop=k == DT - 1))
        xT_free[j % 2] = T.own()
        gate = do(S, lambda: S.e.activation(act[j % 2][:], b.ap[:, 0:F], ACT.Silu), T.own(), mid_ready.get(j - 2))
        b.free = mid_ready[j] = do(V, lambda: V.e.tensor_tensor(
            mid_[j % 2][:], act[j % 2][:], b.ap[:, F:2 * F], ALU.mult), gate, mid_free[j % 2], rs_ready.get(j - 2))
        if rms:
            s4 = ss[j % 4]
            sqd = do(S, lambda: S.e.activation(sq[:], mid_[j % 2][:], ACT.Square, accum_out=s4[:]),
                     mid_ready[j], rs_ready.get(j - 4), S.own())
            ve = do(V, lambda: V.e.tensor_scalar(s4[:], s4[:], 1.0 / F, 1e-6, ALU.mult, ALU.add), sqd)
            rs_ready[j] = do(G, lambda: G.e.tensor_tensor(rs[j % 4][:], s4[:], K.neghalf[:, 0:1], ALU.pow),
                             ve, stored_mark.get(j - 4))

    stored_mark = {}

    def turn(j):
        b = hb[j % len(hb)]
        T.wait(mid_ready[j], b.free)
        for k in range(FK):
            T.did(T.e.transpose(b.ap[:, k * P:(k + 1) * P], mid_[j % 2][:, k * P:(k + 1) * P], K.ident[:]))
        mid_free[j % 2] = T.own()
        b.free = midT_ready[j] = do(V, lambda: V.e.tensor_copy(
            midT[j % 2][:], b.ap[:, 0:F].rearrange("p (k q) -> p k q", k=FK)), T.own(), midT_free[j % 2])

    def down(j):
        b = ob[j % len(ob)]
        T.wait(midT_ready[j], b.free)
        for k in range(FK):
            T.did(T.e.matmul(b.ap[:, 0:D], midT[j % 2][:, k, :],
                             d_flat[:, bass.ds(expert[j] * (FK * D) + k * D, D)], start=k == 0, stop=k == FK - 1))
        midT_free[j % 2] = T.own()
        o = out[j % RING]
        if rms:
            b.free = do(S, lambda: S.e.activation(o[:], b.ap[:, 0:D], ACT.Copy, scale=rs[j % 4][:]),
                        T.own(), stored[j % RING], rs_ready[j])
        else:
            b.free = do(S, lambda: S.e.activation(o[:], b.ap[:, 0:D], ACT.Copy), T.own(), stored[j % RING])
        stored_mark[j] = b.free
        Q.wait(b.free)
        stored[j % RING] = K.dma(Q, K.sorted_out[j * P:(j + 1) * P, :], o[:], f"store{j % RING}")

    for j in range(RING - 1):
        load(j)
    for i in range(n_tiles + 3):
        if i < n_tiles:
            transpose(i)
        if 0 <= i - 1 < n_tiles:
            up(i - 1)
        if 0 <= i - 2 < n_tiles:
            turn(i - 2)
        if 0 <= i - 3 < n_tiles:
            down(i - 3)
        if i + RING - 1 < n_tiles:
            load(i + RING - 1)
    K.sorted_read = [rows_here[j] for j in range(n_tiles - RING, n_tiles)]
    return stored


def ssm1_stage(K, W):
    V, S, G, T, Q = K.V, K.S, K.G, K.T, K.Q
    X, E, F, NS = K.X, 4, 512, 16
    M = Memory(K)
    R = Routing(K, M, E)
    y_rows = M.sb("y_rows", [P, NT, D])
    norm_w = M.sb("norm_w", [P, D])
    M0, M = M, Memory(K)
    ln_buffers(M, TPC)
    w_delta = M.sb("w_delta", [P, DT, D])
    w_bc = M.sb("w_bc", [P, DT, 3, 2 * NS])
    w_router = M.sb("w_router", [P, DT, E])
    vec = M.sb("ssm_vectors", [P, DT, 2])
    A = M.sb("A", [P, DT, NS])
    sel = M.sb("selectors", [96, 32, P], BF16)
    K.dma(Q, w_delta[:], W["L1_attn_a_W_delta"].rearrange("(k p) e -> p k e", p=P), "weights")
    K.dma(Q, w_router[:], W["L1_attn_a_W_router"].rearrange("(k p) e -> p k e", p=P), "weights")
    for j in range(3):
        K.dma(Q, w_bc[:, :, j, 0:NS], W["L1_attn_a_W_B"].rearrange("(k p) e -> p k e", p=P), "weights")
        K.dma(Q, w_bc[:, :, j, NS:], W["L1_attn_a_W_C"].rearrange("(k p) e -> p k e", p=P), "weights")
    K.dma(Q, vec[:], W["ssm_vectors"], "weights")
    K.dma(Q, A[:], W["L1_attn_a_A_log"].rearrange("(k p) n -> p k n", p=P), "weights")
    K.dma(Q, norm_w[:], W["L1_norm_w"], "weights")
    loaded = K.dma(Q, sel[:], W["const_selectors"], "weights")
    S.wait(loaded)
    V.wait(S.did(S.e.activation(A[:], A[:], ACT.Exp)))
    a_ready = V.did(V.e.tensor_scalar(A[:], A[:], -1.0, None, ALU.mult))
    for e in (V, S, G, T):
        e.wait(loaded, a_ready)

    sc = Scan(K, M, DT, NS)
    xn = M.sb("xn", [P, TPC, D])
    xT = [M.sb(f"xT{i}", [P, DT, CH]) for i in range(2)]
    dt = [M.sb(f"dt{i}", [P, DT, CH]) for i in range(2)]
    dtu = [M.sb(f"dtu{i}", [P, DT, CH]) for i in range(2)]
    BC3 = [M.sb(f"BC3_{i}", [96, CH], BF16) for i in range(2)]
    y = [M.sb(f"y{i}", [P, DT, CH]) for i in range(2)]
    rest, ab = M.sb("bc_rest", [96, CH]), M.sb("softplus", [P, DT, CH])
    stat = M.sb("stat", [P, 4])
    small = M.sb("bound", [1, 8])
    flag = [M.sb(f"clip_flag{i}", [1, 1], I32) for i in range(2)]
    state = M.sb("clipped_state", [P, DT])
    fp = M.ps("front", [P, CH])
    st = {"bank": None, "ready": [None, None], "done": [None, None], "xn_free": None}
    V.did(V.e.memset(stat[:], 0.0))
    V.did(V.e.memset(small[:], 0.0))
    V.wait(V.own())

    def front(c):
        r = c % 2
        V.wait(st["done"][r])
        normed = layernorm_tiles(K, M, X[:, TPC * c:TPC * (c + 1), :], xn, TPC, [st["xn_free"], K.x_ready])
        yield
        yield
        for k in range(DT):
            T.wait(normed, st["bank"])
            for i in range(TPC):
                T.did(T.e.transpose(fp[:, i * P:(i + 1) * P], xn[:, i, k * P:(k + 1) * P], K.ident[:]))
            st["xn_free"] = made = T.own()
            yield
            st["bank"] = do(S, lambda: S.e.activation(xT[r][:, k, :], fp[:], ACT.Copy), made, st["done"][r])
            yield
        x_here = st["bank"]
        T.wait(x_here)
        for k in range(DT):
            T.did(T.e.matmul(fp[0:96, :], w_bc[:, k, :, :].rearrange("p a b -> p (a b)"), xT[r][:, k, :],
                             start=k == 0, stop=k == DT - 1))
        made = T.own()
        yield
        max_b = do(V, lambda: V.e.tensor_reduce(stat[0:NS, 2:3], fp[0:NS, :], AX.X, ALU.max,
                                                apply_absolute_value=True), made, V.own(), st.get("stat_read"))
        st["bank"] = split_done = split3(K, fp, BC3[r], rest, [made, st["done"][r], V.own()])
        yield
        for d in range(DT):
            T.wait(st["bank"])
            for k in range(DT):
                T.did(T.e.matmul(fp[:], w_delta[:, k, d * P:(d + 1) * P], xT[r][:, k, :],
                                 start=k == 0, stop=k == DT - 1))
            made = T.own()
            yield
            a1 = do(S, lambda: S.e.activation(ab[:, d, :], fp[:], ACT.Abs, bias=vec[:, d, 0:1]), made, st.get("ab_free"))
            st["bank"] = do(V, lambda: V.e.tensor_scalar(dt[r][:, d, :], fp[:], vec[:, d, 0:1], 0.0, ALU.add, ALU.max), a1)
            yield
        e1 = do(S, lambda: S.e.activation(ab[:], ab[:], ACT.Exp, scale=-1.0), S.own())
        e2 = do(S, lambda: S.e.activation(ab[:], ab[:], ACT.Ln, bias=1.0), e1)
        yield
        yield
        made_dt = do(V, lambda: V.e.tensor_tensor(dt[r][:], dt[r][:], ab[:], ALU.add), e2, V.own())
        made_dtu = do(G, lambda: G.e.tensor_tensor(dtu[r][:], dt[r][:], xT[r][:], ALU.mult), made_dt)
        yield
        yield
        s1 = do(V, lambda: V.e.tensor_reduce(stat[:, 0:1], dt[r][:], AX.XY, ALU.max), made_dt, max_b)
        s2 = do(V, lambda: V.e.tensor_reduce(ab[:, :, 0], dtu[r][:], AX.X, ALU.add, apply_absolute_value=True), made_dtu)
        s3 = do(V, lambda: V.e.tensor_reduce(stat[:, 1:2], ab[:, :, 0], AX.X, ALU.max), s2)
        T.wait(s1, s3, st["bank"])
        for j in range(3):
            T.did(T.e.matmul(fp[0:1, j * P:(j + 1) * P], stat[:, j:j + 1], K.ident[:], start=True, stop=True))
        st["ab_free"] = s3
        made = st["stat_read"] = T.own()
        yield

        def v(inst):
            V.wait(V.did(inst))
        V.wait(made)
        v(V.e.tensor_reduce(small[:, 0:3], fp[0:1, 0:3 * P].rearrange("p (a b) -> p a b", a=3), AX.X, ALU.max))
        st["bank"] = V.own()
        v(V.e.tensor_tensor(small[:, 3:5], small[:, 0:2], small[:, 2:3].to_broadcast([1, 2]), ALU.mult))
        if c % CPB:
            v(V.e.tensor_tensor(small[:, 5:6], small[:, 5:6], small[:, 4:5], ALU.add))
        else:
            v(V.e.tensor_copy(small[:, 5:6], small[:, 4:5]))
        v(V.e.tensor_scalar(small[:, 6:7], small[:, 3:4], BAR_B_MAX * 0.99, None, ALU.is_gt))
        v(V.e.tensor_scalar(small[:, 7:8], small[:, 5:6], H_MAX * 0.99, None, ALU.is_gt))
        v(V.e.tensor_tensor(small[:, 6:7], small[:, 6:7], small[:, 7:8], ALU.add))
        flagged = do(V, lambda: V.e.tensor_copy(flag[r][:], small[:, 6:7]))
        st["ready"][r] = [made_dtu, made_dt, split_done]
        st["flag"] = flagged
        yield

    regs = {}

    def clipped(sc, r, n, c):
        if n == 0:
            V.wait(st["flag"])
            regs[c] = V.e.value_load(flag[c % 2][0:1, 0:1], min_val=0, max_val=2)
        q = c % 2
        with V.e.If(regs[c] > 0):
            V.e.drain()
            for d in range(DT):
                V.e.tensor_tensor(sc.dBu[r][:, d, :], dt[q][:, d, :], sc.Bb[r][:], ALU.mult)
            V.e.drain()
            V.e.tensor_scalar(sc.dBu[r][:], sc.dBu[r][:], BAR_B_MAX, -BAR_B_MAX, ALU.min, ALU.max)
            V.e.drain()
            V.e.tensor_tensor(sc.dBu[r][:], sc.dBu[r][:], xT[q][:], ALU.mult)
            if c % CPB:
                V.e.tensor_copy(state[:], sc.carry[:, n, :])
            else:
                V.e.memset(state[:], 0.0)
            with V.e.Fori(0, CH) as t:
                V.e.drain()
                V.e.tensor_tensor(state[:], state[:], sc.dA[r][:, :, bass.ds(t, 1)], ALU.mult)
                V.e.drain()
                V.e.tensor_tensor(state[:], state[:], sc.dBu[r][:, :, bass.ds(t, 1)], ALU.add)
                V.e.drain()
                V.e.tensor_scalar(state[:], state[:], H_MAX, -H_MAX, ALU.min, ALU.max)
                V.e.drain()
                V.e.tensor_copy(sc.h[r][:, :, bass.ds(t, 1)], state[:])
            V.e.drain()

    def back(c):
        r = c % 2
        V.wait(sc.summed[0], sc.summed[1], st["done"][r])
        for d in range(DT):
            V.did(V.e.scalar_tensor_tensor(y[r][:, d, :], xT[r][:, d, :], vec[:, d, 1:2], sc.y[d][:],
                                           ALU.mult, ALU.add))
        sc.y_free = y_made = V.own()
        T.wait(y_made)
        for i in range(TPC):
            for k in range(DT):
                T.did(T.e.matmul(R.logits[:, TPC * c + i, :], y[r][:, k, i * P:(i + 1) * P], w_router[:, k, :],
                                 start=k == 0, stop=k == DT - 1))
        for i in range(0, TPC, 2):
            T.wait(st["bank"])
            for j in range(2):
                for k in range(DT):
                    T.did(T.e.transpose(fp[:, j * D + k * P:j * D + (k + 1) * P],
                                        y[r][:, k, (i + j) * P:(i + j + 1) * P], K.ident[:]))
            st["bank"] = do(S, lambda: S.e.activation(
                y_rows[:, TPC * c + i:TPC * c + i + 2, :], fp[:].rearrange("p (a c) -> p a c", a=2), ACT.Copy), T.own())
        st["done"][r] = [T.own(), V.own()]

    sc.pairs = 11
    run_scan(sc, front, back, lambda c: (dt[c % 2], dtu[c % 2][:], BC3[c % 2][:], A, sel, st["ready"][c % 2]),
             clipped)
    M.free()
    M = M0
    w_gu = M.sb("w_gate_up", [P, E, DT, 2 * F])
    w_d = M.sb("w_down", [P, E, F // P, D])
    gain = M.sb("inner_gain", [P, E, F // P])
    K.dma(Q, gain[:], W["L1_inner_gain"], "weights")
    for e in range(E):
        for j, n in enumerate(("Wg", "Wu")):
            K.dma(Q, w_gu[:, e, :, j * F:(j + 1) * F], W["L1_attn_a_" + n][e].rearrange("(k p) f -> p k f", p=P), "weights")
        loaded = K.dma(Q, w_d[:, e, :, :], W["L1_attn_a_Wd"][e].rearrange("(k p) c -> p k c", p=P), "weights")
    routed = R.run(T.own(), normalise=True)
    scattered = R.scatter(y_rows, routed)
    V.wait(loaded)
    folded = V.did(V.e.tensor_tensor(w_d[:].rearrange("p e k c -> p (e k) c"), w_d[:].rearrange("p e k c -> p (e k) c"),
                                     last(gain[:].rearrange("p e k -> p (e k)"), D), ALU.mult))
    T.wait(loaded, folded)
    stored = expert_tiles(K, M, R, E, F, w_gu, w_d, routed, scattered, rms=True)
    V.wait(scattered)
    R.combine(stored, y_rows)
    sums, rt = M.sb("y_sums", [P, NT]), M.sb("y_rms", [P, NT])
    sq = M.sb("y_squares", [P, D])
    S.wait(V.own())
    for t in range(NT):
        do(S, lambda: S.e.activation(sq[:], y_rows[:, t, :], ACT.Square, accum_out=sums[:, t:t + 1]), S.own())
    ve = do(V, lambda: V.e.tensor_scalar(sums[:], sums[:], 1.0 / D, 1e-6, ALU.mult, ALU.add), S.own())
    rt_ready = do(G, lambda: G.e.tensor_tensor(rt[:], sums[:], K.neghalf[:], ALU.pow), ve)
    scaled = do(V, lambda: V.e.tensor_tensor(y_rows[:], y_rows[:], mid(norm_w[:], NT), ALU.mult), S.own())
    for t in range(NT):
        do(V, lambda: V.e.scalar_tensor_tensor(X[:, t, :], y_rows[:, t, :], rt[:, t:t + 1], X[:, t, :],
                                               ALU.mult, ALU.add), rt_ready, scaled)
    K.x_ready = V.own()
    M.free()


def moe1_stage(K, W):
    V, S, G, T, Q = K.V, K.S, K.G, K.T, K.Q
    X, E, F, FS = K.X, 16, 128, 256
    M = Memory(K)
    R = Routing(K, M, E)
    ln_buffers(M, TPC)
    xn = M.sb("xn", [P, NT, D])
    wr = M.sb("w_router", [P, DT, E])
    w_s = M.sb("w_shared_gate_up", [P, DT, 2 * FS])
    w_sd = M.sb("w_shared_down", [P, FS // P, D])
    w_gu = M.sb("w_gate_up", [P, E, DT, 2 * F])
    w_d = M.sb("w_down", [P, E, 1, D])
    rows_of = lambda n: W["L1_ffn_" + n].rearrange("(k p) e -> p k e", p=P)
    K.dma(Q, wr[:], rows_of("Wr"), "weights")
    K.dma(Q, w_s[:, :, 0:FS], rows_of("Sg"), "weights")
    K.dma(Q, w_s[:, :, FS:], rows_of("Su"), "weights")
    shared_here = K.dma(Q, w_sd[:], rows_of("Sd"), "weights")
    for j, n in enumerate(("Wg", "Wu")):
        for e in range(E):
            K.dma(Q, w_gu[:, e, :, j * F:(j + 1) * F], W["L1_ffn_" + n][e].rearrange("(k p) f -> p k f", p=P), "experts")
    experts_here = K.dma(Q, w_d[:, :, 0, :], W["L1_ffn_Wd"].rearrange("e p c -> p e c"), "experts")
    xT = [M.sb(f"xT{i}", [P, DT, CH]) for i in range(2)]
    hs = M.sb("shared_act", [P, FS // P, CH])
    hm = M.sb("shared_mid", [P, FS // P, CH])
    MS = Memory(K)
    tbank = Bank(MS.ps("transposed_x", [P, CH]))
    sb_ = [Bank(MS.ps(f"shared{i}", [P, CH])) for i in range(3)]
    T.wait(shared_here)
    used, hm_free, nb = [None, None], None, 0
    for c in range(NC):
        r = c % 2
        _, marks = prepare_tiles(K, M, c, xn[:, TPC * c:TPC * (c + 1), :], xT[r], tbank, [used[r], K.x_ready])
        T.wait(marks)
        for i in range(TPC):
            for k in range(DT):
                T.did(T.e.matmul(R.logits[:, TPC * c + i, :], xT[r][:, k, i * P:(i + 1) * P], wr[:, k, :],
                                 start=k == 0, stop=k == DT - 1))
        logits_made = T.own()
        for f in range(FS // P):
            made = []
            for j in range(2):
                b = sb_[nb % 3]
                nb += 1
                T.wait(b.free)
                for k in range(DT):
                    T.did(T.e.matmul(b.ap[:], w_s[:, k, j * FS + f * P:j * FS + (f + 1) * P], xT[r][:, k, :],
                                     start=k == 0, stop=k == DT - 1))
                made.append((b, T.own()))
            (gb, g_made), (ub, u_made) = made
            gb.free = do(S, lambda: S.e.activation(hs[:, f, :], gb.ap[:], ACT.Silu), g_made, V.own())
            ub.free = mid_made = do(V, lambda: V.e.tensor_tensor(hm[:, f, :], hs[:, f, :], ub.ap[:], ALU.mult),
                                    gb.free, u_made, hm_free)
        used[r] = T.own()
        for i in range(0, TPC, 2):
            b = sb_[nb % 3]
            nb += 1
            T.wait(b.free, mid_made)
            for j in range(2):
                for f in range(FS // P):
                    T.did(T.e.matmul(b.ap[:, j * D:(j + 1) * D], hm[:, f, (i + j) * P:(i + j + 1) * P], w_sd[:, f, :],
                                     start=f == 0, stop=f == FS // P - 1))
            xt = X[:, TPC * c + i:TPC * c + i + 2, :]
            b.free = do(V, lambda: V.e.tensor_tensor(xt, xt, b.ap[:].rearrange("p (a c) -> p a c", a=2), ALU.add), T.own())
        hm_free = T.own()
    MS.free()
    routed = R.run(logits_made)
    scattered = R.scatter(xn, routed)
    T.wait(experts_here)
    stored = expert_tiles(K, M, R, E, F, w_gu, w_d, routed, scattered)
    K.x_ready = V.own()
    R.combine(stored, X)
    K.x_ready = V.own()
    M.free()


def attention_stage(K, W):
    V, S, G, T, Q = K.V, K.S, K.G, K.T, K.Q
    X = K.X
    HD, HU, DC = 16, 8, 64
    KT = L // P
    Q_PARTS, K_PARTS = (0, 0, 1, 0, 2, 1), (0, 1, 0, 2, 0, 1)
    ROWS = 6 * HD
    M = Memory(K)
    ln_buffers(M, TPC)
    w = {}
    for n, rows, c in (("wq", D, DC), ("wkv", D, DC), ("wqr", D, P), ("wqr_turned", D, P), ("wkr", D, P),
                       ("wkr_turned", D, P), ("wo", D, D)):
        w[n] = M.sb("w_" + n, [P, DT, c])
        K.dma(Q, w[n][:], W["attn_" + n].rearrange("(k p) c -> p k c", p=P), "weights")
    for n, c in (("wqc", P), ("wkc", P), ("wv", D)):
        w[n] = M.sb("w_" + n, [DC, c])
        K.dma(Q, w[n][:], W["attn_" + n], "weights")
    b64 = M.sb("latent_biases", [DC, 2])
    b128 = M.sb("biases", [P, 6])
    bv, bo = M.sb("bv", [P, D]), M.sb("bo", [P, D])
    cos, sin = M.sb("cos", [P, L]), M.sb("sin", [P, L])
    ident_bf = M.sb("ident_bf", [P, P], BF16)
    mask_qk, mask_kq = M.sb("mask_qk", [P, P], BF16), M.sb("mask_kq", [P, P], BF16)
    for to, n in ((b64, "attn_b64"), (b128, "attn_b128"), (bv, "attn_bv"), (bo, "attn_bo"), (cos, "const_cos"),
                  (sin, "const_sin"), (ident_bf, "const_ident_bf"), (mask_qk, "const_mask_qk"),
                  (mask_kq, "const_mask_kq")):
        loaded = K.dma(Q, to[:], W[n], "weights")
    for e in (V, S, G, T):
        e.wait(loaded)
    xn = M.sb("xn", [P, TPC, D])
    xT = M.sb("xT", [P, DT, L])
    latent = {"q": M.sb("latent_q", [DC, L]), "k": M.sb("latent_k", [DC, L])}
    pre, pre2 = M.sb("pre_gelu", [P, CH]), M.sb("rotated", [P, CH])
    full = M.sb("activated", [P, CH])
    parts = {n: M.sb("parts_" + n, [P, 3, L], BF16) for n in "qk"}
    QS = [M.sb(f"queries{i}", [ROWS + 3, HU, L], BF16) for i in range(2)]
    KS = [M.sb(f"keys{i}", [ROWS + 3, HU, L], BF16) for i in range(2)]
    V1 = [M.sb(f"values{i}", [P, KT, HU, 32]) for i in range(2)]
    mx = M.sb("maxima", [P, KT, HU, 2])
    mn = M.sb("minus_max", [P, KT * HU])
    mT = M.sb("max_rows", [KT * HU, P])
    mP = M.sb("max_parts", [KT * HU, 3, P], BF16)
    PT = [M.sb(f"weights_T{i}", [P, 4, CH]) for i in range(2)]
    oT = M.sb("out_T", [P, CH])
    rec = M.sb("reciprocal", [P, 4, 4])
    O = M.sb("out_rows", [P, KT, D])
    oTT = M.sb("out_channels", [P, DT, P])
    dram = {n: K.nc.dram_tensor(f"parts_of_{n}", [3, P, L], BF16, kind="Internal").ap() for n in "qk"}
    dram_m = K.nc.dram_tensor("parts_of_max", [3, HU, KT, P], BF16, kind="Internal").ap()
    st_ = [M.ps(f"scores_T{i}", [P, 2, CH]) for i in range(2)]
    sb2 = [Bank(M.ps(f"scores{i}", [P, CH])) for i in range(2)]
    ob, mb = Bank(M.ps("out_sum", [P, CH])), Bank(M.ps("misc", [P, CH]))
    for i in range(2):
        V.did(V.e.memset(V1[i][:], 0.0))
        V.did(V.e.memset(KS[i][ROWS:ROWS + 3, :, :], 1.0))
    V.wait(V.own())
    for i in range(2):
        V.did(V.e.memset(V1[i][:, :, :, HD], 1.0))
    V.did(V.e.memset(mx[:], -1e38))
    V.wait(V.own())
    for e in (S, T, Q):
        e.wait(V.own())
    unit_done = [None, None]
    ready = {}
    st = {"xT_free": None, "staged": {"q": None, "k": None}, "mx": None, "m_stored": None, "part_free": None}

    def unit_a(u):
        b, ct, r = u // DT, u % DT, u % 2
        if ct == 0:
            for c2 in range(CPB):
                c = b * CPB + c2
                normed = layernorm_tiles(K, M, X[:, TPC * c:TPC * (c + 1), :], xn, TPC, [st["xT_free"], K.x_ready])
                for k in range(DT):
                    T.wait(normed, mb.free)
                    for i in range(TPC):
                        T.did(T.e.transpose(mb.ap[:, i * P:(i + 1) * P], xn[:, i, k * P:(k + 1) * P], K.ident[:]))
                    st["xT_free"] = T.own()
                    mb.free = x_here = do(S, lambda: S.e.activation(xT[:, k, c2 * CH:(c2 + 1) * CH], mb.ap[:], ACT.Copy),
                                          T.own(), st["part_free"])
                    yield
            for j, (n, wn) in enumerate((("q", "wq"), ("k", "wkv"))):
                for c2 in range(CPB):
                    T.wait(x_here, mb.free)
                    for k in range(DT):
                        T.did(T.e.matmul(mb.ap[0:DC, :], w[wn][:, k, :], xT[:, k, c2 * CH:(c2 + 1) * CH],
                                         start=k == 0, stop=k == DT - 1))
                    mb.free = do(S, lambda: S.e.activation(latent[n][:, c2 * CH:(c2 + 1) * CH], mb.ap[0:DC, :],
                                                           ACT.Gelu, bias=b64[:, j:j + 1]), T.own(), st["part_free"])
                    yield
        for j, n in enumerate("qk"):
            for c2 in range(CPB):
                cs = slice(c2 * CH, (c2 + 1) * CH)
                if ct == 0:
                    T.wait(mb.free)
                    T.did(T.e.matmul(mb.ap[:], w["wqc" if n == "q" else "wkc"][:], latent[n][:, cs], start=True, stop=True))
                    mb.free = made = do(S, lambda: S.e.activation(full[:], mb.ap[:], ACT.Gelu, bias=b128[:, j:j + 1]),
                                        T.own(), st.get("full_free"))
                else:
                    marks = []
                    for i, (wn, table, to) in enumerate((("r", cos, pre), ("r_turned", sin, pre2))):
                        T.wait(mb.free)
                        for k in range(DT):
                            T.did(T.e.matmul(mb.ap[:], w["w" + n + wn][:, k, :], xT[:, k, cs],
                                             start=k == 0, stop=k == DT - 1))
                        bias = b128[:, 2 + 2 * j + i:3 + 2 * j + i]
                        mb.free = do(V, lambda: V.e.scalar_tensor_tensor(to[:], mb.ap[:], bias, table[:, cs],
                                                                         ALU.add, ALU.mult), T.own(), st.get("pre_free"))
                    summed = do(V, lambda: V.e.tensor_tensor(pre[:], pre[:], pre2[:], ALU.add), V.own())
                    made = do(S, lambda: S.e.activation(full[:], pre[:], ACT.Gelu), summed, st.get("full_free"))
                    st["pre_free"] = made
                pt = parts[n]
                p1 = do(V, lambda: V.e.tensor_copy(pt[:, 0, cs], full[:]), made, st["staged"][n])
                r1 = do(V, lambda: V.e.tensor_tensor(full[:], full[:], pt[:, 0, cs], ALU.subtract), p1)
                p2 = do(V, lambda: V.e.tensor_copy(pt[:, 1, cs], full[:]), r1)
                r2 = do(V, lambda: V.e.tensor_tensor(full[:], full[:], pt[:, 1, cs], ALU.subtract), p2)
                p3 = do(V, lambda: V.e.tensor_copy(pt[:, 2, cs], full[:]), r2)
                st["full_free"] = p3
                yield
            Q.wait(p3, st.get("stacked_" + n))
            st["staged"][n] = K.dma(Q, dram[n].rearrange("a c t -> c a t"), pt[:], "stage_" + n)
            to, order = (QS[r], Q_PARTS) if n == "q" else (KS[r], K_PARTS)
            Q.wait(st["staged"][n], unit_done[r])
            for i, part in enumerate(order):
                here = K.dma(Q, to[i * HD:(i + 1) * HD, :, :], dram[n][part].rearrange("(h d) t -> d h t", d=HD),
                             f"stack_{n}{r}")
            st["stacked_" + n] = here
        for i in range(0, KT, 4):
            T.wait(mb.free)
            for j in range(4):
                T.did(T.e.matmul(mb.ap[:, j * P:(j + 1) * P], latent["k"][:, (i + j) * P:(i + j + 1) * P],
                                 w["wv"][:, ct * P:(ct + 1) * P], start=True, stop=True))
            T_done = T.own()
            V.wait(T_done, unit_done[r])
            for j in range(4):
                mb.free = v_ready = V.did(V.e.tensor_tensor(
                    V1[r][:, i + j, :, 0:HD], mb.ap[:, j * P:(j + 1) * P].rearrange("p (h d) -> p h d", d=HD),
                    bv[:, ct * P:(ct + 1) * P].rearrange("p (h d) -> p h d", d=HD), ALU.add))
            yield
        st["part_free"] = T.own()
        T.wait(st["stacked_q"], st["stacked_k"])
        nb = 0
        V.wait(st["mx"])
        for h in range(HU):
            for qt in range(KT):
                for half in range(qt // 4 + 1):
                    f = sb2[nb % 2]
                    nb += 1
                    n_keys = min(CH, (qt + 1) * P - half * CH)
                    diagonal = half == qt // 4
                    T.wait(f.free)
                    T.did(T.e.matmul(f.ap[:, 0:n_keys], QS[r][0:ROWS, h, qt * P:(qt + 1) * P],
                                     KS[r][0:ROWS, h, half * CH:half * CH + n_keys], start=True, stop=not diagonal))
                    if diagonal:
                        T.did(T.e.matmul(f.ap[:, n_keys - P:n_keys], ident_bf[:], mask_qk[:], start=False, stop=True))
                    f.free = do(V, lambda: V.e.tensor_reduce(mx[:, qt, h, half:half + 1], f.ap[:, 0:n_keys], AX.X, ALU.max),
                                T.own())
                    yield
        neg = do(V, lambda: V.e.tensor_reduce(mn[:], mx[:], AX.X, ALU.max, negate=True), V.own(), st.get("mn_free"))
        st["mx"] = neg
        T.wait(neg, mb.free)
        st["mn_free"] = T.did(T.e.transpose(mb.ap[0:KT * HU, 0:P], mn[:], K.ident[:]))
        mb.free = c0 = do(V, lambda: V.e.tensor_copy(mT[:], mb.ap[0:KT * HU, 0:P]), T.own())
        m1 = do(V, lambda: V.e.tensor_copy(mP[:, 0, :], mT[:]), c0, st["m_stored"])
        r1 = do(V, lambda: V.e.tensor_tensor(mT[:], mT[:], mP[:, 0, :], ALU.subtract), m1)
        m2 = do(V, lambda: V.e.tensor_copy(mP[:, 1, :], mT[:]), r1)
        r2 = do(V, lambda: V.e.tensor_tensor(mT[:], mT[:], mP[:, 1, :], ALU.subtract), m2)
        m3 = do(V, lambda: V.e.tensor_copy(mP[:, 2, :], mT[:]), r2)
        Q.wait(m3, st.get("m_stacked"))
        for qt in range(KT):
            st["m_stored"] = K.dma(Q, dram_m[:, :, qt, :].rearrange("a h t -> h a t"),
                                   mP[qt * HU:(qt + 1) * HU, :, :], "stage_m")
        Q.wait(st["m_stored"])
        st["m_stacked"] = K.dma(Q, QS[r][ROWS:ROWS + 3, :, :], dram_m.rearrange("a h q t -> a h (q t)"), f"stack_m{r}")
        ready[u] = [v_ready, st["m_stacked"], st["stacked_q"], st["stacked_k"]]
        yield

    score_free, pt_free, pt_n = [None, None], [None, None], [0]
    o_read = [None]

    def unit_b(u):
        b, ct, r = u // DT, u % DT, u % 2
        T.wait(ready[u])
        for hg in range(2):
            for qh in range(2):
                last_kt = 4 * qh + 3
                for kt in range(last_kt + 1):
                    o = max(0, kt * P - qh * CH)
                    q0 = qh * CH + o
                    n = CH - o
                    pt = PT[pt_n[0] % 2]
                    for pair in range(2):
                        T.wait(score_free[pair])
                        for j in range(2):
                            h = hg * 4 + pair * 2 + j
                            diagonal = kt * P >= qh * CH
                            T.did(T.e.matmul(st_[pair][:, j, o:CH], KS[r][:, h, kt * P:(kt + 1) * P],
                                             QS[r][:, h, q0:q0 + n], start=True, stop=not diagonal))
                            if diagonal:
                                T.did(T.e.matmul(st_[pair][:, j, o:o + P], ident_bf[:], mask_kq[:], start=False, stop=True))
                        score_free[pair] = do(S, lambda: S.e.activation(
                            pt[:, 2 * pair:2 * pair + 2, o:CH], st_[pair][:, :, o:CH], ACT.Exp, scale=HD ** -0.5),
                            T.own(), pt_free[pt_n[0] % 2])
                    weighed = S.own()
                    yield
                    T.wait(weighed, ob.free if kt == 0 else None)
                    for j in range(4):
                        T.did(T.e.matmul(ob.ap[32 * j:32 * j + 32, o:CH], V1[r][:, kt, hg * 4 + j, :],
                                         pt[:, j, o:CH], start=kt == 0, stop=kt == last_kt))
                    pt_free[pt_n[0] % 2] = T.own()
                    pt_n[0] += 1
                ob.free = taken = do(S, lambda: S.e.activation(oT[:], ob.ap[:], ACT.Copy), T.own(), st.get("oT_free"))
                T.wait(taken, mb.free)
                for t in range(4):
                    T.did(T.e.transpose(mb.ap[:, t * P:(t + 1) * P], oT[:, t * P:(t + 1) * P], K.ident[:]))
                st["oT_free"] = T.own()
                v4 = mb.ap[:].rearrange("p (t h d) -> p t h d", t=4, h=4)
                rc = do(V, lambda: V.e.reciprocal(rec[:], v4[:, :, :, HD]), T.own(), st.get("rec_free"))
                h0 = (ct * HU + hg * 4) * HD
                V.wait(rc, o_read[0])
                for t in range(4):
                    V.did(V.e.tensor_tensor(
                        O[:, qh * 4 + t, h0:h0 + 4 * HD].rearrange("p (h d) -> p h d", h=4), v4[:, t, :, 0:HD],
                        last(rec[:, t, :], HD), ALU.mult))
                mb.free = st["rec_free"] = V.own()
                yield
        unit_done[r] = [T.own()]
        if ct == DT - 1:
            for t in range(KT):
                T.wait(mb.free, V.own())
                for k in range(DT):
                    T.did(T.e.transpose(mb.ap[:, k * P:(k + 1) * P], O[:, t, k * P:(k + 1) * P], K.ident[:]))
                o_read[0] = T.own()
                taken = do(S, lambda: S.e.activation(oTT[:], mb.ap[:, 0:D].rearrange("p (k q) -> p k q", k=DT), ACT.Copy),
                           T.own(), st.get("oTT_free"))
                T.wait(taken)
                for k in range(DT):
                    T.did(T.e.matmul(mb.ap[:, D:2 * D], oTT[:, k, :], w["wo"][:, k, :], start=k == 0, stop=k == DT - 1))
                st["oTT_free"] = T.own()
                xt = X[:, b * KT + t, :]
                s1 = do(V, lambda: V.e.tensor_tensor(xt, xt, mb.ap[:, D:2 * D], ALU.add), T.own(), K.x_ready)
                mb.free = s1
                do(V, lambda: V.e.tensor_tensor(xt, xt, bo[:], ALU.add), s1)
                yield

    n_units = NB * DT
    for _ in unit_a(0):
        pass
    for u in range(n_units):
        side = unit_a(u + 1) if u + 1 < n_units else iter(())
        for _ in unit_b(u):
            for _ in range(5):
                next(side, None)
        for _ in side:
            pass
    K.x_ready = V.own()
    M.free()


STAGES = {"mamba": mamba_stage, "moe0a": moe0_stage, "moe0b": moe0_stage,
          "rwkv": rwkv_stage, "ssm1": ssm1_stage, "moe1a": moe1_stage, "moe1b": moe1_stage,
          "attn": attention_stage}
ORDER = ["mamba", "moe0a", "rwkv", "moe0b", "ssm1", "moe1a", "attn", "moe1b"]


def build_program(nc, W, x_in, out, stages):
    with ExitStack() as stack:
        K = Core(nc, stack)
        K.X = stack.enter_context(nc.sbuf_tensor("residual", [P, NT, D], F32))
        K.ident = stack.enter_context(nc.sbuf_tensor("identity", [P, P], F32))
        K.neghalf = stack.enter_context(nc.sbuf_tensor("neghalf", [P, NT], F32))
        K.V.did(K.V.e.memset(K.neghalf[:], -0.5))
        half = K.V.own()
        K.dma(K.Q, K.ident[:], W["const_identity"], "x")
        K.x_ready = K.dma(K.Q, K.X[:], x_in.rearrange("(t p) c -> p t c", p=P), "x")
        for e in (K.V, K.S, K.G, K.T):
            e.wait(K.x_ready, half)
        K.iota, K.before, K.ones_bf = (stack.enter_context(nc.sbuf_tensor(n, [P, P], t)) for n, t in
                                       (("iota", F32), ("before", BF16), ("ones_bf", BF16)))
        K.dma(K.Q, K.iota[:], W["const_iota"], "const")
        K.dma(K.Q, K.before[:], W["const_before"], "const")
        consts = K.dma(K.Q, K.ones_bf[:], W["const_ones"], "const")
        K.sorted_in = nc.dram_tensor("sorted_rows", [SLOTS, D], F32, kind="Internal").ap()
        K.sorted_out = nc.dram_tensor("sorted_results", [SLOTS + 1, D], F32, kind="Internal").ap()
        zeros = stack.enter_context(nc.sbuf_tensor("zeros", [P, D], F32))
        K.G.wait(K.G.did(K.G.e.memset(zeros[:], 0.0)))
        for s0 in range(0, SLOT_TILES, 8):
            for to in (K.sorted_in, K.sorted_out):
                K.dma(K.G, to[s0 * P:(s0 + 8) * P, :].rearrange("(p a) c -> p a c", p=P), mid(zeros[:], 8), "zeros")
        K.sorted_read = K.dma(K.G, K.sorted_out[SLOTS:SLOTS + 1, :], zeros[0:1, :], "zeros")
        K.G.wait(K.sorted_read)
        for e in (K.V, K.S, K.G, K.T):
            e.wait(consts)
        for s in stages:
            STAGES[s](K, W)
        K.Q.wait(K.x_ready)
        stored = K.dma(K.Q, out.rearrange("(t p) c -> p t c", p=P), K.X[:], "out")
        K.Q.wait(stored)
        K.barrier()


def prepare(inputs):
    bf16 = mybir.dt.np(BF16)
    a = {k: np.asarray(v) for k, v in inputs.items()}
    x = np.ascontiguousarray(a.pop("L0_attn_a_x").reshape(T_ALL, D))

    def cols(v):
        return v.reshape(-1, P).T

    W = {k: np.ascontiguousarray(a["L0_attn_a_" + k[10:]]) for k in
         ("L0_attn_a_W_in", "L0_attn_a_W_out", "L0_attn_a_W_dt", "L0_attn_a_W_xproj", "L0_attn_a_A_log")}
    conv = a["L0_attn_a_conv_w"][:, 0, :]
    W["mamba_vectors"] = np.ascontiguousarray(np.stack(
        [cols(conv[:, t]) for t in range(4)]
        + [cols(a["L0_attn_a_" + n]) for n in ("conv_b", "b_dt", "D", "D")], axis=-1))
    W["mamba_ln"] = np.ascontiguousarray(np.stack([cols(a["L0_attn_a_ln_g"]), cols(a["L0_attn_a_ln_b"])], axis=-1))
    W["const_identity"] = np.eye(P, dtype=np.float32)
    sel = np.zeros((96, 32, P), np.float32)
    for j in range(32):
        sel[[j, 32 + j, 64 + j], j, :] = 1
    W["const_selectors"] = sel.astype(bf16)
    iota = np.arange(P, dtype=np.float32)
    W["const_iota"] = np.tile(iota, (P, 1))
    W["const_before"] = (iota[:, None] < iota[None, :]).astype(bf16)
    W["const_ones"] = np.ones((P, P), bf16)
    W["L0_router_T"] = np.ascontiguousarray(a["L0_ffn_W_router"].T)
    W["L0_router_bias"] = np.ascontiguousarray(np.broadcast_to(a["L0_ffn_b_router"], (P, 8)))
    for k in ("k", "v", "r", "cr", "ck", "cv"):
        W[f"rwkv_W{k}_T"] = np.ascontiguousarray(a["L0_attn_b_W" + k].T)
    W["rwkv_vectors"] = np.ascontiguousarray(np.stack([cols(a["L0_attn_b_" + n]) for n in (
        "w", "u", "rk", "rv", "rr", "crk", "crr", "ln1_g", "ln1_b", "ln2_g", "ln2_b", "w")], axis=-1))
    W["ssm_vectors"] = np.ascontiguousarray(np.stack([cols(a["L1_attn_a_b_delta"]), cols(a["L1_attn_a_D_param"])], axis=-1))
    W["L1_norm_w"] = np.ascontiguousarray(np.broadcast_to(a["L1_attn_a_norm_w"], (P, D)))
    W["L1_inner_gain"] = np.ascontiguousarray(a["L1_attn_a_wn_exp"].reshape(4, 4, P).transpose(2, 0, 1))
    for k in ("W_delta", "W_router", "W_B", "W_C", "A_log", "Wg", "Wu", "Wd"):
        W["L1_attn_a_" + k] = a["L1_attn_a_" + k]
    for k in ("Wr", "Wg", "Wu", "Wd", "Sg", "Su", "Sd"):
        W["L1_ffn_" + k] = a["L1_ffn_" + k]
    at = {k[10:]: v for k, v in a.items() if k.startswith("L1_attn_b_")}
    for k in ("wq", "wkv", "wqr", "wkr", "wqc", "wkc", "wv", "wo"):
        W["attn_" + k] = at[k]
    turn = lambda v: np.concatenate([v[..., P // 2:], v[..., :P // 2]], axis=-1)
    W["attn_wqr_turned"], W["attn_wkr_turned"] = (np.ascontiguousarray(turn(at[k])) for k in ("wqr", "wkr"))
    W["attn_b64"] = np.ascontiguousarray(np.stack([at["bq"], at["bkv"]], axis=-1))
    W["attn_b128"] = np.ascontiguousarray(np.stack(
        [at["bqc"], at["bkc"], at["bqr"], turn(at["bqr"]), at["bkr"], turn(at["bkr"])], axis=-1))
    for k in ("bv", "bo"):
        W["attn_" + k] = np.ascontiguousarray(np.broadcast_to(at[k], (P, D)))
    inv_freq = (1.0 / np.float32(10000.0) ** (np.arange(0, P, 2, dtype=np.float32) / np.float32(P))).astype(np.float32)
    freqs = np.arange(L, dtype=np.float32)[:, None] * inv_freq[None, :]
    W["const_cos"] = np.ascontiguousarray(np.cos(np.concatenate([freqs, freqs], -1)).T.astype(np.float32))
    W["const_sin"] = np.ascontiguousarray(np.sin(np.concatenate([-freqs, freqs], -1)).T.astype(np.float32))
    W["const_ident_bf"] = np.eye(P).astype(bf16)
    above = iota[:, None] < iota[None, :]
    W["const_mask_qk"] = np.where(above, -1e30, 0).astype(bf16)
    W["const_mask_kq"] = np.where(above.T, -1e30, 0).astype(bf16)
    for k in ("L0_ffn_experts_inter", "L0_ffn_experts_out"):
        W[k] = a[k]
    return x, W


def kernel(**inputs):
    import concourse.bacc as _bacc
    from concourse.bass_utils import run_bass_kernel_spmd as _run

    nc = _bacc.Bacc("TRN2", target_bir_lowering=False, num_devices=1)
    x, W = prepare(inputs)
    arrays = {"in_x": x, **{"in_" + k: np.ascontiguousarray(v) for k, v in W.items()}}
    aps = {k: nc.dram_tensor(k, v.shape, mybir.dt.from_np(v.dtype), kind="ExternalInput").ap()
           for k, v in arrays.items()}
    out = nc.dram_tensor("out_x", (T_ALL, D), F32, kind="ExternalOutput").ap()
    build_program(nc, {k: aps["in_" + k] for k in W}, aps["in_x"], out, ORDER)
    r = _run(nc, [arrays], core_ids=[0])
    return r.results[0]["out_x"].reshape(NB, L, D)
```

```python
import itertools
from contextlib import ExitStack

import numpy as np
import concourse.bass as bass
from concourse import mybir

F32, BF16, I32 = mybir.dt.float32, mybir.dt.bfloat16, mybir.dt.int32
ACT, ALU, AX = mybir.ActivationFunctionType, mybir.AluOpType, mybir.AxisListType

P = 128
NB, L, D = 4, 1024, 256
T_ALL = NB * L
NT = T_ALL // P
DT = D // P
CH = 512
NC = T_ALL // CH
TPC = CH // P
CPB = L // CH
LN_EPS = 1e-5
BAR_B_MAX, H_MAX = 10.0, 10000.0


class Engine:

    def __init__(self, eng, name, stack, nc):
        self.e, self.n, self.seen = eng, 0, {}
        self.sem = stack.enter_context(nc.semaphore("done_" + name))

    def did(self, inst):
        self.n += 1
        inst.then_inc(self.sem, 1)
        return (self.sem, self.n)

    def wait(self, *marks):
        for m in marks:
            if m is None:
                continue
            if type(m) is list:
                self.wait(*m)
                continue
            sem, value = m
            if self.seen.get(sem.name, 0) < value:
                self.e.wait_ge(sem, value)
                self.seen[sem.name] = value

    def own(self):
        return (self.sem, self.n)


class Core:
    def __init__(self, nc, stack):
        self.nc, self.stack = nc, stack
        self.V = Engine(nc.vector, "vector", stack, nc)
        self.S = Engine(nc.scalar, "scalar", stack, nc)
        self.G = Engine(nc.gpsimd, "gpsimd", stack, nc)
        self.T = Engine(nc.tensor, "tensor", stack, nc)
        self.Q = Engine(nc.sync, "sync", stack, nc)
        self.streams, self.stage = {}, 0
        self.chunk_marks = [None] * NC
        self.owed, self.pending = False, None

    def dma(self, queue, out, in_, stream):
        return self.count(queue.e.dma_start(out, in_), stream)

    def count(self, inst, stream):
        if stream not in self.streams:
            self.streams[stream] = [self.stack.enter_context(self.nc.semaphore("dma_" + stream)), 0]
        s = self.streams[stream]
        s[1] += 16
        inst.then_inc(s[0], 16)
        return (s[0], s[1])

    def x_ready(self, c):
        if self.pending is not None:
            self.chunk_marks[c] = self.pending.through(TPC * (c + 1))
        return self.chunk_marks[c]

    def prefetch(self, n=1):
        if self.pending is not None:
            self.pending.prefetch(n)

    def x_is_ready(self):
        self.chunk_marks, self.pending = [self.V.own()] * NC, None

    def start_combine(self, M, ring=TPC):
        if self.owed:
            self.pending, self.owed = Combine(self, M, self.X, ring), False

    def barrier(self):
        marks = [e.own() for e in (self.V, self.S, self.G, self.T) if e.n]
        marks += [(s[0], s[1]) for s in self.streams.values()]
        for e in (self.V, self.S, self.G, self.T, self.Q):
            e.wait(*marks)


class Memory:

    def __init__(self, K):
        self.K, self.stack = K, ExitStack()
        K.stage += 1
        self.tag = f"s{K.stage}_"

    def sb(self, name, shape, dt=F32):
        return self.stack.enter_context(self.K.nc.sbuf_tensor(self.tag + name, shape, dt))

    def ps(self, name, shape, dt=F32):
        return self.stack.enter_context(self.K.nc.psum_tensor(self.tag + name, shape, dt))

    def free(self):
        self.K.barrier()
        self.stack.close()


def mid(ap, n):
    p, c = ap.shape
    return ap.unsqueeze(1).to_broadcast([p, n, c])


def last(ap, n):
    p, a = ap.shape
    return ap.unsqueeze(2).to_broadcast([p, a, n])


def layernorm_stats(K, M, src, n, wait, eps=LN_EPS):
    V, G = K.V, K.G
    st, mv, ve, rs = M.ln
    V.wait(wait)
    for i in range(n):
        V.did(V.e.bn_stats(st[:, i, :], src[:, i, :]))
    V.wait(V.own())
    for i in range(n):
        V.did(V.e.bn_aggr(mv[:, i, :], st[:, i, :]))
    V.wait(V.own())
    G.wait(V.did(V.e.tensor_scalar(ve[:, 0:n], mv[:, 0:n, 1], eps, None, ALU.add)))
    return G.did(G.e.tensor_tensor(rs[:, 0:n], ve[:, 0:n], K.neghalf[:, 0:n], ALU.pow))


def layernorm_apply(K, M, src, dst, n, stats):
    V = K.V
    st, mv, ve, rs = M.ln
    V.wait(stats)
    for i in range(n):
        V.did(V.e.tensor_scalar(dst[:, i, :], src[:, i, :], mv[:, i, 0:1], rs[:, i:i + 1],
                                ALU.subtract, ALU.mult))
    return V.own()


def layernorm_tiles(K, M, src, dst, n, wait):
    return layernorm_apply(K, M, src, dst, n, layernorm_stats(K, M, src, n, wait))


class Statistics:

    def __init__(self, M, i):
        self.ln = (M.sb(f"ln_stats{i}", [P, TPC, 6]), M.sb(f"ln_meanvar{i}", [P, TPC, 2]),
                   M.sb(f"ln_vareps{i}", [P, TPC]), M.sb(f"ln_rstd{i}", [P, TPC]))


def ln_buffers(M, n):
    M.ln = (M.sb("ln_stats", [P, n, 6]), M.sb("ln_meanvar", [P, n, 2]),
            M.sb("ln_vareps", [P, n]), M.sb("ln_rstd", [P, n]))


class Bank:

    def __init__(self, ap):
        self.ap, self.free = ap, None


def rotation(banks):
    turns = itertools.cycle(banks)
    return lambda: next(turns)


class Scan:
    AHEAD, RING = 2, 3

    def __init__(self, K, M, nd, ns):
        self.K, self.M, self.nd, self.ns = K, M, nd, ns
        self.dA = [M.sb(f"dA{i}", [P, nd, CH]) for i in range(self.RING)]
        self.dBu = [M.sb(f"dBu{i}", [P, nd, CH]) for i in range(self.RING)]
        self.Bb = [M.sb(f"Bb{i}", [P, CH]) for i in range(self.RING)]
        self.carry = M.sb("carry", [P, ns, nd])
        self.Bps = M.ps("B_rows", [P, CH])
        self.Cps = M.ps("C_rows", [P, CH])
        self.y = [M.ps(f"y_sum{i}", [P, CH]) for i in range(nd)]
        self.b_copied = self.y_free = None
        self.dbu_done, self.decayed, self.scanned, self.c_made, self.weighed, self.summed, self.b_marks = {}, {}, {}, {}, {}, {}, {}

    def rows_b(self, g, BC3, sel, ready):
        n, r, S, T = g % self.ns, g % self.RING, self.K.S, self.K.T
        T.wait(ready, self.b_copied)
        b_made = T.did(T.e.matmul(self.Bps[:], sel[:, n, :], BC3, start=True, stop=True))
        before = g - self.RING
        S.wait(b_made, self.dbu_done.get(before), self.scanned.get(before))
        self.b_copied = self.b_marks[g] = S.did(S.e.activation(self.Bb[r][:], self.Bps[:], ACT.Copy))

    def inputs(self, g, dt, dtu, A, ready):
        nd, n, r, S, G = self.nd, g % self.ns, g % self.RING, self.K.S, self.K.G
        before = g - self.RING
        S.wait(ready, self.scanned.get(before))
        for d in range(nd):
            S.did(S.e.activation(self.dA[r][:, d, :], dt[:, d, :], ACT.Exp, scale=A[:, d, n:n + 1]))
        self.decayed[g] = S.own()
        G.wait(ready, self.b_marks[g], self.summed.get(before))
        self.dbu_done[g] = G.did(G.e.tensor_tensor(self.dBu[r][:], dtu, mid(self.Bb[r][:], nd), ALU.mult))

    def rows_c(self, g, BC3, sel, ready):
        T, n = self.K.T, g % self.ns
        T.wait(ready, self.weighed.get(g - 1))
        self.c_made[g] = T.did(T.e.matmul(self.Cps[:], sel[:, 16 + n, :], BC3, start=True, stop=True))

    def scan(self, g, general=None):
        nd, V = self.nd, self.K.V
        c, n, r = g // self.ns, g % self.ns, g % self.RING
        V.wait(self.decayed[g], self.dbu_done[g])
        for d in range(nd):
            V.did(V.e.tensor_tensor_scan(
                self.dBu[r][:, d, :], self.dA[r][:, d, :], self.dBu[r][:, d, :],
                0.0 if c % CPB == 0 else self.carry[:, n, d:d + 1], ALU.mult, ALU.add))
        if general is not None:
            general(self, r, n, c)
        self.scanned[g] = V.own()

    def weigh(self, g):
        nd, V, n, r = self.nd, self.K.V, g % self.ns, g % self.RING
        V.wait(self.scanned[g])
        V.did(V.e.tensor_copy(self.carry[:, n, :], self.dBu[r][:, :, CH - 1]))
        V.wait(self.c_made[g], V.own())
        self.weighed[g] = V.did(V.e.tensor_tensor(
            self.dBu[r][:], self.dBu[r][:], mid(self.Cps[:], nd), ALU.mult))

    def total(self, g):
        T, n, r = self.K.T, g % self.ns, g % self.RING
        T.wait(self.weighed[g])
        if n == 0:
            T.wait(self.y_free)
        for d in range(self.nd):
            T.did(T.e.matmul(self.y[d][:], self.K.ident[:], self.dBu[r][:, d, :],
                             start=n == 0, stop=n == self.ns - 1))
        self.summed[g] = T.own()


def run_scan(sc, front, take_y, back, operands, general=None):
    n_side = sum(1 for _ in front(0))
    last_side = sc.ns - 1 - sc.AHEAD
    n_total = NC * sc.ns

    def rows_b(g):
        dt, dtu, BC3, A, sel, ready = operands(g // sc.ns)
        sc.rows_b(g, BC3, sel, ready)

    def rows_c(g):
        dt, dtu, BC3, A, sel, ready = operands(g // sc.ns)
        sc.rows_c(g, BC3, sel, ready)

    def inputs(g):
        dt, dtu, BC3, A, sel, ready = operands(g // sc.ns)
        sc.inputs(g, dt, dtu, A, ready)

    for g in range(sc.AHEAD):
        rows_b(g)
        inputs(g)
    rows_c(0)
    for c in range(NC):
        side = itertools.chain(back(c - 1) if c else (), front(c + 1) if c + 1 < NC else ())
        pairs = -(-(n_side + 6) // 2)
        for n in range(sc.ns):
            g = c * sc.ns + n
            left = last_side + 1 - n
            take = -(-pairs // left) if left > 0 and n else 0
            pairs -= take
            if left == 0:
                for _ in side:
                    pass
            ahead = g + sc.AHEAD < n_total
            if ahead:
                rows_b(g + sc.AHEAD)
            if take:
                next(side, None)
            sc.scan(g, general)
            if take > 1:
                next(side, None)
                next(side, None)
            sc.weigh(g)
            if g + 1 < n_total:
                rows_c(g + 1)
            if n == 0 and c:
                take_y(c - 1)
            sc.total(g)
            for _ in range(1 + 2 * max(0, take - 2) if take else 0):
                next(side, None)
            if ahead:
                inputs(g + sc.AHEAD)
    take_y(NC - 1)
    for _ in back(NC - 1):
        pass


def split3(K, src, dst, rest, ready):
    V = K.V
    V.wait(ready)
    V.wait(V.did(V.e.tensor_copy(dst[0:96, :], src[0:96, :])))
    V.did(V.e.tensor_tensor(rest[32:64, :], src[32:64, :], dst[32:64, :], ALU.subtract))
    V.wait(V.did(V.e.tensor_tensor(rest[64:96, :], src[64:96, :], dst[64:96, :], ALU.subtract)))
    V.did(V.e.tensor_copy(dst[32:64, :], rest[32:64, :]))
    V.wait(V.did(V.e.tensor_copy(dst[64:96, :], rest[64:96, :])))
    V.wait(V.did(V.e.tensor_tensor(rest[64:96, :], rest[64:96, :], dst[64:96, :], ALU.subtract)))
    return V.did(V.e.tensor_copy(dst[64:96, :], rest[64:96, :]))


def mamba_stage(K, W):
    V, S, G, T, Q = K.V, K.S, K.G, K.T, K.Q
    X = K.X
    DI, NS, R = 512, 16, 16
    ND = DI // P
    M = Memory(K)
    ln_buffers(M, TPC)
    w_in = M.sb("w_in", [P, DT, 2 * DI])
    w_bc = M.sb("w_bc", [P, ND, 3, 2 * NS])
    w_dtr = M.sb("w_dtr", [P, ND, R])
    w_dt = M.sb("w_dt", [R, DI])
    w_out = M.sb("w_out", [P, ND, D])
    vec = M.sb("mamba_vectors", [P, ND, 8])
    lnv = M.sb("mamba_ln", [P, DT, 2])
    A = M.sb("A", [P, ND, NS])
    sel = M.sb("selectors", [96, 32, P], BF16)
    loads = [
        K.dma(Q, w_in[:], W["L0_attn_a_W_in"].rearrange("(k p) e -> p k e", p=P), "weights"),
        K.dma(Q, w_out[:], W["L0_attn_a_W_out"].rearrange("(k p) e -> p k e", p=P), "weights"),
        K.dma(Q, w_dt[:], W["L0_attn_a_W_dt"], "weights"),
        K.dma(Q, w_dtr[:], W["L0_attn_a_W_xproj"].rearrange("(k p) e -> p k e", p=P)[:, :, 0:R], "weights"),
        K.dma(Q, vec[:], W["mamba_vectors"], "weights"),
        K.dma(Q, lnv[:], W["mamba_ln"], "weights"),
        K.dma(Q, A[:], W["L0_attn_a_A_log"].rearrange("(k p) n -> p k n", p=P), "weights"),
        K.dma(Q, sel[:], W["const_selectors"], "weights"),
    ]
    for j in range(3):
        loads.append(K.dma(Q, w_bc[:, :, j, :], W["L0_attn_a_W_xproj"].rearrange("(k p) e -> p k e", p=P)[:, :, R:], "weights"))
    loaded = loads[-1]
    zero_rows(K, [loaded] + K.chunk_marks)
    S.wait(loaded)
    S.wait(S.did(S.e.activation(A[:], A[:], ACT.Exp)))
    V.wait(S.own())
    a_ready = V.did(V.e.tensor_scalar(A[:], A[:], -1.0, None, ALU.mult))
    for e in (V, S, G, T):
        e.wait(loaded, a_ready)

    sc = Scan(K, M, ND, NS)
    xn = M.sb("xn", [P, TPC, D])
    hT = M.sb("hT", [P, DT, CH])
    uraw = M.sb("uraw", [P, ND, 3 + CH])
    cv = M.sb("conv", [P, ND, CH])
    zs = [M.sb(f"z{i}", [P, ND, CH]) for i in range(2)]
    u = [M.sb(f"u{i}", [P, ND, CH]) for i in range(2)]
    dt = [M.sb(f"dt{i}", [P, ND, CH]) for i in range(2)]
    dtu = [M.sb(f"dtu{i}", [P, ND, CH]) for i in range(2)]
    BC3 = [M.sb(f"BC3_{i}", [96, CH], BF16) for i in range(2)]
    rest = M.sb("bc_rest", [96, CH])
    dtr = M.sb("dt_rank", [R, CH])
    pick = rotation([Bank(M.ps(f"front{i}", [P, CH])) for i in range(2)])
    st = {"chunk_done": [None, None], "hT_free": None, "ready": [None, None],
          "hist": None, "u_free": None}

    def front(c):
        r = c % 2
        x4 = X[:, TPC * c:TPC * (c + 1), :]
        yield
        stats = layernorm_stats(K, M, x4, TPC, K.x_ready(c))
        yield
        yield
        V.wait(st["hT_free"])
        normed = layernorm_apply(K, M, x4, xn, TPC, stats)
        stats = layernorm_stats(K, M, xn, TPC, normed)
        K.x_written[c] = added = V.did(V.e.tensor_tensor(x4, x4, xn[:], ALU.add))
        yield
        yield
        h_ready = layernorm_apply(K, M, xn, xn, TPC, [stats, added])
        yield
        for k in range(DT):
            f = pick()
            T.wait(h_ready, f.free)
            for i in range(TPC):
                T.did(T.e.transpose(f.ap[:, i * P:(i + 1) * P], xn[:, i, k * P:(k + 1) * P], K.ident[:]))
            made = T.own()
            yield
            S.wait(made, st["hT_free"])
            f.free = hT_ready = S.did(S.e.activation(hT[:, k, :], f.ap[:], ACT.Identity,
                                                     bias=lnv[:, k, 1:2], scale=lnv[:, k, 0:1]))
            yield
        V.wait(st["hist"])
        if c % CPB:
            hist = V.did(V.e.tensor_copy(uraw[:, :, 0:3], uraw[:, :, CH:CH + 3]))
        else:
            hist = V.did(V.e.memset(uraw[:, :, 0:3], 0.0))
        for step in range(2 * ND):
            d, is_z = step // 2, step % 2
            e = d + ND * is_z
            f = pick()
            T.wait(hT_ready, f.free)
            for k in range(DT):
                T.did(T.e.matmul(f.ap[:], w_in[:, k, e * P:(e + 1) * P], hT[:, k, :],
                                 start=k == 0, stop=k == DT - 1))
            made = T.own()
            yield
            S.wait(made, hist, st["chunk_done"][r])
            f.free = S.did(S.e.activation(zs[r][:, d, :] if is_z else uraw[:, d, 3:3 + CH], f.ap[:], ACT.Copy))
            if not is_z:
                S.wait(f.free, st["u_free"])
                tapped = S.did(S.e.activation(cv[:, d, :], uraw[:, d, 0:CH], ACT.Identity,
                                              bias=vec[:, d, 4:5], scale=vec[:, d, 0:1]))
                yield
                continue
            V.wait(tapped)
            for t in range(1, 4):
                V.wait(V.did(V.e.scalar_tensor_tensor(cv[:, d, :], uraw[:, d, t:t + CH], vec[:, d, t:t + 1],
                                                      cv[:, d, :], ALU.mult, ALU.add)))
            yield
        st["hT_free"] = T.own()
        st["hist"] = V.own()
        S.wait(st["hist"], S.own())
        S.did(S.e.activation(u[r][:], cv[:], ACT.Silu))
        S.did(S.e.activation(zs[r][:], zs[r][:], ACT.Silu))
        st["u_free"] = S.own()
        yield
        yield
        f = pick()
        T.wait(st["u_free"], f.free)
        for k in range(ND):
            T.did(T.e.matmul(f.ap[0:96, :], w_bc[:, k, :, :].rearrange("p a b -> p (a b)"), u[r][:, k, :],
                             start=k == 0, stop=k == ND - 1))
        made = T.own()
        yield
        split_done = f.free = split3(K, f.ap, BC3[r], rest, [made, st["chunk_done"][r]])
        yield
        f = pick()
        T.wait(f.free)
        for k in range(ND):
            T.did(T.e.matmul(f.ap[0:R, :], w_dtr[:, k, :], u[r][:, k, :], start=k == 0, stop=k == ND - 1))
        made = T.own()
        yield
        S.wait(made)
        f.free = rank_ready = S.did(S.e.activation(dtr[:], f.ap[0:R, :], ACT.Copy))
        yield
        ab = cv
        for d in range(ND):
            f = pick()
            T.wait(f.free, rank_ready)
            T.did(T.e.matmul(f.ap[:], w_dt[:, d * P:(d + 1) * P], dtr[:], start=True, stop=True))
            made = T.own()
            yield
            S.wait(made, st["u_free"])
            absolute = S.did(S.e.activation(ab[:, d, :], f.ap[:], ACT.Abs, bias=vec[:, d, 5:6]))
            V.wait(absolute)
            relu = V.did(V.e.tensor_scalar(dt[r][:, d, :], f.ap[:], vec[:, d, 5:6], 0.0, ALU.add, ALU.max))
            f.free = [absolute, relu]
            yield
        S.wait(S.own())
        S.wait(S.did(S.e.activation(ab[:], ab[:], ACT.Exp, scale=-1.0)))
        S.did(S.e.activation(ab[:], ab[:], ACT.Ln, bias=1.0))
        yield
        yield
        V.wait(S.own(), V.own())
        made = V.did(V.e.tensor_tensor(dt[r][:], dt[r][:], ab[:], ALU.add))
        st["u_free"] = made
        G.wait(made)
        st["ready"][r] = [G.did(G.e.tensor_tensor(dtu[r][:], dt[r][:], u[r][:], ALU.mult)), made, split_done]
        yield

    def take_y(c):
        r = c % 2
        V.wait(sc.summed[(c + 1) * NS - 1])
        for d in range(ND):
            V.did(V.e.scalar_tensor_tensor(u[r][:, d, :], u[r][:, d, :], vec[:, d, 6:7], sc.y[d][:],
                                           ALU.mult, ALU.add))
        sc.y_free = V.own()

    def back(c):
        r = c % 2
        yield
        V.wait(sc.y_free)
        gated = V.did(V.e.tensor_tensor(u[r][:], u[r][:], zs[r][:], ALU.mult))
        yield
        for i in range(0, TPC, 2):
            f = pick()
            T.wait(f.free, gated)
            for j in range(2):
                for k in range(ND):
                    T.did(T.e.matmul(f.ap[:, j * D:(j + 1) * D], u[r][:, k, (i + j) * P:(i + j + 1) * P],
                                     w_out[:, k, :], start=k == 0, stop=k == ND - 1))
            made = T.own()
            yield
            xt = X[:, TPC * c + i:TPC * c + i + 2, :]
            V.wait(made, K.x_written[c])
            f.free = V.did(V.e.tensor_tensor(xt, xt, f.ap[:].rearrange("p (a b) -> p a b", a=2), ALU.add))
            yield
        st["chunk_done"][r] = [T.own(), V.own()]

    K.x_written = [None] * NC
    run_scan(sc, front, take_y, back, lambda c: (dt[c % 2], dtu[c % 2][:], BC3[c % 2][:], A, sel, st["ready"][c % 2]))
    K.x_is_ready()
    M.free()



SLOT_TILES = 80
SLOTS = SLOT_TILES * P
ZERO_ROW = SLOTS
DROPPED = 1 << 20


def channel_major(K, xn, xT, bank, ready, free):
    S, T = K.S, K.T
    marks = []
    for k in range(DT):
        f = bank()
        T.wait(ready, f.free)
        for i in range(TPC):
            T.did(T.e.transpose(f.ap[:, i * P:(i + 1) * P], xn[:, i, k * P:(k + 1) * P], K.ident[:]))
        S.wait(T.own(), free)
        f.free = S.did(S.e.activation(xT[:, k, :], f.ap[:], ACT.Copy))
        marks.append(f.free)
    return marks


class Routing:

    def __init__(self, K, M, E, capacity=None):
        self.K, self.M, self.E, self.cap = K, M, E, capacity
        self.logits = M.ps("logits", [P, NT, E])
        n = [P, NT, E]
        self.p, self.a, self.b = M.sb("probs", n), M.sb("route_a", n), M.sb("route_b", n)
        self.oh = [M.sb(f"onehot{i}", n) for i in range(2)]
        self.mask = M.sb("mask", n, BF16)
        self.tot = M.sb("totals", [P, E, NT])
        self.cum = M.sb("cumulated", [P, E, NT])
        self.keep = M.sb("keep", [P, E, NT])
        self.w, self.gather_of = K.pick_weight, K.pick_row
        self.red = M.sb("route_red", [P, NT])
        self.fl = M.sb("route_slot", [P, NT])
        self.scatter_to = [M.sb(f"scatter_to{i}", [P, NT], I32) for i in range(2)]
        self.small = M.sb("route_small", [P, E, NT])
        self.nt, self.end = M.sb("n_tiles", [P, E]), M.sb("end_tile", [P, E])
        self.rev = M.sb("reversed_iota", [P, E])
        self.ones = M.sb("route_ones", [P, E])
        if capacity is None:
            self.ej = M.sb("tile_compare", [P, SLOT_TILES, E])
            self.ef = M.sb("tile_expert_f", [P, SLOT_TILES])
            self.tile_expert = M.sb("tile_expert", [P, SLOT_TILES], I32)

    def run(self, made, bias=None, normalise=False):
        K, E = self.K, self.E
        V, S, T = K.V, K.S, K.T
        p, a, b, red, fl = self.p, self.a, self.b, self.red, self.fl
        ranks = ExitStack()
        self.within = ranks.enter_context(K.nc.psum_tensor(self.M.tag + "rank_within_tile", [P, NT, E], F32))
        self.totals = ranks.enter_context(K.nc.psum_tensor(self.M.tag + "tile_totals", [P, NT, E], F32))

        def v(inst):
            V.wait(V.did(inst))

        V.wait(made)
        if bias is not None:
            v(V.e.tensor_tensor(p[:], self.logits[:], mid(bias, NT), ALU.add))
        else:
            v(V.e.tensor_copy(p[:], self.logits[:]))
        v(V.e.tensor_reduce(red[:], p[:], AX.X, ALU.max))
        v(V.e.tensor_tensor(p[:], p[:], last(red[:], E), ALU.subtract))
        S.wait(V.own())
        V.wait(S.did(S.e.activation(p[:], p[:], ACT.Exp)))
        v(V.e.tensor_reduce(red[:], p[:], AX.X, ALU.add))
        v(V.e.reciprocal(red[:], red[:]))
        v(V.e.tensor_tensor(p[:], p[:], last(red[:], E), ALU.mult))
        v(V.e.tensor_scalar(self.rev[:], K.iota[:, 0:E], -1.0, float(E), ALU.mult, ALU.add))
        v(V.e.tensor_copy(a[:], p[:]))
        for i in range(2):
            v(V.e.tensor_reduce(self.w[i][:], a[:], AX.X, ALU.max))
            v(V.e.tensor_tensor(b[:], a[:], last(self.w[i][:], E), ALU.is_equal))
            v(V.e.tensor_tensor(b[:], b[:], mid(self.rev[:], NT), ALU.mult))
            v(V.e.tensor_reduce(red[:], b[:], AX.X, ALU.max))
            v(V.e.tensor_tensor(self.oh[i][:], b[:], last(red[:], E), ALU.is_equal))
            if i == 0:
                v(V.e.scalar_tensor_tensor(a[:], self.oh[0][:], -2.0, a[:], ALU.mult, ALU.add))
        v(V.e.tensor_tensor(b[:], self.oh[0][:], self.oh[1][:], ALU.add))
        if self.cap is not None:
            v(V.e.tensor_scalar(a[:], p[:], 0.0, None, ALU.is_gt))
            v(V.e.tensor_tensor(b[:], b[:], a[:], ALU.mult))
        v(V.e.tensor_copy(self.mask[:], b[:]))
        T.wait(V.own())
        T.did(T.e.matmul(self.within[:].rearrange("p t e -> p (t e)"), K.before[:],
                         self.mask[:].rearrange("p t e -> p (t e)"), start=True, stop=True))
        T.did(T.e.matmul(self.totals[:].rearrange("p t e -> p (t e)"), K.ones_bf[:],
                         self.mask[:].rearrange("p t e -> p (t e)"), start=True, stop=True))
        V.wait(T.own())
        v(V.e.tensor_copy(self.tot[:], self.totals[:].rearrange("p t e -> p e t")))
        v(V.e.memset(self.keep[:], 1.0))
        v(V.e.memset(self.keep[:, :, 0], 0.0))
        flat = lambda t: t[:].rearrange("p e t -> p (e t)")
        v(V.e.tensor_tensor_scan(flat(self.cum), flat(self.keep), flat(self.tot), 0.0, ALU.mult, ALU.add))
        count = self.small
        if self.cap is None:
            v(V.e.tensor_scalar(self.keep[:], mid(K.iota[:, 0:NT], E), float(P), None, ALU.mult))
            v(V.e.tensor_tensor(count[:], last(self.cum[:, :, NT - 1], NT), self.keep[:], ALU.is_gt))
            v(V.e.tensor_reduce(self.nt[:], count[:], AX.X, ALU.add))
            v(V.e.memset(self.ones[:], 1.0))
            v(V.e.tensor_tensor_scan(self.end[:], self.ones[:], self.nt[:], 0.0, ALU.mult, ALU.add))
            v(V.e.tensor_tensor(self.ej[:], last(K.iota[:, 0:SLOT_TILES], E), mid(self.end[:], SLOT_TILES), ALU.is_ge))
            v(V.e.tensor_reduce(self.ef[:], self.ej[:], AX.X, ALU.add))
            v(V.e.tensor_scalar(self.ef[:], self.ef[:], float(E - 1), None, ALU.min))
            v(V.e.tensor_copy(self.tile_expert[:], self.ef[:]))
            v(V.e.tensor_tensor(self.nt[:], self.end[:], self.nt[:], ALU.subtract))
            v(V.e.tensor_scalar(self.nt[:], self.nt[:], float(P), None, ALU.mult))
        else:
            v(V.e.tensor_scalar(self.nt[:], K.iota[:, 0:E], float(self.cap), None, ALU.mult))
        v(V.e.tensor_tensor(self.cum[:], self.cum[:], self.tot[:], ALU.subtract))
        v(V.e.tensor_tensor(a[:], self.within[:], self.cum[:].rearrange("p e t -> p t e"), ALU.add))
        for i in range(2):
            if self.cap is not None:
                v(V.e.tensor_tensor(b[:], self.oh[i][:], a[:], ALU.mult))
                v(V.e.tensor_reduce(red[:], b[:], AX.X, ALU.add))
                v(V.e.tensor_scalar(red[:], red[:], float(self.cap), None, ALU.is_lt))
                v(V.e.tensor_scalar(fl[:], self.w[i][:], 0.0, None, ALU.is_gt))
                v(V.e.tensor_tensor(red[:], red[:], fl[:], ALU.mult))
            v(V.e.tensor_tensor(b[:], a[:], mid(self.nt[:], NT), ALU.add))
            v(V.e.tensor_tensor(b[:], b[:], self.oh[i][:], ALU.mult))
            v(V.e.tensor_reduce(fl[:], b[:], AX.X, ALU.add))
            if self.cap is not None:
                v(V.e.tensor_tensor(fl[:], fl[:], red[:], ALU.mult))
                v(V.e.tensor_scalar(red[:], red[:], -1.0, 1.0, ALU.mult, ALU.add))
                v(V.e.scalar_tensor_tensor(self.small[:, 0, :], red[:], float(DROPPED), fl[:], ALU.mult, ALU.add))
                v(V.e.tensor_copy(self.scatter_to[i][:], self.small[:, 0, :]))
                v(V.e.scalar_tensor_tensor(fl[:], red[:], float(ZERO_ROW), fl[:], ALU.mult, ALU.add))
                v(V.e.tensor_copy(self.gather_of[i][:], fl[:]))
            else:
                v(V.e.tensor_copy(self.scatter_to[i][:], fl[:]))
                v(V.e.tensor_copy(self.gather_of[i][:], fl[:]))
        if normalise:
            v(V.e.tensor_tensor(red[:], self.w[0][:], self.w[1][:], ALU.add))
            v(V.e.tensor_scalar(red[:], red[:], 1e-9, None, ALU.add))
            v(V.e.reciprocal(red[:], red[:]))
            for i in range(2):
                v(V.e.tensor_tensor(self.w[i][:], self.w[i][:], red[:], ALU.mult))
        T.wait(V.own())
        ranks.close()
        return V.own()

    def scatter(self, rows, routed):
        K, G = self.K, self.K.G
        G.wait(routed, K.sorted_read)
        for t in range(NT):
            for i in range(2):
                done = K.count(G.e.indirect_dma_start(
                    K.sorted_in, bass.IndirectOffsetOnAxis(ap=self.scatter_to[i][:, t:t + 1], axis=0),
                    rows[:, t, :], None, bounds_check=SLOTS - 1, oob_is_err=False), "scatter")
        return done


class Combine:

    def __init__(self, K, M, into, ring=4):
        self.K, self.into, self.ring, self.at = K, into, ring, 0
        self.got = [[M.sb(f"gathered{i}_{j}", [P, D]) for j in range(2)] for i in range(ring)]
        self.used, self.arrived, self.gathered = [None] * ring, {}, 0
        self.prefetch(ring)

    def prefetch(self, n):
        for t in range(self.gathered, min(self.gathered + n, self.at + self.ring, NT)):
            self.gather(t)

    def gather(self, t):
        G, s = self.K.G, t % self.ring
        self.gathered = t + 1
        G.wait(self.used[s])
        for i in range(2):
            self.arrived[t] = self.K.count(G.e.indirect_dma_start(
                self.got[s][i][:], None, self.K.sorted_out,
                bass.IndirectOffsetOnAxis(ap=self.K.pick_row[i][:, t:t + 1], axis=0),
                bounds_check=SLOTS, oob_is_err=False), f"gather{s}")

    def through(self, end, ready=None):
        V, step = self.K.V, min(self.ring, TPC)
        V.wait(ready)
        while self.at < end:
            tiles = range(self.at, self.at + step)
            self.prefetch(max(0, tiles.stop - self.gathered))
            for i in range(2):
                for t in tiles:
                    V.wait(self.arrived[t])
                    V.did(V.e.scalar_tensor_tensor(
                        self.into[:, t, :], self.got[t % self.ring][i][:], self.K.pick_weight[i][:, t:t + 1],
                        self.into[:, t, :], ALU.mult, ALU.add))
                V.wait(V.own())
            for t in tiles:
                self.used[t % self.ring] = V.own()
            self.at += step
        return V.own()


def moe0_stage(K, W):
    V, S, G, T, Q = K.V, K.S, K.G, K.T, K.Q
    E, I = 8, 1024
    CAP = -(-T_ALL * 5 // (4 * E))
    CT = CAP // P
    KI = I // P
    M = Memory(K)
    lns = [Statistics(M, i) for i in range(2)]
    R = Routing(K, M, E, CAP)
    wr = M.sb("w_router", [P, DT, E])
    rb = M.sb("b_router", [P, E])
    xn = M.sb("xn", [P, NT, D])
    xT = [M.sb(f"xT{i}", [P, DT, CH]) for i in range(2)]
    tbank = [Bank(M.ps(f"transposed{i}", [P, CH])) for i in range(2)]
    w_in = [M.sb(f"w_inter{i}", [P, DT, I]) for i in range(2)]
    w_out = [M.sb(f"w_exp_out{i}", [P, KI, D]) for i in range(2)]
    rows = [M.sb(f"rows{i}", [P, CT, D]) for i in range(2)]
    K.dma(Q, wr[:], W["L0_router_T"].rearrange("(k p) e -> p k e", p=P), "weights")
    loaded = K.dma(Q, rb[:], W["L0_router_bias"], "weights")
    freed = [None, None]

    def load_expert(e):
        r = e % 2
        Q.wait(freed[r])
        K.dma(Q, w_in[r][:], W["L0_ffn_experts_inter"][e].rearrange("(k p) i -> p k i", p=P), f"expert{r}")
        return K.dma(Q, w_out[r][:], W["L0_ffn_experts_out"][e].rearrange("(k p) i -> p k i", p=P), f"expert{r}")

    expert_here = [load_expert(0), load_expert(1)]
    T.wait(loaded)
    V.wait(loaded)
    used, turn = [None, None], rotation(tbank)
    stats = layernorm_stats(K, lns[0], K.X[:, 0:TPC, :], TPC, K.x_ready(0))
    for c in range(NC):
        r = c % 2
        tiles = slice(TPC * c, TPC * (c + 1))
        if c + 1 < NC:
            ahead = layernorm_stats(K, lns[1 - r], K.X[:, TPC * (c + 1):TPC * (c + 2), :], TPC, K.x_ready(c + 1))
        normed = layernorm_apply(K, lns[r], K.X[:, tiles, :], xn[:, tiles, :], TPC, stats)
        stats = ahead
        T.wait(channel_major(K, xn[:, tiles, :], xT[r], turn, normed, used[r]))
        for i in range(TPC):
            for k in range(DT):
                T.did(T.e.matmul(R.logits[:, TPC * c + i, :], xT[r][:, k, i * P:(i + 1) * P], wr[:, k, :],
                                 start=k == 0, stop=k == DT - 1))
        used[r] = T.own()
    routed = R.run(T.own(), bias=rb[:])
    scattered = R.scatter(xn, routed)

    xsT = [M.sb(f"rowsT{i}", [P, DT, CAP]) for i in range(2)]
    hT = M.sb("hidden", [P, KI, CAP])
    out = [M.sb(f"result{i}", [P, D]) for i in range(4)]
    hb = [Bank(M.ps(f"hidden_sum{i}", [P, 512])) for i in range(2)]
    ob = Bank(M.ps("result_sum", [P, 2, D]))
    HALF = CAP // 2
    rows_here, rows_free, xsT_free, xsT_ready = [None, None], [None, None], [None, None], [None, None]
    out_stored = [None] * 4
    Q.wait(scattered)

    def load_rows(e):
        r = e % 2
        Q.wait(rows_free[r])
        rows_here[r] = K.dma(Q, rows[r][:], K.sorted_in[e * CAP:(e + 1) * CAP, :].rearrange("(t p) c -> p t c", p=P), f"rows{r}")

    def transpose_rows(e):
        r = e % 2
        T.wait(rows_here[r])
        for t in range(CT):
            b = tbank[t % 2]
            T.wait(b.free)
            for k in range(DT):
                T.did(T.e.transpose(b.ap[:, k * P:(k + 1) * P], rows[r][:, t, k * P:(k + 1) * P], K.ident[:]))
            S.wait(T.own(), xsT_free[r])
            b.free = S.did(S.e.activation(xsT[r][:, :, t * P:(t + 1) * P],
                                          b.ap[:, 0:DT * P].rearrange("p (k q) -> p k q", k=DT), ACT.Copy))
        rows_free[r] = T.own()
        xsT_ready[r] = S.own()

    load_rows(0)
    load_rows(1)
    transpose_rows(0)
    h_free, n_out, stored = None, 0, None
    for e in range(E):
        r = e % 2
        T.wait(xsT_ready[r], expert_here[r])
        for i in range(KI):
            for half in range(2):
                b = hb[half]
                T.wait(b.free)
                for k in range(DT):
                    T.did(T.e.matmul(b.ap[:, 0:HALF], w_in[r][:, k, i * P:(i + 1) * P],
                                     xsT[r][:, k, half * HALF:(half + 1) * HALF], start=k == 0, stop=k == DT - 1))
                to = hT[:, i, half * HALF:(half + 1) * HALF]
                if half:
                    S.wait(T.own(), h_free)
                    b.free = S.did(S.e.activation(to, b.ap[:, 0:HALF], ACT.Relu))
                else:
                    V.wait(T.own(), h_free)
                    b.free = V.did(V.e.tensor_scalar(to, b.ap[:, 0:HALF], 0.0, None, ALU.max))
        xsT_free[r] = T.own()
        h_ready = [S.own(), V.own()]
        if e + 1 < E:
            transpose_rows(e + 1)
            if e + 2 < E:
                load_rows(e + 2)
        T.wait(h_ready)
        for t in range(CT):
            half = n_out % 2
            T.wait(ob.free if half == 0 else None)
            for i in range(KI):
                T.did(T.e.matmul(ob.ap[:, half, :], hT[:, i, t * P:(t + 1) * P], w_out[r][:, i, :],
                                 start=i == 0, stop=i == KI - 1))
            T_mark = T.own()
            V.wait(T_mark, out_stored[n_out % 4])
            ob.free = V.did(V.e.tensor_copy(out[n_out % 4][:], ob.ap[:, half, :]))
            S.wait(ob.free)
            row = (e * CT + t) * P
            out_stored[n_out % 4] = stored = K.dma(S, K.sorted_out[row:row + P, :], out[n_out % 4][:], f"store{n_out % 4}")
            T.wait(ob.free)
            n_out += 1
        h_free = T.own()
        freed[r] = T.own()
        if e + 2 < E:
            expert_here[r] = load_expert(e + 2)
    K.sorted_read = [rows_here[0], rows_here[1]]
    K.owed = True
    M.free()


def do(E, issue, *marks):
    E.wait(*marks)
    return E.did(issue())


def run_lanes(chunk, n, skew, lanes=2):
    active, started, since = [], 0, skew
    while active or started < n:
        if started < n and len(active) < lanes and since >= skew:
            active.append(chunk(started))
            started += 1
            since = 0
        since += 1
        for g in list(active):
            if next(g, "end") == "end":
                active.remove(g)


class Lane:

    def __init__(self, ln, xn, hh, xa, mx, pp, aa, m0, k, v, sr, kw, ea, eb, rr, d1, scr):
        self.ln, self.done = ln, None
        self.xn, self.hh, self.xa, self.mx, self.pp, self.aa, self.m0 = xn, hh, xa, mx, pp, aa, m0
        self.k, self.v, self.sr, self.kw, self.ea, self.eb, self.rr = k, v, sr, kw, ea, eb, rr
        self.d1, self.scr = d1, scr


def rwkv_stage(K, W):
    V, S, G, T, Q = K.V, K.S, K.G, K.T, K.Q
    X = K.X
    HID = 4 * D
    KH = HID // P
    NEG = -1e38
    M = Memory(K)
    w = {n: M.sb("w_" + n, [P, DT, D]) for n in ("k", "v", "r", "cr")}
    for n in w:
        K.dma(Q, w[n][:], W[f"rwkv_W{n}_T"].rearrange("(k p) d -> p k d", p=P), "weights")
    w_ck = M.sb("w_ck", [P, DT, HID])
    w_cv = M.sb("w_cv", [P, KH, D])
    vec = M.sb("rwkv_vectors", [P, DT, 12])
    K.dma(Q, w_ck[:], W["rwkv_Wck_T"].rearrange("(k p) d -> p k d", p=P), "weights")
    K.dma(Q, w_cv[:], W["rwkv_Wcv_T"].rearrange("(k p) d -> p k d", p=P), "weights")
    loaded = K.dma(Q, vec[:], W["rwkv_vectors"], "weights")
    for e in (V, S, G, T):
        e.wait(loaded)
    WD, U, G1, B1, G2, B2 = 0, 1, 7, 8, 9, 10
    MIX = {"k": 2, "v": 3, "r": 4, "ck": 5, "cr": 6}
    omr = M.sb("one_minus_mix", [P, DT, 12])
    nu = M.sb("minus_u", [P, DT])
    V.did(V.e.tensor_scalar(omr[:], vec[:], -1.0, 1.0, ALU.mult, ALU.add))
    prep = V.did(V.e.tensor_scalar(nu[:], vec[:, :, U], -1.0, None, ALU.mult))
    for e in (V, S, G):
        e.wait(prep)

    def lane(i):
        shapes = {n: [P, TPC, D] for n in ("xn", "hh")}
        shapes.update({n: [P, DT, 1 + CH] for n in ("xa", "mx", "pp", "aa")})
        shapes.update({n: [P, DT, CH] for n in ("m0", "k", "v", "sr", "kw", "ea", "eb", "rr", "d1")})
        shapes["scr"] = [P, D]
        ln = tuple(M.sb(f"l{i}_{n}", sh) for n, sh in (("st", [P, TPC, 6]), ("mv", [P, TPC, 2]),
                                                       ("ve", [P, TPC]), ("rs", [P, TPC])))
        return Lane(ln, **{n: M.sb(f"l{i}_{n}", sh) for n, sh in shapes.items()})

    lanes = [lane(i) for i in range(2)]
    K.start_combine(M)
    kc, kc_free = M.sb("kc", [P, KH, CH]), [None]
    banks = [Bank(M.ps(f"bank{i}", [P, CH])) for i in range(8)]
    tb, pb, kb, ob = banks[0:2], banks[2:4], banks[4:6], banks[6:8]
    turn = {"t": 0, "p": 0, "k": 0, "o": 0}

    def bank(kind):
        turn[kind] += 1
        return {"t": tb, "p": pb, "k": kb, "o": ob}[kind][turn[kind] % 2]

    def to_channels(src, dst, gain, bias, ready, free):
        marks = []
        for k in range(DT):
            f = bank("t")
            T.wait(ready, f.free)
            for i in range(TPC):
                T.did(T.e.transpose(f.ap[:, i * P:(i + 1) * P], src[:, i, k * P:(k + 1) * P], K.ident[:]))
            f.free = do(S, lambda: S.e.activation(dst[:, k, 1:], f.ap[:], ACT.Identity,
                                                  bias=vec[:, k, bias:bias + 1], scale=vec[:, k, gain:gain + 1]),
                        T.own(), free)
            marks.append(f.free)
        return marks

    def mixed(xa, dst, kind, ready, free):
        m, marks = MIX[kind], []
        for k in range(DT):
            s1 = do(S, lambda: S.e.activation(dst[:, k, :], xa[:, k, 0:CH], ACT.Copy, scale=omr[:, k, m:m + 1]),
                    ready, free)
            marks.append(do(V, lambda: V.e.scalar_tensor_tensor(
                dst[:, k, :], xa[:, k, 1:], vec[:, k, m:m + 1], dst[:, k, :], ALU.mult, ALU.add), s1, ready))
        return marks

    prev = {}
    carry = {n: [M.sb(f"carry_{n}{i}", [P, DT, 1]) for i in range(2)] for n in ("xa", "mx", "rr", "pp", "aa", "xb")}

    def start_column(name, buf, c, value, free=None):
        if c % CPB == 0:
            return do(V, lambda: V.e.memset(buf[:, :, 0:1], value), free)
        return do(V, lambda: V.e.tensor_copy(buf[:, :, 0:1], carry[name][(c - 1) % 2][:]), prev[name], free)

    def save_column(name, ap, c, ready):
        prev[name] = do(V, lambda: V.e.tensor_copy(carry[name][c % 2][:], ap), ready)

    def chunk(c):
        b = lanes[c % 2]
        x4 = X[:, TPC * c:TPC * (c + 1), :]
        first = c % CPB == 0
        for e in (V, S, G, T):
            e.wait(b.done)
        xn_ready = layernorm_tiles(K, b, x4, b.xn, TPC, K.x_ready(c))
        yield
        h_ready = layernorm_tiles(K, b, b.xn, b.hh, TPC, xn_ready)
        yield
        col = start_column("xa", b.xa, c, 0.0)
        xa_ready = to_channels(b.hh, b.xa, G1, B1, h_ready, None)
        save_column("xa", b.xa[:, :, CH:], c, list(xa_ready))
        xa_ready.append(col)
        yield
        proj, read = {}, None
        for kind, dst in (("k", b.k), ("v", b.v), ("r", b.sr)):
            m_ready = mixed(b.xa, b.m0, kind, xa_ready, read)
            yield
            marks = []
            for d in range(DT):
                f = bank("p")
                T.wait(m_ready, f.free)
                for k in range(DT):
                    T.did(T.e.matmul(f.ap[:], w[kind][:, k, d * P:(d + 1) * P], b.m0[:, k, :],
                                     start=k == 0, stop=k == DT - 1))
                f.free = do(S, lambda: S.e.activation(dst[:, d, :], f.ap[:], ACT.Copy), T.own())
                marks.append(f.free)
            read = T.own()
            proj[kind] = marks
            K.prefetch()
            yield
        kw_ready = [do(V, lambda: V.e.tensor_scalar(b.kw[:, d, :], b.k[:, d, :], vec[:, d, WD:WD + 1], None, ALU.add),
                       proj["k"]) for d in range(DT)]
        col = start_column("mx", b.mx, c, NEG)
        for d in range(DT):
            mx = do(V, lambda: V.e.tensor_tensor_scan(
                b.mx[:, d, 1:], vec[:, d, WD:WD + 1].to_broadcast([P, CH]), b.kw[:, d, :],
                b.mx[:, d, 0:1], ALU.add, ALU.max), col, kw_ready)
        save_column("mx", b.mx[:, :, CH:], c, mx)
        K.prefetch()
        yield
        d_a = do(V, lambda: V.e.tensor_tensor(b.ea[:], b.mx[:, :, 0:CH], b.mx[:, :, 1:], ALU.subtract), mx)
        d_b = do(V, lambda: V.e.tensor_tensor(b.eb[:], b.kw[:], b.mx[:, :, 1:], ALU.subtract), mx)
        for d in range(DT):
            e_a = do(S, lambda: S.e.activation(b.ea[:, d, :], b.ea[:, d, :], ACT.Exp, bias=vec[:, d, WD:WD + 1]), d_a)
        e_b = do(S, lambda: S.e.activation(b.eb[:], b.eb[:], ACT.Exp), d_b)
        yield
        for d in range(DT):
            r_ready = do(V, lambda: V.e.tensor_tensor_scan(
                b.rr[:, d, :], b.ea[:, d, :], b.eb[:, d, :],
                0.0 if first else carry["rr"][(c - 1) % 2][:, d, :], ALU.mult, ALU.add),
                e_a, e_b, prev.get("rr"))
        save_column("rr", b.rr[:, :, CH - 1:CH], c, r_ready)
        ln_r = do(S, lambda: S.e.activation(b.eb[:], b.rr[:], ACT.Ln), r_ready)
        yield
        col = start_column("pp", b.pp, c, NEG)
        pp = do(V, lambda: V.e.tensor_tensor(b.pp[:, :, 1:], b.eb[:], b.mx[:, :, 1:], ALU.add), ln_r, col)
        save_column("pp", b.pp[:, :, CH:], c, pp)
        d1 = do(V, lambda: V.e.tensor_tensor(b.d1[:], b.pp[:, :, 0:CH], b.k[:], ALU.subtract), pp)
        neg = do(V, lambda: V.e.tensor_scalar(b.ea[:], b.d1[:], 0.0, None, ALU.min), d1)
        pos = do(V, lambda: V.e.tensor_scalar(b.kw[:], b.d1[:], 0.0, None, ALU.max), d1)
        e1u = do(S, lambda: S.e.activation(b.ea[:], b.ea[:], ACT.Exp), neg)
        e2u = do(S, lambda: S.e.activation(b.kw[:], b.kw[:], ACT.Exp, scale=-1.0), pos)
        yield
        bv = do(G, lambda: G.e.tensor_tensor(b.kw[:], b.kw[:], b.v[:], ALU.mult), e2u, proj["v"])
        col = start_column("aa", b.aa, c, 0.0)
        for d in range(DT):
            aa = do(V, lambda: V.e.tensor_tensor_scan(
                b.aa[:, d, 1:], b.ea[:, d, :], b.kw[:, d, :], b.aa[:, d, 0:1], ALU.mult, ALU.add), e1u, bv, col)
        save_column("aa", b.aa[:, :, CH:], c, aa)
        yield
        for d in range(DT):
            S.wait(ln_r, d1)
            g1 = S.did(S.e.activation(b.eb[:, d, :], b.d1[:, d, :], ACT.Sigmoid, bias=nu[:, d:d + 1]))
            g2 = do(S, lambda: S.e.activation(b.rr[:, d, :], b.d1[:, d, :], ACT.Sigmoid,
                                              bias=vec[:, d, U:U + 1], scale=-1.0), prev["rr"])
        sr = do(S, lambda: S.e.activation(b.sr[:], b.sr[:], ACT.Sigmoid), proj["r"])
        ya = do(G, lambda: G.e.tensor_tensor(b.eb[:], b.eb[:], b.aa[:, :, 0:CH], ALU.mult), g1, aa)
        yb = do(V, lambda: V.e.tensor_tensor(b.rr[:], b.rr[:], b.v[:], ALU.mult), g2)
        y = do(V, lambda: V.e.tensor_tensor(b.rr[:], b.rr[:], b.eb[:], ALU.add), ya, yb)
        gated = do(V, lambda: V.e.tensor_tensor(b.rr[:], b.rr[:], b.sr[:], ALU.mult), y, sr)
        yield
        for i in range(0, TPC, 2):
            f = bank("t")
            T.wait(gated, f.free)
            for j in range(2):
                for k in range(DT):
                    T.did(T.e.transpose(f.ap[:, j * D + k * P:j * D + (k + 1) * P],
                                        b.rr[:, k, (i + j) * P:(i + j + 1) * P], K.ident[:]))
            x1 = f.free = do(V, lambda: V.e.tensor_tensor(
                b.xn[:, i:i + 2, :], b.xn[:, i:i + 2, :], f.ap[:].rearrange("p (a c) -> p a c", a=2), ALU.add), T.own())
        yield
        grown = do(V, lambda: V.e.tensor_tensor(x4, x4, b.xn[:], ALU.add), x1)
        h_ready = layernorm_tiles(K, b, b.xn, b.hh, TPC, x1)
        yield
        col = start_column("xb", b.mx, c, 0.0, [pp, d_a, d_b, prev["mx"]])
        xb_ready = to_channels(b.hh, b.mx, G2, B2, h_ready, [pp, d_a, d_b, prev["mx"]])
        save_column("xb", b.mx[:, :, CH:], c, list(xb_ready))
        xb_ready.append(col)
        mk = mixed(b.mx, b.m0, "ck", xb_ready, read)
        mr = mixed(b.mx, b.k, "cr", xb_ready, d1)
        yield
        for h in range(KH):
            f = bank("k")
            T.wait(mk, f.free)
            for k in range(DT):
                T.did(T.e.matmul(f.ap[:], w_ck[:, k, h * P:(h + 1) * P], b.m0[:, k, :],
                                 start=k == 0, stop=k == DT - 1))
            relu = f.free = do(S, lambda: S.e.activation(kc[:, h, :], f.ap[:], ACT.Relu), T.own(), kc_free[0])
            sq = do(V, lambda: V.e.tensor_tensor(kc[:, h, :], kc[:, h, :], kc[:, h, :], ALU.mult), relu)
            yield
        for i in range(TPC):
            f = bank("o")
            T.wait(mr, sq, f.free)
            for k in range(DT):
                T.did(T.e.matmul(f.ap[:, 0:D], b.k[:, k, i * P:(i + 1) * P], w["cr"][:, k, :],
                                 start=k == 0, stop=k == DT - 1))
            c_made = T.own()
            for h in range(KH):
                T.did(T.e.matmul(f.ap[:, D:2 * D], kc[:, h, i * P:(i + 1) * P], w_cv[:, h, :],
                                 start=h == 0, stop=h == KH - 1))
            scr = do(S, lambda: S.e.activation(b.scr[:], f.ap[:, 0:D], ACT.Sigmoid), T.own(), V.own())
            prod = f.free = do(V, lambda: V.e.tensor_tensor(b.scr[:], b.scr[:], f.ap[:, D:2 * D], ALU.mult), scr)
            do(V, lambda: V.e.tensor_tensor(x4[:, i, :], x4[:, i, :], b.scr[:], ALU.add), prod, grown)
            yield
        kc_free[0] = T.own()
        b.done = [V.own(), S.own(), G.own(), T.own()]

    run_lanes(chunk, NC, 11)
    K.x_is_ready()
    M.free()


def expert_tiles(K, M, R, E, F, w_gu, w_d, routed, scattered, rms=False):
    V, S, G, T, Q = K.V, K.S, K.G, K.T, K.Q
    FK = F // P
    n_tiles = 2 * NT + E
    wide = 2 * F > CH
    RING = 4
    rows = [M.sb(f"rows{i}", [P, D]) for i in range(RING)]
    xT = [M.sb(f"rowsT{i}", [P, DT, P]) for i in range(2)]
    act = [M.sb(f"act{i}", [P, F]) for i in range(2)]
    mid_ = [M.sb(f"mid{i}", [P, F]) for i in range(2)]
    midT = [M.sb(f"midT{i}", [P, FK, P]) for i in range(2)]
    out = [M.sb(f"result{i}", [P, D]) for i in range(RING)]
    sq = M.sb("squares", [P, F])
    ss = [M.sb(f"sum_squares{i}", [P, 1]) for i in range(4)]
    rs = [M.sb(f"inverse_rms{i}", [P, 1]) for i in range(4)]
    if wide:
        tb = [Bank(M.ps("transposed", [P, CH]))]
        gb = [Bank(M.ps(f"gate_up{i}", [P, 2 * CH])) for i in range(2)]
        hb = [Bank(M.ps("mid_transposed", [P, CH]))]
        ob = [Bank(M.ps("result_sum", [P, CH]))]
    else:
        tb, gb, hb, ob = ([Bank(M.ps(f"{n}{i}", [P, CH])) for i in range(n_b)]
                          for n, n_b in (("transposed", 1), ("gate_up", 2), ("mid_transposed", 1), ("result_sum", 1)))
    gu_flat = w_gu[:].rearrange("p e k f -> p (e k f)")
    d_flat = w_d[:].rearrange("p e k c -> p (e k c)")
    rows_here, rows_free = {}, [None] * RING
    xT_ready, xT_free, mid_ready, mid_free, midT_ready, midT_free = {}, [None] * 2, {}, [None] * 2, {}, [None] * 2
    rs_ready, stored, expert = {}, [None] * RING, {}
    Q.wait(scattered)
    T.wait(routed)

    def load(j):
        Q.wait(rows_free[j % RING])
        rows_here[j] = K.dma(Q, rows[j % RING][:], K.sorted_in[j * P:(j + 1) * P, :], f"rows{j % RING}")

    def transpose(j):
        b = tb[j % len(tb)]
        T.wait(rows_here[j], b.free)
        for k in range(DT):
            T.did(T.e.transpose(b.ap[:, k * P:(k + 1) * P], rows[j % RING][:, k * P:(k + 1) * P], K.ident[:]))
        rows_free[j % RING] = T.own()
        b.free = xT_ready[j] = do(S, lambda: S.e.activation(
            xT[j % 2][:], b.ap[:, 0:DT * P].rearrange("p (k q) -> p k q", k=DT), ACT.Copy), T.own(), xT_free[j % 2])

    def up(j):
        b = gb[j % len(gb)]
        expert[j] = T.e.value_load(R.tile_expert[0:1, j:j + 1], min_val=0, max_val=E - 1)
        T.wait(xT_ready[j], b.free)
        for at in range(0, 2 * F, CH):
            n = min(CH, 2 * F)
            for k in range(DT):
                T.did(T.e.matmul(b.ap[:, at:at + n], xT[j % 2][:, k, :],
                                 gu_flat[:, bass.ds(expert[j] * (DT * 2 * F) + (k * 2 * F + at), n)],
                                 start=k == 0, stop=k == DT - 1))
        xT_free[j % 2] = T.own()
        gate = do(S, lambda: S.e.activation(act[j % 2][:], b.ap[:, 0:F], ACT.Silu), T.own(), mid_ready.get(j - 2))
        b.free = mid_ready[j] = do(V, lambda: V.e.tensor_tensor(
            mid_[j % 2][:], act[j % 2][:], b.ap[:, F:2 * F], ALU.mult), gate, mid_free[j % 2], rs_ready.get(j - 2))
        if rms:
            s4 = ss[j % 4]
            sqd = do(S, lambda: S.e.activation(sq[:], mid_[j % 2][:], ACT.Square, accum_out=s4[:]),
                     mid_ready[j], rs_ready.get(j - 4), S.own())
            ve = do(V, lambda: V.e.tensor_scalar(s4[:], s4[:], 1.0 / F, 1e-6, ALU.mult, ALU.add), sqd)
            rs_ready[j] = do(G, lambda: G.e.tensor_tensor(rs[j % 4][:], s4[:], K.neghalf[:, 0:1], ALU.pow),
                             ve, stored_mark.get(j - 4))

    stored_mark = {}

    def turn(j):
        b = hb[j % len(hb)]
        T.wait(mid_ready[j], b.free)
        for k in range(FK):
            T.did(T.e.transpose(b.ap[:, k * P:(k + 1) * P], mid_[j % 2][:, k * P:(k + 1) * P], K.ident[:]))
        mid_free[j % 2] = T.own()
        b.free = midT_ready[j] = do(V, lambda: V.e.tensor_copy(
            midT[j % 2][:], b.ap[:, 0:F].rearrange("p (k q) -> p k q", k=FK)), T.own(), midT_free[j % 2])

    def down(j):
        b = ob[j % len(ob)]
        T.wait(midT_ready[j], b.free)
        for k in range(FK):
            T.did(T.e.matmul(b.ap[:, 0:D], midT[j % 2][:, k, :],
                             d_flat[:, bass.ds(expert[j] * (FK * D) + k * D, D)], start=k == 0, stop=k == FK - 1))
        midT_free[j % 2] = T.own()
        o = out[j % RING]
        if rms:
            b.free = do(S, lambda: S.e.activation(o[:], b.ap[:, 0:D], ACT.Copy, scale=rs[j % 4][:]),
                        T.own(), stored[j % RING], rs_ready[j])
        else:
            b.free = do(S, lambda: S.e.activation(o[:], b.ap[:, 0:D], ACT.Copy), T.own(), stored[j % RING])
        stored_mark[j] = b.free
        Q.wait(b.free)
        stored[j % RING] = K.dma(Q, K.sorted_out[j * P:(j + 1) * P, :], o[:], f"store{j % RING}")

    for j in range(RING - 1):
        load(j)
    for i in range(n_tiles + 3):
        if i < n_tiles:
            transpose(i)
        if 0 <= i - 1 < n_tiles:
            up(i - 1)
        if 0 <= i - 2 < n_tiles:
            turn(i - 2)
        if 0 <= i - 3 < n_tiles:
            down(i - 3)
        if i + RING - 1 < n_tiles:
            load(i + RING - 1)
    K.sorted_read = [rows_here[j] for j in range(n_tiles - RING, n_tiles)]
    return stored


def ssm1_stage(K, W):
    V, S, G, T, Q = K.V, K.S, K.G, K.T, K.Q
    X, E, F, NS = K.X, 4, 512, 16
    M = Memory(K)
    R = Routing(K, M, E)
    y_rows = M.sb("y_rows", [P, NT, D])
    norm_w = M.sb("norm_w", [P, D])
    M0, M = M, Memory(K)
    ln_buffers(M, TPC)
    w_delta = M.sb("w_delta", [P, DT, D])
    w_bc = M.sb("w_bc", [P, DT, 3, 2 * NS])
    w_router = M.sb("w_router", [P, DT, E])
    vec = M.sb("ssm_vectors", [P, DT, 2])
    A = M.sb("A", [P, DT, NS])
    sel = M.sb("selectors", [96, 32, P], BF16)
    K.dma(Q, w_delta[:], W["L1_attn_a_W_delta"].rearrange("(k p) e -> p k e", p=P), "weights")
    K.dma(Q, w_router[:], W["L1_attn_a_W_router"].rearrange("(k p) e -> p k e", p=P), "weights")
    for j in range(3):
        K.dma(Q, w_bc[:, :, j, 0:NS], W["L1_attn_a_W_B"].rearrange("(k p) e -> p k e", p=P), "weights")
        K.dma(Q, w_bc[:, :, j, NS:], W["L1_attn_a_W_C"].rearrange("(k p) e -> p k e", p=P), "weights")
    K.dma(Q, vec[:], W["ssm_vectors"], "weights")
    K.dma(Q, A[:], W["L1_attn_a_A_log"].rearrange("(k p) n -> p k n", p=P), "weights")
    K.dma(Q, norm_w[:], W["L1_norm_w"], "weights")
    loaded = K.dma(Q, sel[:], W["const_selectors"], "weights")
    S.wait(loaded)
    V.wait(S.did(S.e.activation(A[:], A[:], ACT.Exp)))
    a_ready = V.did(V.e.tensor_scalar(A[:], A[:], -1.0, None, ALU.mult))
    for e in (V, S, G, T):
        e.wait(loaded, a_ready)

    K.start_combine(M)
    sc = Scan(K, M, DT, NS)
    xn = M.sb("xn", [P, TPC, D])
    xT = [M.sb(f"xT{i}", [P, DT, CH]) for i in range(2)]
    dt = [M.sb(f"dt{i}", [P, DT, CH]) for i in range(2)]
    dtu = [M.sb(f"dtu{i}", [P, DT, CH]) for i in range(2)]
    BC3 = [M.sb(f"BC3_{i}", [96, CH], BF16) for i in range(2)]
    y = [M.sb(f"y{i}", [P, DT, CH]) for i in range(2)]
    rest, ab = M.sb("bc_rest", [96, CH]), M.sb("softplus", [P, DT, CH])
    stat = M.sb("stat", [P, 4])
    small = M.sb("bound", [1, 8])
    flag = [M.sb(f"clip_flag{i}", [1, 1], I32) for i in range(2)]
    state = M.sb("clipped_state", [P, DT])
    pick = rotation([Bank(M.ps(f"front{i}", [P, CH])) for i in range(2)])
    st = {"ready": [None, None], "done": [None, None], "xn_free": None,
          "y_read": [None, None]}
    V.did(V.e.memset(stat[:], 0.0))
    V.did(V.e.memset(small[:], 0.0))
    V.wait(V.own())

    def front(c):
        r = c % 2
        V.wait(st["done"][r])
        x4 = X[:, TPC * c:TPC * (c + 1), :]
        yield
        stats = layernorm_stats(K, M, x4, TPC, K.x_ready(c))
        yield
        yield
        V.wait(st["xn_free"])
        normed = layernorm_apply(K, M, x4, xn, TPC, stats)
        yield
        for k in range(DT):
            f = pick()
            T.wait(normed, f.free)
            for i in range(TPC):
                T.did(T.e.transpose(f.ap[:, i * P:(i + 1) * P], xn[:, i, k * P:(k + 1) * P], K.ident[:]))
            st["xn_free"] = made = T.own()
            yield
            f.free = x_here = do(S, lambda: S.e.activation(xT[r][:, k, :], f.ap[:], ACT.Copy), made, st["done"][r])
            yield
        f = pick()
        T.wait(x_here, f.free)
        for k in range(DT):
            T.did(T.e.matmul(f.ap[0:96, :], w_bc[:, k, :, :].rearrange("p a b -> p (a b)"), xT[r][:, k, :],
                             start=k == 0, stop=k == DT - 1))
        made = T.own()
        yield
        max_b = do(V, lambda: V.e.tensor_reduce(stat[0:NS, 2:3], f.ap[0:NS, :], AX.X, ALU.max,
                                                apply_absolute_value=True), made, V.own(), st.get("stat_read"))
        f.free = split_done = split3(K, f.ap, BC3[r], rest, [made, st["done"][r], V.own()])
        yield
        for d in range(DT):
            f = pick()
            T.wait(f.free)
            for k in range(DT):
                T.did(T.e.matmul(f.ap[:], w_delta[:, k, d * P:(d + 1) * P], xT[r][:, k, :],
                                 start=k == 0, stop=k == DT - 1))
            made = T.own()
            yield
            K.prefetch(2)
            a1 = do(S, lambda: S.e.activation(ab[:, d, :], f.ap[:], ACT.Abs, bias=vec[:, d, 0:1]), made, st.get("ab_free"))
            f.free = do(V, lambda: V.e.tensor_scalar(dt[r][:, d, :], f.ap[:], vec[:, d, 0:1], 0.0, ALU.add, ALU.max), a1)
            yield
        e1 = do(S, lambda: S.e.activation(ab[:], ab[:], ACT.Exp, scale=-1.0), S.own())
        e2 = do(S, lambda: S.e.activation(ab[:], ab[:], ACT.Ln, bias=1.0), e1)
        yield
        yield
        made_dt = do(V, lambda: V.e.tensor_tensor(dt[r][:], dt[r][:], ab[:], ALU.add), e2, V.own())
        made_dtu = do(G, lambda: G.e.tensor_tensor(dtu[r][:], dt[r][:], xT[r][:], ALU.mult), made_dt)
        yield
        yield
        s1 = do(V, lambda: V.e.tensor_reduce(stat[:, 0:1], dt[r][:], AX.XY, ALU.max), made_dt, max_b)
        s2 = do(V, lambda: V.e.tensor_reduce(ab[:, :, 0], dtu[r][:], AX.X, ALU.add, apply_absolute_value=True), made_dtu)
        s3 = do(V, lambda: V.e.tensor_reduce(stat[:, 1:2], ab[:, :, 0], AX.X, ALU.max), s2)
        f = pick()
        T.wait(s1, s3, f.free)
        for j in range(3):
            T.did(T.e.matmul(f.ap[0:1, j * P:(j + 1) * P], stat[:, j:j + 1], K.ident[:], start=True, stop=True))
        st["ab_free"] = s3
        made = st["stat_read"] = T.own()
        yield

        def v(inst):
            V.wait(V.did(inst))
        V.wait(made)
        v(V.e.tensor_reduce(small[:, 0:3], f.ap[0:1, 0:3 * P].rearrange("p (a b) -> p a b", a=3), AX.X, ALU.max))
        f.free = V.own()
        v(V.e.tensor_tensor(small[:, 3:5], small[:, 0:2], small[:, 2:3].to_broadcast([1, 2]), ALU.mult))
        if c % CPB:
            v(V.e.tensor_tensor(small[:, 5:6], small[:, 5:6], small[:, 4:5], ALU.add))
        else:
            v(V.e.tensor_copy(small[:, 5:6], small[:, 4:5]))
        v(V.e.tensor_scalar(small[:, 6:7], small[:, 3:4], BAR_B_MAX * 0.99, None, ALU.is_gt))
        v(V.e.tensor_scalar(small[:, 7:8], small[:, 5:6], H_MAX * 0.99, None, ALU.is_gt))
        v(V.e.tensor_tensor(small[:, 6:7], small[:, 6:7], small[:, 7:8], ALU.add))
        flagged = do(V, lambda: V.e.tensor_copy(flag[r][:], small[:, 6:7]))
        st["ready"][r] = [made_dtu, made_dt, split_done]
        st["flag"] = flagged
        yield

    regs = {}

    def clipped(sc, r, n, c):
        if n == 0:
            V.wait(st["flag"])
            regs[c] = V.e.value_load(flag[c % 2][0:1, 0:1], min_val=0, max_val=2)
        q = c % 2
        with V.e.If(regs[c] > 0):
            V.e.drain()
            for d in range(DT):
                V.e.tensor_tensor(sc.dBu[r][:, d, :], dt[q][:, d, :], sc.Bb[r][:], ALU.mult)
            V.e.drain()
            V.e.tensor_scalar(sc.dBu[r][:], sc.dBu[r][:], BAR_B_MAX, -BAR_B_MAX, ALU.min, ALU.max)
            V.e.drain()
            V.e.tensor_tensor(sc.dBu[r][:], sc.dBu[r][:], xT[q][:], ALU.mult)
            if c % CPB:
                V.e.tensor_copy(state[:], sc.carry[:, n, :])
            else:
                V.e.memset(state[:], 0.0)
            with V.e.Fori(0, CH) as t:
                V.e.drain()
                V.e.tensor_tensor(state[:], state[:], sc.dA[r][:, :, bass.ds(t, 1)], ALU.mult)
                V.e.drain()
                V.e.tensor_tensor(state[:], state[:], sc.dBu[r][:, :, bass.ds(t, 1)], ALU.add)
                V.e.drain()
                V.e.tensor_scalar(state[:], state[:], H_MAX, -H_MAX, ALU.min, ALU.max)
                V.e.drain()
                V.e.tensor_copy(sc.dBu[r][:, :, bass.ds(t, 1)], state[:])
            V.e.drain()

    def take_y(c):
        r = c % 2
        V.wait(sc.summed[(c + 1) * NS - 1], st["y_read"][r])
        for d in range(DT):
            V.did(V.e.scalar_tensor_tensor(y[r][:, d, :], xT[r][:, d, :], vec[:, d, 1:2], sc.y[d][:],
                                           ALU.mult, ALU.add))
        sc.y_free = st["done"][r] = V.own()

    def back(c):
        r = c % 2
        y_made = st["done"][r]
        for i in range(0, TPC, 2):
            f = pick()
            T.wait(f.free, y_made)
            for j in range(2):
                for k in range(DT):
                    T.did(T.e.transpose(f.ap[:, j * D + k * P:j * D + (k + 1) * P],
                                        y[r][:, k, (i + j) * P:(i + j + 1) * P], K.ident[:]))
            made = T.own()
            yield
            f.free = do(S, lambda: S.e.activation(
                y_rows[:, TPC * c + i:TPC * c + i + 2, :], f.ap[:].rearrange("p (a c) -> p a c", a=2), ACT.Copy), made)
            yield
        for i in range(TPC):
            for k in range(DT):
                T.did(T.e.matmul(R.logits[:, TPC * c + i, :], y[r][:, k, i * P:(i + 1) * P], w_router[:, k, :],
                                 start=k == 0, stop=k == DT - 1))
        st["y_read"][r] = T.own()
        yield
        yield

    run_scan(sc, front, take_y, back, lambda c: (dt[c % 2], dtu[c % 2][:], BC3[c % 2][:], A, sel, st["ready"][c % 2]),
             clipped)
    M.free()
    M = M0
    w_gu = M.sb("w_gate_up", [P, E, DT, 2 * F])
    w_d = M.sb("w_down", [P, E, F // P, D])
    gain = M.sb("inner_gain", [P, E, F // P])
    K.dma(Q, gain[:], W["L1_inner_gain"], "weights")
    for e in range(E):
        for j, n in enumerate(("Wg", "Wu")):
            K.dma(Q, w_gu[:, e, :, j * F:(j + 1) * F], W["L1_attn_a_" + n][e].rearrange("(k p) f -> p k f", p=P), "weights")
        loaded = K.dma(Q, w_d[:, e, :, :], W["L1_attn_a_Wd"][e].rearrange("(k p) c -> p k c", p=P), "weights")
    routed = R.run(T.own(), normalise=True)
    scattered = R.scatter(y_rows, routed)
    V.wait(loaded)
    folded = V.did(V.e.tensor_tensor(w_d[:].rearrange("p e k c -> p (e k) c"), w_d[:].rearrange("p e k c -> p (e k) c"),
                                     last(gain[:].rearrange("p e k -> p (e k)"), D), ALU.mult))
    T.wait(loaded, folded)
    G.wait(expert_tiles(K, M, R, E, F, w_gu, w_d, routed, scattered, rms=True))
    V.wait(scattered)
    own = Combine(K, M, y_rows)
    sums, rt = M.sb("y_sums", [P, NT]), M.sb("y_rms", [P, NT])
    sq = M.sb("y_squares", [P, D])

    def normalise(tiles, ready):
        V.wait(ready)
        for t in range(tiles.start, tiles.stop):
            do(V, lambda: V.e.scalar_tensor_tensor(X[:, t, :], y_rows[:, t, :], rt[:, t:t + 1], X[:, t, :],
                                                   ALU.mult, ALU.add))

    behind = None
    for c in range(NC):
        tiles = slice(TPC * c, TPC * (c + 1))
        S.wait(own.through(tiles.stop))
        own.prefetch(TPC)
        for t in range(tiles.start, tiles.stop):
            do(S, lambda: S.e.activation(sq[:], y_rows[:, t, :], ACT.Square, accum_out=sums[:, t:t + 1]), S.own())
        if behind is not None:
            normalise(*behind)
        ve = do(V, lambda: V.e.tensor_scalar(sums[:, tiles], sums[:, tiles], 1.0 / D, 1e-6, ALU.mult, ALU.add), S.own())
        rooted = do(G, lambda: G.e.tensor_tensor(rt[:, tiles], sums[:, tiles], K.neghalf[:, tiles], ALU.pow), ve)
        scaled = do(V, lambda: V.e.tensor_tensor(y_rows[:, tiles, :], y_rows[:, tiles, :], mid(norm_w[:], TPC), ALU.mult))
        behind = (tiles, [rooted, scaled])
    normalise(*behind)
    K.x_is_ready()
    M.free()


def moe1_stage(K, W):
    V, S, G, T, Q = K.V, K.S, K.G, K.T, K.Q
    X, E, F, FS = K.X, 16, 128, 256
    M = Memory(K)
    R = Routing(K, M, E)
    lns = [Statistics(M, i) for i in range(2)]
    xn = M.sb("xn", [P, NT, D])
    wr = M.sb("w_router", [P, DT, E])
    w_s = M.sb("w_shared_gate_up", [P, DT, 2 * FS])
    w_sd = M.sb("w_shared_down", [P, FS // P, D])
    w_gu = M.sb("w_gate_up", [P, E, DT, 2 * F])
    w_d = M.sb("w_down", [P, E, 1, D])
    rows_of = lambda n: W["L1_ffn_" + n].rearrange("(k p) e -> p k e", p=P)
    K.dma(Q, wr[:], rows_of("Wr"), "weights")
    K.dma(Q, w_s[:, :, 0:FS], rows_of("Sg"), "weights")
    K.dma(Q, w_s[:, :, FS:], rows_of("Su"), "weights")
    shared_here = K.dma(Q, w_sd[:], rows_of("Sd"), "weights")
    for j, n in enumerate(("Wg", "Wu")):
        for e in range(E):
            K.dma(Q, w_gu[:, e, :, j * F:(j + 1) * F], W["L1_ffn_" + n][e].rearrange("(k p) f -> p k f", p=P), "experts")
    experts_here = K.dma(Q, w_d[:, :, 0, :], W["L1_ffn_Wd"].rearrange("e p c -> p e c"), "experts")
    MS = Memory(K)
    xT = [MS.sb(f"xT{i}", [P, DT, CH]) for i in range(NC)]
    hs = [MS.sb(f"shared_act{i}", [P, FS // P, CH]) for i in range(2)]
    hm = [MS.sb(f"shared_mid{i}", [P, FS // P, CH]) for i in range(2)]
    sb_ = [Bank(MS.ps(f"shared{i}", [P, CH])) for i in range(4)]
    T.wait(shared_here)
    turn = rotation(sb_)
    stats = layernorm_stats(K, lns[0], X[:, 0:TPC, :], TPC, K.x_ready(0))
    for c in range(NC):
        r = c % 2
        tiles = slice(TPC * c, TPC * (c + 1))
        if c + 1 < NC:
            ahead = layernorm_stats(K, lns[1 - r], X[:, TPC * (c + 1):TPC * (c + 2), :], TPC, K.x_ready(c + 1))
        normed = layernorm_apply(K, lns[r], X[:, tiles, :], xn[:, tiles, :], TPC, stats)
        stats = ahead
        T.wait(channel_major(K, xn[:, tiles, :], xT[c], turn, normed, None))
        for i in range(TPC):
            for k in range(DT):
                T.did(T.e.matmul(R.logits[:, TPC * c + i, :], xT[c][:, k, i * P:(i + 1) * P], wr[:, k, :],
                                 start=k == 0, stop=k == DT - 1))
    routed = R.run(T.own())
    scattered = R.scatter(xn, routed)
    act_free, mid_free = [None, None], [None, None]
    for c in range(NC):
        r = c % 2
        for f in range(FS // P):
            made = []
            for j in range(2):
                b = turn()
                T.wait(b.free)
                for k in range(DT):
                    T.did(T.e.matmul(b.ap[:], w_s[:, k, j * FS + f * P:j * FS + (f + 1) * P], xT[c][:, k, :],
                                     start=k == 0, stop=k == DT - 1))
                made.append((b, T.own()))
            (gb, g_made), (ub, u_made) = made
            gb.free = do(S, lambda: S.e.activation(hs[r][:, f, :], gb.ap[:], ACT.Silu), g_made, act_free[r])
            ub.free = mid_made = do(V, lambda: V.e.tensor_tensor(hm[r][:, f, :], hs[r][:, f, :], ub.ap[:], ALU.mult),
                                    gb.free, u_made, mid_free[r])
        act_free[r] = mid_made
        for i in range(0, TPC, 2):
            b = turn()
            T.wait(b.free, mid_made)
            for j in range(2):
                for f in range(FS // P):
                    T.did(T.e.matmul(b.ap[:, j * D:(j + 1) * D], hm[r][:, f, (i + j) * P:(i + j + 1) * P], w_sd[:, f, :],
                                     start=f == 0, stop=f == FS // P - 1))
            xt = X[:, TPC * c + i:TPC * c + i + 2, :]
            b.free = do(V, lambda: V.e.tensor_tensor(xt, xt, b.ap[:].rearrange("p (a c) -> p a c", a=2), ALU.add), T.own())
        mid_free[r] = T.own()
    MS.free()
    T.wait(experts_here)
    expert_tiles(K, M, R, E, F, w_gu, w_d, routed, scattered)
    K.x_is_ready()
    K.owed = True
    M.free()


def attention_stage(K, W):
    V, S, G, T, Q = K.V, K.S, K.G, K.T, K.Q
    X = K.X
    HD, HU, DC = 16, 8, 64
    KT = L // P
    Q_PARTS, K_PARTS = (0, 0, 1, 0, 2, 1), (0, 1, 0, 2, 0, 1)
    ROWS = 6 * HD
    M = Memory(K)
    ln_buffers(M, TPC)
    w = {}
    for n, rows, c in (("wq", D, DC), ("wkv", D, DC), ("wqr", D, P), ("wqr_turned", D, P), ("wkr", D, P),
                       ("wkr_turned", D, P), ("wo", D, D)):
        w[n] = M.sb("w_" + n, [P, DT, c])
        K.dma(Q, w[n][:], W["attn_" + n].rearrange("(k p) c -> p k c", p=P), "weights")
    for n, c in (("wqc", P), ("wkc", P), ("wv", D)):
        w[n] = M.sb("w_" + n, [DC, c])
        K.dma(Q, w[n][:], W["attn_" + n], "weights")
    b64 = M.sb("latent_biases", [DC, 2])
    b128 = M.sb("biases", [P, 6])
    bv, bo = M.sb("bv", [P, D]), M.sb("bo", [P, D])
    cos, sin = M.sb("cos", [P, L]), M.sb("sin", [P, L])
    ident_bf = M.sb("ident_bf", [P, P], BF16)
    mask_qk, mask_kq = M.sb("mask_qk", [P, P], BF16), M.sb("mask_kq", [P, P], BF16)
    for to, n in ((b64, "attn_b64"), (b128, "attn_b128"), (bv, "attn_bv"), (bo, "attn_bo"), (cos, "const_cos"),
                  (sin, "const_sin"), (ident_bf, "const_ident_bf"), (mask_qk, "const_mask_qk"),
                  (mask_kq, "const_mask_kq")):
        loaded = K.dma(Q, to[:], W[n], "weights")
    for e in (V, S, G, T):
        e.wait(loaded)
    xT = M.sb("xT", [P, DT, L])
    latent = {"q": M.sb("latent_q", [DC, L]), "k": M.sb("latent_k", [DC, L])}
    pre = M.sb("pre_gelu", [P, L])
    full = M.sb("activated", [P, L])
    xn = full[:].rearrange("p (a c) -> p a c", a=TPC)
    parts = {n: M.sb("parts_" + n, [P, 3, L], BF16) for n in "qk"}
    QS = [M.sb(f"queries{i}", [ROWS + 3, HU, L], BF16) for i in range(2)]
    KS = [M.sb(f"keys{i}", [ROWS + 3, HU, L], BF16) for i in range(2)]
    V1 = [M.sb(f"values{i}", [P, KT, HU, 32]) for i in range(2)]
    mx = M.sb("maxima", [P, KT, HU, 2])
    mn = M.sb("minus_max", [P, KT * HU])
    mT = M.sb("max_rows", [KT * HU, P])
    mP = M.sb("max_parts", [KT * HU, 3, P], BF16)
    PT = [M.sb(f"weights_T{i}", [P, 4, CH]) for i in range(2)]
    oT = M.sb("out_T", [P, CH])
    rec = M.sb("reciprocal", [P, 4, 4])
    O = M.sb("out_rows", [P, KT, D])
    oTT, oTT_free = [M.sb(f"out_channels{i}", [P, DT, P]) for i in range(2)], [None, None]
    dram = {n: K.nc.dram_tensor(f"parts_of_{n}", [3, P, L], BF16, kind="Internal").ap() for n in "qk"}
    dram_m = K.nc.dram_tensor("parts_of_max", [3, HU, KT, P], BF16, kind="Internal").ap()
    st_ = [M.ps(f"scores_T{i}", [P, 2, CH]) for i in range(2)]
    sb2 = [Bank(M.ps(f"scores{i}", [P, CH])) for i in range(2)]
    ob, mb = Bank(M.ps("out_sum", [P, CH])), Bank(M.ps("misc", [P, CH]))
    for i in range(2):
        V.did(V.e.memset(V1[i][:], 0.0))
        V.did(V.e.memset(KS[i][ROWS:ROWS + 3, :, :], 1.0))
    V.wait(V.own())
    for i in range(2):
        V.did(V.e.memset(V1[i][:, :, :, HD], 1.0))
    V.did(V.e.memset(mx[:], -1e38))
    V.wait(V.own())
    for e in (S, T, Q):
        e.wait(V.own())
    unit_done = [None, None]
    ready = {}
    st = {"staged": {"q": None, "k": None}, "mx": None, "m_stored": None, "part_free": None}

    def unit_a(u):
        b, ct, r = u // DT, u % DT, u % 2
        spare = [mb] + sb2
        turns = itertools.cycle(spare)
        if ct == 0:
            for c2 in range(CPB):
                c = b * CPB + c2
                stats = layernorm_stats(K, M, X[:, TPC * c:TPC * (c + 1), :], TPC, K.x_ready(c))
                yield
                V.wait(st.get("full_free"))
                normed = layernorm_apply(K, M, X[:, TPC * c:TPC * (c + 1), :], xn, TPC, stats)
                yield
                for k in range(DT):
                    f = next(turns)
                    T.wait(normed, f.free)
                    for i in range(TPC):
                        T.did(T.e.transpose(f.ap[:, i * P:(i + 1) * P], xn[:, i, k * P:(k + 1) * P], K.ident[:]))
                    st["full_free"] = T.own()
                    f.free = x_here = do(S, lambda: S.e.activation(xT[:, k, c2 * CH:(c2 + 1) * CH], f.ap[:], ACT.Copy),
                                         T.own(), st["part_free"])
                K.prefetch(2)
                yield
            for j, (n, wn) in enumerate((("q", "wq"), ("k", "wkv"))):
                for c2 in range(CPB):
                    f = next(turns)
                    T.wait(x_here, f.free)
                    for k in range(DT):
                        T.did(T.e.matmul(f.ap[0:DC, :], w[wn][:, k, :], xT[:, k, c2 * CH:(c2 + 1) * CH],
                                         start=k == 0, stop=k == DT - 1))
                    K.prefetch()
                    f.free = latent_here = do(S, lambda: S.e.activation(
                        latent[n][:, c2 * CH:(c2 + 1) * CH], f.ap[0:DC, :], ACT.Gelu, bias=b64[:, j:j + 1]),
                        T.own(), st["part_free"])
                yield
            T.wait(latent_here)
        for j, n in enumerate("qk"):
            if ct == 0:
                for c2 in range(CPB):
                    cs, f = slice(c2 * CH, (c2 + 1) * CH), next(turns)
                    T.wait(f.free)
                    T.did(T.e.matmul(f.ap[:], w["wqc" if n == "q" else "wkc"][:], latent[n][:, cs], start=True, stop=True))
                    f.free = made = do(S, lambda: S.e.activation(full[:, cs], f.ap[:], ACT.Gelu, bias=b128[:, j:j + 1]),
                                       T.own(), st.get("full_free"))
                yield
            else:
                for i, (wn, table, to) in enumerate((("r", cos, pre), ("r_turned", sin, full))):
                    for c2 in range(CPB):
                        cs, f = slice(c2 * CH, (c2 + 1) * CH), next(turns)
                        T.wait(f.free)
                        for k in range(DT):
                            T.did(T.e.matmul(f.ap[:], w["w" + n + wn][:, k, :], xT[:, k, cs],
                                             start=k == 0, stop=k == DT - 1))
                        bias = b128[:, 2 + 2 * j + i:3 + 2 * j + i]
                        f.free = do(V, lambda: V.e.scalar_tensor_tensor(to[:, cs], f.ap[:], bias, table[:, cs],
                                                                        ALU.add, ALU.mult), T.own(), st.get("pre_free"),
                                    st.get("full_free"))
                    yield
                summed = do(V, lambda: V.e.tensor_tensor(pre[:], pre[:], full[:], ALU.add), V.own())
                made = do(S, lambda: S.e.activation(full[:], pre[:], ACT.Gelu), summed, st.get("full_free"))
                st["pre_free"] = made
                yield
            pt = parts[n]
            p1 = do(V, lambda: V.e.tensor_copy(pt[:, 0, :], full[:]), made, st["staged"][n])
            r1 = do(V, lambda: V.e.tensor_tensor(full[:], full[:], pt[:, 0, :], ALU.subtract), p1)
            p2 = do(V, lambda: V.e.tensor_copy(pt[:, 1, :], full[:]), r1)
            r2 = do(V, lambda: V.e.tensor_tensor(full[:], full[:], pt[:, 1, :], ALU.subtract), p2)
            p3 = do(V, lambda: V.e.tensor_copy(pt[:, 2, :], full[:]), r2)
            st["full_free"] = p3
            yield
            Q.wait(p3, st.get("stacked_" + n))
            st["staged"][n] = K.dma(Q, dram[n].rearrange("a c t -> c a t"), pt[:], "stage_" + n)
            to, order = (QS[r], Q_PARTS) if n == "q" else (KS[r], K_PARTS)
            Q.wait(st["staged"][n], unit_done[r])
            for i, part in enumerate(order):
                here = K.dma(Q, to[i * HD:(i + 1) * HD, :, :], dram[n][part].rearrange("(h d) t -> d h t", d=HD),
                             f"stack_{n}{r}")
            st["stacked_" + n] = here
        for i in range(0, KT, 4):
            f = next(turns)
            T.wait(f.free)
            for j in range(4):
                T.did(T.e.matmul(f.ap[:, j * P:(j + 1) * P], latent["k"][:, (i + j) * P:(i + j + 1) * P],
                                 w["wv"][:, ct * P:(ct + 1) * P], start=True, stop=True))
            T_done = T.own()
            V.wait(T_done, unit_done[r])
            for j in range(4):
                f.free = v_ready = V.did(V.e.tensor_tensor(
                    V1[r][:, i + j, :, 0:HD], f.ap[:, j * P:(j + 1) * P].rearrange("p (h d) -> p h d", d=HD),
                    bv[:, ct * P:(ct + 1) * P].rearrange("p (h d) -> p h d", d=HD), ALU.add))
            yield
        st["part_free"] = T.own()
        for _ in range(3):
            yield
        T.wait(st["stacked_q"], st["stacked_k"])
        nb = 0
        V.wait(st["mx"])
        for h in range(HU):
            for qt in range(KT):
                for half in range(qt // 4 + 1):
                    f = sb2[nb % 2]
                    nb += 1
                    n_keys = min(CH, (qt + 1) * P - half * CH)
                    diagonal = half == qt // 4
                    T.wait(f.free)
                    T.did(T.e.matmul(f.ap[:, 0:n_keys], QS[r][0:ROWS, h, qt * P:(qt + 1) * P],
                                     KS[r][0:ROWS, h, half * CH:half * CH + n_keys], start=True, stop=not diagonal))
                    if diagonal:
                        T.did(T.e.matmul(f.ap[:, n_keys - P:n_keys], ident_bf[:], mask_qk[:], start=False, stop=True))
                    f.free = do(V, lambda: V.e.tensor_reduce(mx[:, qt, h, half:half + 1], f.ap[:, 0:n_keys], AX.X, ALU.max),
                                T.own())
                    yield "short"
        neg = do(V, lambda: V.e.tensor_reduce(mn[:], mx[:], AX.X, ALU.max, negate=True), V.own(), st.get("mn_free"))
        st["mx"] = neg
        T.wait(neg, mb.free)
        st["mn_free"] = T.did(T.e.transpose(mb.ap[0:KT * HU, 0:P], mn[:], K.ident[:]))
        mb.free = c0 = do(V, lambda: V.e.tensor_copy(mT[:], mb.ap[0:KT * HU, 0:P]), T.own())
        m1 = do(V, lambda: V.e.tensor_copy(mP[:, 0, :], mT[:]), c0, st["m_stored"])
        r1 = do(V, lambda: V.e.tensor_tensor(mT[:], mT[:], mP[:, 0, :], ALU.subtract), m1)
        m2 = do(V, lambda: V.e.tensor_copy(mP[:, 1, :], mT[:]), r1)
        r2 = do(V, lambda: V.e.tensor_tensor(mT[:], mT[:], mP[:, 1, :], ALU.subtract), m2)
        m3 = do(V, lambda: V.e.tensor_copy(mP[:, 2, :], mT[:]), r2)
        Q.wait(m3, st.get("m_stacked"))
        for qt in range(KT):
            st["m_stored"] = K.dma(Q, dram_m[:, :, qt, :].rearrange("a h t -> h a t"),
                                   mP[qt * HU:(qt + 1) * HU, :, :], "stage_m")
        Q.wait(st["m_stored"])
        st["m_stacked"] = K.dma(Q, QS[r][ROWS:ROWS + 3, :, :], dram_m.rearrange("a h q t -> a h (q t)"), f"stack_m{r}")
        ready[u] = [v_ready, st["m_stacked"], st["stacked_q"], st["stacked_k"]]
        yield

    score_free, pt_free, pt_n = [None, None], [None, None], [0]
    o_read = [None]

    def unit_b(u):
        b, ct, r = u // DT, u % DT, u % 2
        T.wait(ready[u])
        steps = [(hg, qh, kt) for hg in range(2) for qh in range(2) for kt in range(4 * qh + 4)]
        later = []

        def product(hg, qh, kt, pt, slot, weighed):
            last_kt = 4 * qh + 3
            o = max(0, kt * P - qh * CH)
            T.wait(weighed, ob.free if kt == 0 else None)
            for j in range(4):
                T.did(T.e.matmul(ob.ap[32 * j:32 * j + 32, o:CH], V1[r][:, kt, hg * 4 + j, :],
                                 pt[:, j, o:CH], start=kt == 0, stop=kt == last_kt))
            pt_free[slot] = T.own()
            if kt == last_kt:
                ob.free = taken = do(S, lambda: S.e.activation(oT[:], ob.ap[:], ACT.Copy), T.own(), st.get("oT_free"))
                later.append(lambda: finish(hg, qh, taken))

        def finish(hg, qh, taken):
            T.wait(taken, mb.free)
            for t in range(4):
                T.did(T.e.transpose(mb.ap[:, t * P:(t + 1) * P], oT[:, t * P:(t + 1) * P], K.ident[:]))
            st["oT_free"] = T.own()
            v4 = mb.ap[:].rearrange("p (t h d) -> p t h d", t=4, h=4)
            rc = do(V, lambda: V.e.reciprocal(rec[:], v4[:, :, :, HD]), T.own(), st.get("rec_free"))
            h0 = (ct * HU + hg * 4) * HD
            V.wait(rc, o_read[0])
            for t in range(4):
                V.did(V.e.tensor_tensor(
                    O[:, qh * 4 + t, h0:h0 + 4 * HD].rearrange("p (h d) -> p h d", h=4), v4[:, t, :, 0:HD],
                    last(rec[:, t, :], HD), ALU.mult))
            mb.free = st["rec_free"] = V.own()

        for hg, qh, kt in steps:
            diagonal = kt * P >= qh * CH
            o = max(0, kt * P - qh * CH)
            slot = pt_n[0] % 2
            pt = PT[slot]
            pt_n[0] += 1
            for pair in range(2):
                T.wait(score_free[pair])
                for j in range(2):
                    h = hg * 4 + pair * 2 + j
                    T.did(T.e.matmul(st_[pair][:, j, o:CH], KS[r][:, h, kt * P:(kt + 1) * P],
                                     QS[r][:, h, qh * CH + o:(qh + 1) * CH], start=True, stop=not diagonal))
                    if diagonal:
                        T.did(T.e.matmul(st_[pair][:, j, o:o + P], ident_bf[:], mask_kq[:], start=False, stop=True))
                score_free[pair] = do(S, lambda: S.e.activation(
                    pt[:, 2 * pair:2 * pair + 2, o:CH], st_[pair][:, :, o:CH], ACT.Exp, scale=HD ** -0.5),
                    T.own(), pt_free[slot])
                if pair == 0:
                    yield
            weighed = S.own()
            due, later = later, []
            for issue in due:
                issue()
            later.append(lambda a=(hg, qh, kt, pt, slot, weighed): product(*a))
            yield
        while later:
            due, later = later, []
            for issue in due:
                issue()
            yield
        unit_done[r] = [T.own()]
        if ct == DT - 1:
            rows_ready, turned = V.own(), {}
            for t in range(KT + 1):
                if t < KT:
                    T.wait(mb.free, rows_ready)
                    for k in range(DT):
                        T.did(T.e.transpose(mb.ap[:, k * P:(k + 1) * P], O[:, t, k * P:(k + 1) * P], K.ident[:]))
                    o_read[0] = T.own()
                    turned[t] = mb.free = do(S, lambda: S.e.activation(
                        oTT[t % 2][:], mb.ap[:, 0:D].rearrange("p (k q) -> p k q", k=DT), ACT.Copy),
                        o_read[0], oTT_free[t % 2])
                if t:
                    q = (t - 1) % 2
                    T.wait(turned[t - 1], ob.free)
                    for k in range(DT):
                        T.did(T.e.matmul(ob.ap[:, q * D:(q + 1) * D], oTT[q][:, k, :], w["wo"][:, k, :],
                                         start=k == 0, stop=k == DT - 1))
                    oTT_free[q] = T.own()
                    xt = X[:, b * KT + t - 1, :]
                    ob.free = s1 = do(V, lambda: V.e.tensor_tensor(xt, xt, ob.ap[:, q * D:(q + 1) * D], ALU.add),
                                      T.own())
                    do(V, lambda: V.e.tensor_tensor(xt, xt, bo[:], ALU.add), s1)
                yield

    K.start_combine(M, ring=2)
    n_units = NB * DT
    n_short = HU * sum(qt // 4 + 1 for qt in range(KT))
    b_steps = 2 * 2 * sum(4 * qh + 4 for qh in range(2)) + 2
    for _ in unit_a(0):
        pass
    for u in range(n_units):
        side = unit_a(u + 1) if u + 1 < n_units else iter(())
        step, short = None, n_short
        left = b_steps + (KT + 1 if u % DT == DT - 1 else 0)
        for _ in unit_b(u):
            take = max(1, -(-short // max(1, left))) if step == "short" else 1
            left -= 1
            for _ in range(take):
                step = next(side, None)
            short -= take if step == "short" else 0
        for _ in side:
            pass
    K.x_is_ready()
    M.free()


STAGES = {"mamba": mamba_stage, "moe0a": moe0_stage, "moe0b": moe0_stage,
          "rwkv": rwkv_stage, "ssm1": ssm1_stage, "moe1a": moe1_stage, "moe1b": moe1_stage,
          "attn": attention_stage}
ORDER = ["mamba", "moe0a", "rwkv", "moe0b", "ssm1", "moe1a", "attn", "moe1b"]


def zero_rows(K, ready):
    K.Q.wait(ready, K.zeros_made)
    for s0 in range(0, SLOT_TILES, 8):
        for to in (K.sorted_in, K.sorted_out):
            K.dma(K.Q, to[s0 * P:(s0 + 8) * P, :].rearrange("(p a) (b c) -> p (a b) c", p=P, b=2),
                  mid(K.zeros[:], 16), "zeros")
    K.sorted_read = K.dma(K.Q, K.sorted_out[SLOTS:SLOTS + 1, :].rearrange("a (b c) -> (a b) c", b=2),
                          K.zeros[0:2, :], "zeros")


def build_program(nc, W, x_in, out, stages):
    with ExitStack() as stack:
        K = Core(nc, stack)
        K.X = stack.enter_context(nc.sbuf_tensor("residual", [P, NT, D], F32))
        K.ident = stack.enter_context(nc.sbuf_tensor("identity", [P, P], F32))
        K.neghalf = stack.enter_context(nc.sbuf_tensor("neghalf", [P, NT], F32))
        K.V.did(K.V.e.memset(K.neghalf[:], -0.5))
        half = K.V.own()
        K.dma(K.Q, K.ident[:], W["const_identity"], "x")
        x_tiles, out_tiles = (ap.rearrange("(t p) c -> p t c", p=P) for ap in (x_in, out))
        for c in range(NC):
            tiles = slice(TPC * c, TPC * (c + 1))
            queue, stream = (K.Q, "x") if c == 0 else (K.S, f"x{c}")
            K.chunk_marks[c] = K.dma(queue, K.X[:, tiles, :], x_tiles[:, tiles, :], stream)
        K.iota, K.before, K.ones_bf = (stack.enter_context(nc.sbuf_tensor(n, [P, P], t)) for n, t in
                                       (("iota", F32), ("before", BF16), ("ones_bf", BF16)))
        K.dma(K.Q, K.iota[:], W["const_iota"], "const")
        K.dma(K.Q, K.before[:], W["const_before"], "const")
        consts = K.dma(K.Q, K.ones_bf[:], W["const_ones"], "const")
        K.sorted_in = nc.dram_tensor("sorted_rows", [SLOTS, D], F32, kind="Internal").ap()
        K.sorted_out = nc.dram_tensor("sorted_results", [SLOTS + 1, D], F32, kind="Internal").ap()
        K.pick_weight, K.pick_row = ([stack.enter_context(nc.sbuf_tensor(f"{n}{i}", [P, NT], t)) for i in range(2)]
                                     for n, t in (("pick_weight", F32), ("pick_row", I32)))
        K.zeros = stack.enter_context(nc.sbuf_tensor("zeros", [P, D // 2], F32))
        K.zeros_made = K.V.did(K.V.e.memset(K.zeros[:], 0.0))
        if stages[0] != "mamba":
            zero_rows(K, None)
        for e in (K.V, K.S, K.G, K.T):
            e.wait(consts, half)
        for s in stages:
            STAGES[s](K, W)
        M = Memory(K)
        K.start_combine(M, ring=2 * TPC)
        for c in range(NC):
            tiles = slice(TPC * c, TPC * (c + 1))
            K.Q.wait(K.x_ready(c))
            K.prefetch(TPC)
            K.dma(K.Q, out_tiles[:, tiles, :], K.X[:, tiles, :], "out")
        M.free()


def prepare(inputs):
    bf16 = mybir.dt.np(BF16)
    a = {k: np.asarray(v) for k, v in inputs.items()}
    x = np.ascontiguousarray(a.pop("L0_attn_a_x").reshape(T_ALL, D))

    def cols(v):
        return v.reshape(-1, P).T

    W = {k: np.ascontiguousarray(a["L0_attn_a_" + k[10:]]) for k in
         ("L0_attn_a_W_in", "L0_attn_a_W_out", "L0_attn_a_W_dt", "L0_attn_a_W_xproj", "L0_attn_a_A_log")}
    conv = a["L0_attn_a_conv_w"][:, 0, :]
    W["mamba_vectors"] = np.ascontiguousarray(np.stack(
        [cols(conv[:, t]) for t in range(4)]
        + [cols(a["L0_attn_a_" + n]) for n in ("conv_b", "b_dt", "D", "D")], axis=-1))
    W["mamba_ln"] = np.ascontiguousarray(np.stack([cols(a["L0_attn_a_ln_g"]), cols(a["L0_attn_a_ln_b"])], axis=-1))
    W["const_identity"] = np.eye(P, dtype=np.float32)
    sel = np.zeros((96, 32, P), np.float32)
    for j in range(32):
        sel[[j, 32 + j, 64 + j], j, :] = 1
    W["const_selectors"] = sel.astype(bf16)
    iota = np.arange(P, dtype=np.float32)
    W["const_iota"] = np.tile(iota, (P, 1))
    W["const_before"] = (iota[:, None] < iota[None, :]).astype(bf16)
    W["const_ones"] = np.ones((P, P), bf16)
    W["L0_router_T"] = np.ascontiguousarray(a["L0_ffn_W_router"].T)
    W["L0_router_bias"] = np.ascontiguousarray(np.broadcast_to(a["L0_ffn_b_router"], (P, 8)))
    for k in ("k", "v", "r", "cr", "ck", "cv"):
        W[f"rwkv_W{k}_T"] = np.ascontiguousarray(a["L0_attn_b_W" + k].T)
    W["rwkv_vectors"] = np.ascontiguousarray(np.stack([cols(a["L0_attn_b_" + n]) for n in (
        "w", "u", "rk", "rv", "rr", "crk", "crr", "ln1_g", "ln1_b", "ln2_g", "ln2_b", "w")], axis=-1))
    W["ssm_vectors"] = np.ascontiguousarray(np.stack([cols(a["L1_attn_a_b_delta"]), cols(a["L1_attn_a_D_param"])], axis=-1))
    W["L1_norm_w"] = np.ascontiguousarray(np.broadcast_to(a["L1_attn_a_norm_w"], (P, D)))
    W["L1_inner_gain"] = np.ascontiguousarray(a["L1_attn_a_wn_exp"].reshape(4, 4, P).transpose(2, 0, 1))
    for k in ("W_delta", "W_router", "W_B", "W_C", "A_log", "Wg", "Wu", "Wd"):
        W["L1_attn_a_" + k] = a["L1_attn_a_" + k]
    for k in ("Wr", "Wg", "Wu", "Wd", "Sg", "Su", "Sd"):
        W["L1_ffn_" + k] = a["L1_ffn_" + k]
    at = {k[10:]: v for k, v in a.items() if k.startswith("L1_attn_b_")}
    for k in ("wq", "wkv", "wqr", "wkr", "wqc", "wkc", "wv", "wo"):
        W["attn_" + k] = at[k]
    turn = lambda v: np.concatenate([v[..., P // 2:], v[..., :P // 2]], axis=-1)
    W["attn_wqr_turned"], W["attn_wkr_turned"] = (np.ascontiguousarray(turn(at[k])) for k in ("wqr", "wkr"))
    W["attn_b64"] = np.ascontiguousarray(np.stack([at["bq"], at["bkv"]], axis=-1))
    W["attn_b128"] = np.ascontiguousarray(np.stack(
        [at["bqc"], at["bkc"], at["bqr"], turn(at["bqr"]), at["bkr"], turn(at["bkr"])], axis=-1))
    for k in ("bv", "bo"):
        W["attn_" + k] = np.ascontiguousarray(np.broadcast_to(at[k], (P, D)))
    inv_freq = (1.0 / np.float32(10000.0) ** (np.arange(0, P, 2, dtype=np.float32) / np.float32(P))).astype(np.float32)
    freqs = np.arange(L, dtype=np.float32)[:, None] * inv_freq[None, :]
    W["const_cos"] = np.ascontiguousarray(np.cos(np.concatenate([freqs, freqs], -1)).T.astype(np.float32))
    W["const_sin"] = np.ascontiguousarray(np.sin(np.concatenate([-freqs, freqs], -1)).T.astype(np.float32))
    W["const_ident_bf"] = np.eye(P).astype(bf16)
    above = iota[:, None] < iota[None, :]
    W["const_mask_qk"] = np.where(above, -1e30, 0).astype(bf16)
    W["const_mask_kq"] = np.where(above.T, -1e30, 0).astype(bf16)
    for k in ("L0_ffn_experts_inter", "L0_ffn_experts_out"):
        W[k] = a[k]
    return x, W


def kernel(**inputs):
    import concourse.bacc as _bacc
    from concourse.bass_utils import run_bass_kernel_spmd as _run

    nc = _bacc.Bacc("TRN2", target_bir_lowering=False, num_devices=1)
    x, W = prepare(inputs)
    arrays = {"in_x": x, **{"in_" + k: np.ascontiguousarray(v) for k, v in W.items()}}
    aps = {k: nc.dram_tensor(k, v.shape, mybir.dt.from_np(v.dtype), kind="ExternalInput").ap()
           for k, v in arrays.items()}
    out = nc.dram_tensor("out_x", (T_ALL, D), F32, kind="ExternalOutput").ap()
    build_program(nc, {k: aps["in_" + k] for k in W}, aps["in_x"], out, ORDER)
    r = _run(nc, [arrays], core_ids=[0])
    return r.results[0]["out_x"].reshape(NB, L, D)
```

```python
import itertools
from contextlib import ExitStack

import numpy as np
import concourse.bass as bass
from concourse import mybir

F32, BF16, I32 = mybir.dt.float32, mybir.dt.bfloat16, mybir.dt.int32
ACT, ALU, AX = mybir.ActivationFunctionType, mybir.AluOpType, mybir.AxisListType

P = 128
NB, L, D = 4, 1024, 256
T_ALL = NB * L
NT = T_ALL // P
DT = D // P
CH = 512
NC = T_ALL // CH
TPC = CH // P
CPB = L // CH
LN_EPS = 1e-5
BAR_B_MAX, H_MAX = 10.0, 10000.0


class Engine:

    def __init__(self, eng, name, stack, nc):
        self.e, self.n, self.seen = eng, 0, {}
        self.sem = stack.enter_context(nc.semaphore("done_" + name))

    def did(self, inst):
        self.n += 1
        inst.then_inc(self.sem, 1)
        return (self.sem, self.n)

    def wait(self, *marks):
        for m in marks:
            if m is None:
                continue
            if type(m) is list:
                self.wait(*m)
                continue
            sem, value = m
            if self.seen.get(sem.name, 0) < value:
                self.e.wait_ge(sem, value)
                self.seen[sem.name] = value

    def own(self):
        return (self.sem, self.n)


class Core:
    def __init__(self, nc, stack):
        self.nc, self.stack = nc, stack
        self.V = Engine(nc.vector, "vector", stack, nc)
        self.S = Engine(nc.scalar, "scalar", stack, nc)
        self.G = Engine(nc.gpsimd, "gpsimd", stack, nc)
        self.T = Engine(nc.tensor, "tensor", stack, nc)
        self.Q = Engine(nc.sync, "sync", stack, nc)
        self.streams, self.stage = {}, 0
        self.chunk_marks = [None] * NC
        self.owed = self.pending = self.kept = None

    def dma(self, queue, out, in_, stream):
        return self.count(queue.e.dma_start(out, in_), stream)

    def count(self, inst, stream):
        if stream not in self.streams:
            self.streams[stream] = [self.stack.enter_context(self.nc.semaphore("dma_" + stream)), 0]
        s = self.streams[stream]
        s[1] += 16
        inst.then_inc(s[0], 16)
        return (s[0], s[1])

    def x_ready(self, c):
        if self.pending is not None:
            self.chunk_marks[c] = self.pending.through(TPC * (c + 1))
        return self.chunk_marks[c]

    def prefetch(self, n=1):
        if self.pending is not None:
            self.pending.prefetch(n)

    def x_is_ready(self):
        self.chunk_marks, self.pending = [self.V.own()] * NC, None

    def start_combine(self, M, ring=TPC):
        if self.owed is not None:
            self.pending, self.owed = self.owed(self, M, ring), None

    def barrier(self):
        marks = [e.own() for e in (self.V, self.S, self.G, self.T) if e.n]
        marks += [(s[0], s[1]) for s in self.streams.values()]
        for e in (self.V, self.S, self.G, self.T, self.Q):
            e.wait(*marks)


class Memory:

    def __init__(self, K):
        self.K, self.stack = K, ExitStack()
        K.stage += 1
        self.tag = f"s{K.stage}_"

    def sb(self, name, shape, dt=F32):
        return self.stack.enter_context(self.K.nc.sbuf_tensor(self.tag + name, shape, dt))

    def ps(self, name, shape, dt=F32):
        return self.stack.enter_context(self.K.nc.psum_tensor(self.tag + name, shape, dt))

    def free(self):
        self.K.barrier()
        self.stack.close()


def mid(ap, n):
    p, c = ap.shape
    return ap.unsqueeze(1).to_broadcast([p, n, c])


def last(ap, n):
    p, a = ap.shape
    return ap.unsqueeze(2).to_broadcast([p, a, n])


def layernorm_stats(K, M, src, n, wait, eps=LN_EPS):
    V, G = K.V, K.G
    st, mv, ve, rs = M.ln
    V.wait(wait)
    for i in range(n):
        V.did(V.e.bn_stats(st[:, i, :], src[:, i, :]))
    V.wait(V.own())
    for i in range(n):
        V.did(V.e.bn_aggr(mv[:, i, :], st[:, i, :]))
    V.wait(V.own())
    G.wait(V.did(V.e.tensor_scalar(ve[:, 0:n], mv[:, 0:n, 1], eps, None, ALU.add)))
    return G.did(G.e.tensor_tensor(rs[:, 0:n], ve[:, 0:n], K.neghalf[:, 0:n], ALU.pow))


def layernorm_apply(K, M, src, dst, n, stats):
    V = K.V
    st, mv, ve, rs = M.ln
    V.wait(stats)
    for i in range(n):
        V.did(V.e.tensor_scalar(dst[:, i, :], src[:, i, :], mv[:, i, 0:1], rs[:, i:i + 1],
                                ALU.subtract, ALU.mult))
    return V.own()


def layernorm_tiles(K, M, src, dst, n, wait):
    return layernorm_apply(K, M, src, dst, n, layernorm_stats(K, M, src, n, wait))


class Statistics:

    def __init__(self, M, i):
        self.ln = (M.sb(f"ln_stats{i}", [P, TPC, 6]), M.sb(f"ln_meanvar{i}", [P, TPC, 2]),
                   M.sb(f"ln_vareps{i}", [P, TPC]), M.sb(f"ln_rstd{i}", [P, TPC]))


def ln_buffers(M, n):
    M.ln = (M.sb("ln_stats", [P, n, 6]), M.sb("ln_meanvar", [P, n, 2]),
            M.sb("ln_vareps", [P, n]), M.sb("ln_rstd", [P, n]))


class Bank:

    def __init__(self, ap):
        self.ap, self.free = ap, None


def rotation(banks):
    turns = itertools.cycle(banks)
    return lambda: next(turns)


class Scan:
    AHEAD, RING = 2, 3

    def __init__(self, K, M, nd, ns):
        self.K, self.M, self.nd, self.ns = K, M, nd, ns
        self.dA = [M.sb(f"dA{i}", [P, nd, CH]) for i in range(self.RING)]
        self.dBu = [M.sb(f"dBu{i}", [P, nd, CH]) for i in range(self.RING)]
        self.Bb = [M.sb(f"Bb{i}", [P, CH]) for i in range(self.RING)]
        self.carry = M.sb("carry", [P, ns, nd])
        self.Bps = M.ps("B_rows", [P, CH])
        self.Cps = M.ps("C_rows", [P, CH])
        self.y = [M.ps(f"y_sum{i}", [P, CH]) for i in range(nd)]
        self.b_copied = self.y_free = None
        self.dbu_done, self.decayed, self.scanned, self.c_made, self.weighed, self.summed, self.b_marks = {}, {}, {}, {}, {}, {}, {}

    def rows_b(self, g, BC3, sel, ready):
        n, r, S, T = g % self.ns, g % self.RING, self.K.S, self.K.T
        T.wait(ready, self.b_copied)
        b_made = T.did(T.e.matmul(self.Bps[:], sel[:, n, :], BC3, start=True, stop=True))
        before = g - self.RING
        S.wait(b_made, self.dbu_done.get(before), self.scanned.get(before))
        self.b_copied = self.b_marks[g] = S.did(S.e.activation(self.Bb[r][:], self.Bps[:], ACT.Copy))

    def inputs(self, g, dt, dtu, A, ready):
        nd, n, r, S, G = self.nd, g % self.ns, g % self.RING, self.K.S, self.K.G
        before = g - self.RING
        S.wait(ready, self.scanned.get(before))
        for d in range(nd):
            S.did(S.e.activation(self.dA[r][:, d, :], dt[:, d, :], ACT.Exp, scale=A[:, d, n:n + 1]))
        self.decayed[g] = S.own()
        G.wait(ready, self.b_marks[g], self.summed.get(before))
        self.dbu_done[g] = G.did(G.e.tensor_tensor(self.dBu[r][:], dtu, mid(self.Bb[r][:], nd), ALU.mult))

    def rows_c(self, g, BC3, sel, ready):
        T, n = self.K.T, g % self.ns
        T.wait(ready, self.weighed.get(g - 1))
        self.c_made[g] = T.did(T.e.matmul(self.Cps[:], sel[:, 16 + n, :], BC3, start=True, stop=True))

    def scan(self, g, general=None):
        nd, V = self.nd, self.K.V
        c, n, r = g // self.ns, g % self.ns, g % self.RING
        V.wait(self.decayed[g], self.dbu_done[g])
        for d in range(nd):
            V.did(V.e.tensor_tensor_scan(
                self.dBu[r][:, d, :], self.dA[r][:, d, :], self.dBu[r][:, d, :],
                0.0 if c % CPB == 0 else self.carry[:, n, d:d + 1], ALU.mult, ALU.add))
        if general is not None:
            general(self, r, n, c)
        self.scanned[g] = V.own()

    def weigh(self, g):
        nd, V, n, r = self.nd, self.K.V, g % self.ns, g % self.RING
        V.wait(self.scanned[g])
        V.did(V.e.tensor_copy(self.carry[:, n, :], self.dBu[r][:, :, CH - 1]))
        V.wait(self.c_made[g], V.own())
        self.weighed[g] = V.did(V.e.tensor_tensor(
            self.dBu[r][:], self.dBu[r][:], mid(self.Cps[:], nd), ALU.mult))

    def total(self, g):
        T, n, r = self.K.T, g % self.ns, g % self.RING
        T.wait(self.weighed[g])
        if n == 0:
            T.wait(self.y_free)
        for d in range(self.nd):
            T.did(T.e.matmul(self.y[d][:], self.K.ident[:], self.dBu[r][:, d, :],
                             start=n == 0, stop=n == self.ns - 1))
        self.summed[g] = T.own()


def run_scan(sc, front, take_y, back, operands, general=None):
    n_side = sum(1 for _ in front(0))
    last_side = sc.ns - 1 - sc.AHEAD
    n_total = NC * sc.ns

    def rows_b(g):
        dt, dtu, BC3, A, sel, ready = operands(g // sc.ns)
        sc.rows_b(g, BC3, sel, ready)

    def rows_c(g):
        dt, dtu, BC3, A, sel, ready = operands(g // sc.ns)
        sc.rows_c(g, BC3, sel, ready)

    def inputs(g):
        dt, dtu, BC3, A, sel, ready = operands(g // sc.ns)
        sc.inputs(g, dt, dtu, A, ready)

    for g in range(sc.AHEAD):
        rows_b(g)
        inputs(g)
    rows_c(0)
    for c in range(NC):
        side = itertools.chain(back(c - 1) if c else (), front(c + 1) if c + 1 < NC else ())
        pairs = -(-(n_side + 6) // 2)
        for n in range(sc.ns):
            g = c * sc.ns + n
            left = last_side + 1 - n
            take = -(-pairs // left) if left > 0 and n else 0
            pairs -= take
            if left == 0:
                for _ in side:
                    pass
            ahead = g + sc.AHEAD < n_total
            if ahead:
                rows_b(g + sc.AHEAD)
            if take:
                next(side, None)
            sc.scan(g, general)
            sc.weigh(g)
            if take > 1:
                next(side, None)
                next(side, None)
            if g + 1 < n_total:
                rows_c(g + 1)
            if n == 0 and c:
                take_y(c - 1)
            sc.total(g)
            for _ in range(1 + 2 * max(0, take - 2) if take else 0):
                next(side, None)
            if ahead:
                inputs(g + sc.AHEAD)
    take_y(NC - 1)
    for _ in back(NC - 1):
        pass


def split3(K, src, dst, rest, ready):
    V = K.V
    V.wait(ready)
    V.wait(V.did(V.e.tensor_copy(dst[0:96, :], src[0:96, :])))
    V.did(V.e.tensor_tensor(rest[32:64, :], src[32:64, :], dst[32:64, :], ALU.subtract))
    V.wait(V.did(V.e.tensor_tensor(rest[64:96, :], src[64:96, :], dst[64:96, :], ALU.subtract)))
    V.did(V.e.tensor_copy(dst[32:64, :], rest[32:64, :]))
    V.wait(V.did(V.e.tensor_copy(dst[64:96, :], rest[64:96, :])))
    V.wait(V.did(V.e.tensor_tensor(rest[64:96, :], rest[64:96, :], dst[64:96, :], ALU.subtract)))
    return V.did(V.e.tensor_copy(dst[64:96, :], rest[64:96, :]))


def mamba_stage(K, W):
    V, S, G, T, Q = K.V, K.S, K.G, K.T, K.Q
    X = K.X
    DI, NS, R = 512, 16, 16
    ND = DI // P
    M = Memory(K)
    ln_buffers(M, TPC)
    w_in = M.sb("w_in", [P, DT, 2 * DI])
    w_bc = M.sb("w_bc", [P, ND, 3, 2 * NS])
    w_dtr = M.sb("w_dtr", [P, ND, R])
    w_dt = M.sb("w_dt", [R, DI])
    w_out = M.sb("w_out", [P, ND, D])
    vec = M.sb("mamba_vectors", [P, ND, 8])
    lnv = M.sb("mamba_ln", [P, DT, 2])
    A = M.sb("A", [P, ND, NS])
    sel = M.sb("selectors", [96, 32, P], BF16)
    loads = [
        K.dma(Q, w_in[:], W["L0_attn_a_W_in"].rearrange("(k p) e -> p k e", p=P), "weights"),
        K.dma(Q, w_out[:], W["L0_attn_a_W_out"].rearrange("(k p) e -> p k e", p=P), "weights"),
        K.dma(Q, w_dt[:], W["L0_attn_a_W_dt"], "weights"),
        K.dma(Q, w_dtr[:], W["L0_attn_a_W_xproj"].rearrange("(k p) e -> p k e", p=P)[:, :, 0:R], "weights"),
        K.dma(Q, vec[:], W["mamba_vectors"], "weights"),
        K.dma(Q, lnv[:], W["mamba_ln"], "weights"),
        K.dma(Q, A[:], W["L0_attn_a_A_log"].rearrange("(k p) n -> p k n", p=P), "weights"),
        K.dma(Q, sel[:], W["const_selectors"], "weights"),
    ]
    for j in range(3):
        loads.append(K.dma(Q, w_bc[:, :, j, :], W["L0_attn_a_W_xproj"].rearrange("(k p) e -> p k e", p=P)[:, :, R:], "weights"))
    loaded = loads[-1]
    zero_rows(K, [loaded] + K.chunk_marks)
    S.wait(loaded)
    S.wait(S.did(S.e.activation(A[:], A[:], ACT.Exp)))
    V.wait(S.own())
    a_ready = V.did(V.e.tensor_scalar(A[:], A[:], -1.0, None, ALU.mult))
    for e in (V, S, G, T):
        e.wait(loaded, a_ready)

    sc = Scan(K, M, ND, NS)
    xn = M.sb("xn", [P, TPC, D])
    hT = M.sb("hT", [P, DT, CH])
    uraw = M.sb("uraw", [P, ND, 3 + CH])
    cv = M.sb("conv", [P, ND, CH])
    zs = [M.sb(f"z{i}", [P, ND, CH]) for i in range(2)]
    u = [M.sb(f"u{i}", [P, ND, CH]) for i in range(2)]
    dt = [M.sb(f"dt{i}", [P, ND, CH]) for i in range(2)]
    dtu = [M.sb(f"dtu{i}", [P, ND, CH]) for i in range(2)]
    BC3 = [M.sb(f"BC3_{i}", [96, CH], BF16) for i in range(2)]
    rest = M.sb("bc_rest", [96, CH])
    dtr = M.sb("dt_rank", [R, CH])
    pick = rotation([Bank(M.ps(f"front{i}", [P, CH])) for i in range(2)])
    st = {"chunk_done": [None, None], "hT_free": None, "ready": [None, None],
          "hist": None, "u_free": None}

    def front(c):
        r = c % 2
        x4 = X[:, TPC * c:TPC * (c + 1), :]
        yield
        stats = layernorm_stats(K, M, x4, TPC, K.x_ready(c))
        yield
        yield
        V.wait(st["hT_free"])
        normed = layernorm_apply(K, M, x4, xn, TPC, stats)
        stats = layernorm_stats(K, M, xn, TPC, normed)
        K.x_written[c] = added = V.did(V.e.tensor_tensor(x4, x4, xn[:], ALU.add))
        yield
        yield
        h_ready = layernorm_apply(K, M, xn, xn, TPC, [stats, added])
        yield
        for k in range(DT):
            f = pick()
            T.wait(h_ready, f.free)
            for i in range(TPC):
                T.did(T.e.transpose(f.ap[:, i * P:(i + 1) * P], xn[:, i, k * P:(k + 1) * P], K.ident[:]))
            made = T.own()
            yield
            S.wait(made, st["hT_free"])
            f.free = hT_ready = S.did(S.e.activation(hT[:, k, :], f.ap[:], ACT.Identity,
                                                     bias=lnv[:, k, 1:2], scale=lnv[:, k, 0:1]))
            yield
        V.wait(st["hist"])
        if c % CPB:
            hist = V.did(V.e.tensor_copy(uraw[:, :, 0:3], uraw[:, :, CH:CH + 3]))
        else:
            hist = V.did(V.e.memset(uraw[:, :, 0:3], 0.0))
        for step in range(2 * ND):
            d, is_z = step // 2, step % 2
            e = d + ND * is_z
            f = pick()
            T.wait(hT_ready, f.free)
            for k in range(DT):
                T.did(T.e.matmul(f.ap[:], w_in[:, k, e * P:(e + 1) * P], hT[:, k, :],
                                 start=k == 0, stop=k == DT - 1))
            made = T.own()
            yield
            S.wait(made, hist, st["chunk_done"][r])
            f.free = S.did(S.e.activation(zs[r][:, d, :] if is_z else uraw[:, d, 3:3 + CH], f.ap[:], ACT.Copy))
            if not is_z:
                S.wait(f.free, st["u_free"])
                tapped = S.did(S.e.activation(cv[:, d, :], uraw[:, d, 0:CH], ACT.Identity,
                                              bias=vec[:, d, 4:5], scale=vec[:, d, 0:1]))
                yield
                continue
            V.wait(tapped)
            for t in range(1, 4):
                V.wait(V.did(V.e.scalar_tensor_tensor(cv[:, d, :], uraw[:, d, t:t + CH], vec[:, d, t:t + 1],
                                                      cv[:, d, :], ALU.mult, ALU.add)))
            yield
        st["hT_free"] = T.own()
        st["hist"] = V.own()
        S.wait(st["hist"], S.own())
        S.did(S.e.activation(u[r][:], cv[:], ACT.Silu))
        S.did(S.e.activation(zs[r][:], zs[r][:], ACT.Silu))
        st["u_free"] = S.own()
        for _ in range(4):
            yield
        f = pick()
        T.wait(st["u_free"], f.free)
        for k in range(ND):
            T.did(T.e.matmul(f.ap[0:96, :], w_bc[:, k, :, :].rearrange("p a b -> p (a b)"), u[r][:, k, :],
                             start=k == 0, stop=k == ND - 1))
        made = T.own()
        yield
        split_done = f.free = split3(K, f.ap, BC3[r], rest, [made, st["chunk_done"][r]])
        yield
        f = pick()
        T.wait(f.free)
        for k in range(ND):
            T.did(T.e.matmul(f.ap[0:R, :], w_dtr[:, k, :], u[r][:, k, :], start=k == 0, stop=k == ND - 1))
        made = T.own()
        yield
        S.wait(made)
        f.free = rank_ready = S.did(S.e.activation(dtr[:], f.ap[0:R, :], ACT.Copy))
        yield
        ab = cv
        for d in range(ND):
            f = pick()
            T.wait(f.free, rank_ready)
            T.did(T.e.matmul(f.ap[:], w_dt[:, d * P:(d + 1) * P], dtr[:], start=True, stop=True))
            made = T.own()
            yield
            S.wait(made, st["u_free"])
            absolute = S.did(S.e.activation(ab[:, d, :], f.ap[:], ACT.Abs, bias=vec[:, d, 5:6]))
            V.wait(absolute)
            relu = V.did(V.e.tensor_scalar(dt[r][:, d, :], f.ap[:], vec[:, d, 5:6], 0.0, ALU.add, ALU.max))
            f.free = [absolute, relu]
            yield
        S.wait(S.own())
        S.wait(S.did(S.e.activation(ab[:], ab[:], ACT.Exp, scale=-1.0)))
        S.did(S.e.activation(ab[:], ab[:], ACT.Ln, bias=1.0))
        yield
        yield
        V.wait(S.own(), V.own())
        made = V.did(V.e.tensor_tensor(dt[r][:], dt[r][:], ab[:], ALU.add))
        st["u_free"] = made
        G.wait(made)
        st["ready"][r] = [G.did(G.e.tensor_tensor(dtu[r][:], dt[r][:], u[r][:], ALU.mult)), made, split_done]
        yield

    def take_y(c):
        r = c % 2
        V.wait(sc.summed[(c + 1) * NS - 1])
        for d in range(ND):
            V.did(V.e.scalar_tensor_tensor(u[r][:, d, :], u[r][:, d, :], vec[:, d, 6:7], sc.y[d][:],
                                           ALU.mult, ALU.add))
        sc.y_free = V.own()

    def back(c):
        r = c % 2
        yield
        V.wait(sc.y_free)
        gated = V.did(V.e.tensor_tensor(u[r][:], u[r][:], zs[r][:], ALU.mult))
        yield
        for i in range(0, TPC, 2):
            f = pick()
            T.wait(f.free, gated)
            for j in range(2):
                for k in range(ND):
                    T.did(T.e.matmul(f.ap[:, j * D:(j + 1) * D], u[r][:, k, (i + j) * P:(i + j + 1) * P],
                                     w_out[:, k, :], start=k == 0, stop=k == ND - 1))
            made = T.own()
            yield
            xt = X[:, TPC * c + i:TPC * c + i + 2, :]
            V.wait(made, K.x_written[c])
            f.free = V.did(V.e.tensor_tensor(xt, xt, f.ap[:].rearrange("p (a b) -> p a b", a=2), ALU.add))
            yield
        st["chunk_done"][r] = [T.own(), V.own()]

    K.x_written = [None] * NC
    run_scan(sc, front, take_y, back, lambda c: (dt[c % 2], dtu[c % 2][:], BC3[c % 2][:], A, sel, st["ready"][c % 2]))
    K.x_is_ready()
    M.free()



SLOT_TILES = 80
SLOTS = SLOT_TILES * P
ZERO_ROW = SLOTS
DROPPED = 1 << 20


def channel_major(K, xn, xT, bank, ready, free):
    S, T = K.S, K.T
    marks = []
    for k in range(DT):
        f = bank()
        T.wait(ready, f.free)
        for i in range(TPC):
            T.did(T.e.transpose(f.ap[:, i * P:(i + 1) * P], xn[:, i, k * P:(k + 1) * P], K.ident[:]))
        S.wait(T.own(), free)
        f.free = S.did(S.e.activation(xT[:, k, :], f.ap[:], ACT.Copy))
        marks.append(f.free)
    return marks


class Routing:

    def __init__(self, K, M, E, capacity=None, parts=1):
        self.K, self.M, self.E, self.cap, self.per = K, M, E, capacity, NT // parts
        self.logits = [M.ps(f"logits{i}", [P, self.per, E]) for i in range(parts)]
        n = [P, self.per, E]
        self.p, self.a, self.b = M.sb("probs", n), M.sb("route_a", n), M.sb("route_b", n)
        self.oh = [M.sb(f"onehot{i}", n) for i in range(2)]
        self.mask = M.sb("mask", n, BF16)
        self.tot = M.sb("totals", [P, E, self.per])
        self.cum = M.sb("cumulated", [P, E, self.per])
        self.keep = M.sb("keep", [P, E, self.per])
        self.w, self.gather_of = K.pick_weight, K.pick_row
        self.red = M.sb("route_red", [P, self.per])
        self.fl = M.sb("route_slot", [P, self.per])
        self.before = M.sb("count_before", [P, E])
        self.scatter_to = [M.sb(f"scatter_to{i}", [P, NT], I32) for i in range(2)]
        self.small = M.sb("route_small", [P, E, self.per])
        self.nt, self.end = M.sb("n_tiles", [P, E]), M.sb("end_tile", [P, E])
        self.rev = M.sb("reversed_iota", [P, E])
        self.ones = M.sb("route_ones", [P, E])
        if capacity is None:
            self.ej = M.sb("tile_compare", [P, SLOT_TILES, E], BF16)
            self.ef = M.sb("tile_expert_f", [P, SLOT_TILES])
            self.tile_expert = M.sb("tile_expert", [P, SLOT_TILES], I32)

    def logit(self, t):
        return self.logits[t // self.per][:, t % self.per, :]

    def run(self, made, part=0, bias=None, normalise=False, beside=()):
        K, E, n = self.K, self.E, self.per
        ts = slice(part * n, (part + 1) * n)
        weight = [w[:, ts] for w in self.w]
        V, S, T = K.V, K.S, K.T
        p, a, b, red, fl = self.p, self.a, self.b, self.red, self.fl
        ranks = ExitStack()
        self.within = ranks.enter_context(K.nc.psum_tensor(self.M.tag + f"rank_within_tile{part}", [P, n, E], F32))
        self.totals = ranks.enter_context(K.nc.psum_tensor(self.M.tag + f"tile_totals{part}", [P, n, E], F32))

        def v(inst):
            V.wait(V.did(inst))

        V.wait(made)
        if bias is not None:
            v(V.e.tensor_tensor(p[:], self.logits[part][:], mid(bias, n), ALU.add))
        else:
            v(V.e.tensor_copy(p[:], self.logits[part][:]))
        v(V.e.tensor_reduce(red[:], p[:], AX.X, ALU.max))
        v(V.e.tensor_tensor(p[:], p[:], last(red[:], E), ALU.subtract))
        S.wait(V.own())
        exponentials = S.did(S.e.activation(p[:], p[:], ACT.Exp))
        if beside:
            beside[0]()
        V.wait(exponentials)
        v(V.e.tensor_reduce(red[:], p[:], AX.X, ALU.add))
        v(V.e.reciprocal(red[:], red[:]))
        v(V.e.tensor_tensor(p[:], p[:], last(red[:], E), ALU.mult))
        v(V.e.tensor_scalar(self.rev[:], K.iota[:, 0:E], -1.0, float(E), ALU.mult, ALU.add))
        v(V.e.tensor_copy(a[:], p[:]))
        for i in range(2):
            v(V.e.tensor_reduce(weight[i], a[:], AX.X, ALU.max))
            v(V.e.tensor_tensor(b[:], a[:], last(weight[i], E), ALU.is_equal))
            v(V.e.tensor_tensor(b[:], b[:], mid(self.rev[:], n), ALU.mult))
            v(V.e.tensor_reduce(red[:], b[:], AX.X, ALU.max))
            v(V.e.tensor_tensor(self.oh[i][:], b[:], last(red[:], E), ALU.is_equal))
            if i == 0:
                v(V.e.scalar_tensor_tensor(a[:], self.oh[0][:], -2.0, a[:], ALU.mult, ALU.add))
        v(V.e.tensor_tensor(b[:], self.oh[0][:], self.oh[1][:], ALU.add))
        if self.cap is not None:
            v(V.e.tensor_scalar(a[:], p[:], 0.0, None, ALU.is_gt))
            v(V.e.tensor_tensor(b[:], b[:], a[:], ALU.mult))
        v(V.e.tensor_copy(self.mask[:], b[:]))
        T.wait(V.own())
        T.did(T.e.matmul(self.within[:].rearrange("p t e -> p (t e)"), K.before[:],
                         self.mask[:].rearrange("p t e -> p (t e)"), start=True, stop=True))
        T.did(T.e.matmul(self.totals[:].rearrange("p t e -> p (t e)"), K.ones_bf[:],
                         self.mask[:].rearrange("p t e -> p (t e)"), start=True, stop=True))
        V.wait(T.own())
        if beside:
            beside[1]()
        v(V.e.tensor_copy(self.tot[:], self.totals[:].rearrange("p t e -> p e t")))
        v(V.e.memset(self.keep[:], 1.0))
        v(V.e.memset(self.keep[:, :, 0], 0.0))
        flat = lambda t: t[:].rearrange("p e t -> p (e t)")
        v(V.e.tensor_tensor_scan(flat(self.cum), flat(self.keep), flat(self.tot), 0.0, ALU.mult, ALU.add))
        count = self.small
        if self.cap is None:
            v(V.e.tensor_scalar(self.keep[:], mid(K.iota[:, 0:n], E), float(P), None, ALU.mult))
            v(V.e.tensor_tensor(count[:], last(self.cum[:, :, n - 1], n), self.keep[:], ALU.is_gt))
            v(V.e.tensor_reduce(self.nt[:], count[:], AX.X, ALU.add))
            v(V.e.memset(self.ones[:], 1.0))
            v(V.e.tensor_tensor_scan(self.end[:], self.ones[:], self.nt[:], 0.0, ALU.mult, ALU.add))
            v(V.e.tensor_tensor(self.ej[:], last(K.iota[:, 0:SLOT_TILES], E), mid(self.end[:], SLOT_TILES), ALU.is_ge))
            v(V.e.tensor_reduce(self.ef[:], self.ej[:], AX.X, ALU.add))
            v(V.e.tensor_scalar(self.ef[:], self.ef[:], float(E - 1), None, ALU.min))
            v(V.e.tensor_copy(self.tile_expert[:], self.ef[:]))
            v(V.e.tensor_tensor(self.nt[:], self.end[:], self.nt[:], ALU.subtract))
            v(V.e.tensor_scalar(self.nt[:], self.nt[:], float(P), None, ALU.mult))
        else:
            v(V.e.tensor_scalar(self.nt[:], K.iota[:, 0:E], float(self.cap), None, ALU.mult))
        v(V.e.tensor_tensor(self.cum[:], self.cum[:], self.tot[:], ALU.subtract))
        if part:
            v(V.e.tensor_tensor(self.cum[:], self.cum[:], last(self.before[:], n), ALU.add))
        if ts.stop < NT:
            v(V.e.tensor_tensor(self.before[:], self.cum[:, :, n - 1], self.tot[:, :, n - 1], ALU.add))
        v(V.e.tensor_tensor(a[:], self.within[:], self.cum[:].rearrange("p e t -> p t e"), ALU.add))
        for i in range(2):
            if self.cap is not None:
                v(V.e.tensor_tensor(b[:], self.oh[i][:], a[:], ALU.mult))
                v(V.e.tensor_reduce(red[:], b[:], AX.X, ALU.add))
                v(V.e.tensor_scalar(red[:], red[:], float(self.cap), None, ALU.is_lt))
                v(V.e.tensor_scalar(fl[:], weight[i], 0.0, None, ALU.is_gt))
                v(V.e.tensor_tensor(red[:], red[:], fl[:], ALU.mult))
            v(V.e.tensor_tensor(b[:], a[:], mid(self.nt[:], n), ALU.add))
            v(V.e.tensor_tensor(b[:], b[:], self.oh[i][:], ALU.mult))
            v(V.e.tensor_reduce(fl[:], b[:], AX.X, ALU.add))
            if self.cap is not None:
                v(V.e.tensor_tensor(fl[:], fl[:], red[:], ALU.mult))
                v(V.e.tensor_scalar(red[:], red[:], -1.0, 1.0, ALU.mult, ALU.add))
                v(V.e.scalar_tensor_tensor(self.small[:, 0, :], red[:], float(DROPPED), fl[:], ALU.mult, ALU.add))
                v(V.e.tensor_copy(self.scatter_to[i][:, ts], self.small[:, 0, :]))
                v(V.e.scalar_tensor_tensor(fl[:], red[:], float(ZERO_ROW), fl[:], ALU.mult, ALU.add))
                v(V.e.tensor_copy(self.gather_of[i][:, ts], fl[:]))
            else:
                v(V.e.tensor_copy(self.scatter_to[i][:, ts], fl[:]))
                v(V.e.tensor_copy(self.gather_of[i][:, ts], fl[:]))
        if normalise:
            v(V.e.tensor_tensor(red[:], weight[0], weight[1], ALU.add))
            v(V.e.tensor_scalar(red[:], red[:], 1e-9, None, ALU.add))
            v(V.e.reciprocal(red[:], red[:]))
            for i in range(2):
                v(V.e.tensor_tensor(weight[i], weight[i], red[:], ALU.mult))
        T.wait(V.own())
        ranks.close()
        return V.own()

    def scatter(self, rows, routed, part=0):
        K, G = self.K, self.K.G
        G.wait(routed, K.sorted_read)
        for t in range(part * self.per, (part + 1) * self.per):
            for i in range(2):
                done = K.count(G.e.indirect_dma_start(
                    K.sorted_in, bass.IndirectOffsetOnAxis(ap=self.scatter_to[i][:, t:t + 1], axis=0),
                    rows[:, t, :], None, bounds_check=SLOTS - 1, oob_is_err=False), "scatter")
        return done


class Combine:

    def __init__(self, K, M, into, ring=4, eager=False):
        self.eager = eager
        self.K, self.into, self.ring, self.at = K, into, ring, 0
        self.got = [[M.sb(f"gathered{i}_{j}", [P, D]) for j in range(2)] for i in range(ring)]
        self.used, self.arrived, self.gathered = [None] * ring, {}, 0
        self.prefetch(ring)

    def prefetch(self, n):
        for t in range(self.gathered, min(self.gathered + n, self.at + self.ring, NT)):
            self.gather(t)

    def gather(self, t):
        G, s = self.K.G, t % self.ring
        self.gathered = t + 1
        G.wait(self.used[s])
        for i in range(2):
            self.arrived[t] = self.K.count(G.e.indirect_dma_start(
                self.got[s][i][:], None, self.K.sorted_out,
                bass.IndirectOffsetOnAxis(ap=self.K.pick_row[i][:, t:t + 1], axis=0),
                bounds_check=SLOTS, oob_is_err=False), f"gather{s}")

    def through(self, end, ready=None):
        V, step = self.K.V, min(self.ring // 2 if self.eager else self.ring, TPC)
        V.wait(ready)
        while self.at < end:
            tiles = range(self.at, self.at + step)
            self.prefetch(max(0, tiles.stop - self.gathered))
            for i in range(2):
                for t in tiles:
                    V.wait(self.arrived[t])
                    V.did(V.e.scalar_tensor_tensor(
                        self.into[:, t, :], self.got[t % self.ring][i][:], self.K.pick_weight[i][:, t:t + 1],
                        self.into[:, t, :], ALU.mult, ALU.add))
                V.wait(V.own())
            for t in tiles:
                self.used[t % self.ring] = V.own()
            self.at += step
            if self.eager:
                self.prefetch(step)
        return V.own()


class NormedCombine:

    def __init__(self, K, M, rows, norm_w, ring):
        self.K, self.rows, self.norm_w = K, rows, norm_w
        self.sums, self.inverse = M.sb("y_sums", [P, NT]), M.sb("y_rms", [P, NT])
        self.squares = M.sb("y_squares", [P, D], BF16)
        self.combine, self.begun, self.squared = Combine(K, M, rows, ring, eager=True), 0, {}

    def prefetch(self, n):
        self.combine.prefetch(n)

    def begin(self, c):
        S = self.K.S
        S.wait(self.combine.through(TPC * (c + 1)))
        for t in range(TPC * c, TPC * (c + 1)):
            self.squared[c] = do(S, lambda: S.e.activation(
                self.squares[:], self.rows[:, t, :], ACT.Square, accum_out=self.sums[:, t:t + 1]), S.own())
        self.begun = c + 1

    def through(self, end):
        K, V, G = self.K, self.K.V, self.K.G
        c = end // TPC - 1
        if self.begun <= c:
            self.begin(c)
        tiles = slice(TPC * c, TPC * (c + 1))
        sums, inverse, rows = self.sums[:, tiles], self.inverse[:, tiles], self.rows[:, tiles, :]
        mean = do(V, lambda: V.e.tensor_scalar(sums, sums, 1.0 / D, 1e-6, ALU.mult, ALU.add), self.squared[c])
        rooted = do(G, lambda: G.e.tensor_tensor(inverse, sums, K.neghalf[:, tiles], ALU.pow), mean)
        if c + 1 < NC:
            self.begin(c + 1)
        V.wait(do(V, lambda: V.e.tensor_tensor(rows, rows, mid(self.norm_w[:], TPC), ALU.mult)), rooted)
        for t in range(tiles.start, tiles.stop):
            V.did(V.e.scalar_tensor_tensor(K.X[:, t, :], self.rows[:, t, :], self.inverse[:, t:t + 1], K.X[:, t, :],
                                           ALU.mult, ALU.add))
        return V.own()


def moe0_stage(K, W):
    V, S, G, T, Q = K.V, K.S, K.G, K.T, K.Q
    E, I = 8, 1024
    CAP = -(-T_ALL * 5 // (4 * E))
    CT = CAP // P
    KI = I // P
    M = Memory(K)
    PARTS = 2
    CPP = NC // PARTS
    lns = [Statistics(M, i) for i in range(CPP)]
    R = Routing(K, M, E, CAP, PARTS)
    wr = M.sb("w_router", [P, DT, E])
    rb = M.sb("b_router", [P, E])
    xn = M.sb("xn", [P, NT, D])
    xT = [M.sb(f"xT{i}", [P, DT, CH]) for i in range(2)]
    tbank = [Bank(M.ps(f"transposed{i}", [P, CH])) for i in range(2)]
    w_in = [M.sb(f"w_inter{i}", [P, DT, I]) for i in range(2)]
    w_out = [M.sb(f"w_exp_out{i}", [P, KI, D]) for i in range(2)]
    rows = [M.sb(f"rows{i}", [P, CT, D]) for i in range(2)]
    K.dma(Q, wr[:], W["L0_router_T"].rearrange("(k p) e -> p k e", p=P), "weights")
    loaded = K.dma(Q, rb[:], W["L0_router_bias"], "weights")
    freed = [None, None]

    def load_expert(e):
        r = e % 2
        Q.wait(freed[r])
        K.dma(Q, w_in[r][:], W["L0_ffn_experts_inter"][e].rearrange("(k p) i -> p k i", p=P), f"expert{r}")
        return K.dma(Q, w_out[r][:], W["L0_ffn_experts_out"][e].rearrange("(k p) i -> p k i", p=P), f"expert{r}")

    expert_here = [load_expert(0), load_expert(1)]
    T.wait(loaded)
    V.wait(loaded)
    used, turn = [None, None], rotation(tbank)

    normed = {}

    def normalise(chunks):
        stats = {}
        for c in chunks:
            stats[c] = layernorm_stats(K, lns[c % CPP], K.X[:, TPC * c:TPC * (c + 1), :], TPC, K.x_ready(c))
            if c > chunks[0]:
                apply(c - 1, stats[c - 1])
        apply(c, stats[c])

    def apply(c, stats):
        tiles = slice(TPC * c, TPC * (c + 1))
        normed[c] = layernorm_apply(K, lns[c % CPP], K.X[:, tiles, :], xn[:, tiles, :], TPC, stats)

    normalise(range(CPP))
    for part in range(PARTS):
        for c in range(part * CPP, (part + 1) * CPP):
            r = c % 2
            tiles = slice(TPC * c, TPC * (c + 1))
            T.wait(channel_major(K, xn[:, tiles, :], xT[r], turn, normed[c], used[r]))
            for i in range(TPC):
                for k in range(DT):
                    T.did(T.e.matmul(R.logit(TPC * c + i), xT[r][:, k, i * P:(i + 1) * P], wr[:, k, :],
                                     start=k == 0, stop=k == DT - 1))
            used[r] = T.own()
        if part + 1 < PARTS:
            normalise(range((part + 1) * CPP, (part + 2) * CPP))
        scattered = R.scatter(xn, R.run(used[r], part, bias=rb[:]), part)

    xsT = [M.sb(f"rowsT{i}", [P, DT, CAP]) for i in range(2)]
    hT = M.sb("hidden", [P, KI, CAP])
    out = [M.sb(f"result{i}", [P, D]) for i in range(4)]
    hb = [Bank(M.ps(f"hidden_sum{i}", [P, 512])) for i in range(2)]
    for_result = rotation([Bank(M.ps(f"result_sum{i}", [P, D])) for i in range(2)])
    HALF = CAP // 2
    rows_here, rows_free, xsT_free, xsT_ready = [None, None], [None, None], [None, None], [None, None]
    out_stored = [None] * 4
    Q.wait(scattered)

    def load_rows(e):
        r = e % 2
        Q.wait(rows_free[r])
        rows_here[r] = K.dma(Q, rows[r][:], K.sorted_in[e * CAP:(e + 1) * CAP, :].rearrange("(t p) c -> p t c", p=P), f"rows{r}")

    def transpose_rows(e):
        r = e % 2
        T.wait(rows_here[r])
        for t in range(CT):
            b = tbank[t % 2]
            T.wait(b.free)
            for k in range(DT):
                T.did(T.e.transpose(b.ap[:, k * P:(k + 1) * P], rows[r][:, t, k * P:(k + 1) * P], K.ident[:]))
            S.wait(T.own(), xsT_free[r])
            b.free = S.did(S.e.activation(xsT[r][:, :, t * P:(t + 1) * P],
                                          b.ap[:, 0:DT * P].rearrange("p (k q) -> p k q", k=DT), ACT.Copy))
        rows_free[r] = T.own()
        xsT_ready[r] = S.own()

    load_rows(0)
    load_rows(1)
    transpose_rows(0)
    h_free, n_out, stored = None, 0, None
    for e in range(E):
        r = e % 2
        T.wait(xsT_ready[r], expert_here[r])
        for i in range(KI):
            for half in range(2):
                b = hb[half]
                T.wait(b.free)
                for k in range(DT):
                    T.did(T.e.matmul(b.ap[:, 0:HALF], w_in[r][:, k, i * P:(i + 1) * P],
                                     xsT[r][:, k, half * HALF:(half + 1) * HALF], start=k == 0, stop=k == DT - 1))
                to = hT[:, i, half * HALF:(half + 1) * HALF]
                if half:
                    S.wait(T.own(), h_free)
                    b.free = S.did(S.e.activation(to, b.ap[:, 0:HALF], ACT.Relu))
                else:
                    V.wait(T.own(), h_free)
                    b.free = V.did(V.e.tensor_scalar(to, b.ap[:, 0:HALF], 0.0, None, ALU.max))
        xsT_free[r] = T.own()
        h_ready = [S.own(), V.own()]
        if e + 1 < E:
            transpose_rows(e + 1)
            if e + 2 < E:
                load_rows(e + 2)
        T.wait(h_ready)
        for t in range(CT):
            ob = for_result()
            T.wait(ob.free)
            for i in range(KI):
                T.did(T.e.matmul(ob.ap[:], hT[:, i, t * P:(t + 1) * P], w_out[r][:, i, :],
                                 start=i == 0, stop=i == KI - 1))
            T_mark = T.own()
            V.wait(T_mark, out_stored[n_out % 4])
            ob.free = V.did(V.e.tensor_copy(out[n_out % 4][:], ob.ap[:]))
            S.wait(ob.free)
            row = (e * CT + t) * P
            out_stored[n_out % 4] = stored = K.dma(S, K.sorted_out[row:row + P, :], out[n_out % 4][:], f"store{n_out % 4}")
            n_out += 1
        h_free = T.own()
        freed[r] = T.own()
        if e + 2 < E:
            expert_here[r] = load_expert(e + 2)
    K.sorted_read = [rows_here[0], rows_here[1]]
    K.owed = lambda K, M, ring: Combine(K, M, K.X, ring)
    M.free()


def do(E, issue, *marks):
    E.wait(*marks)
    return E.did(issue())


def run_lanes(chunk, n, skew, lanes=2):
    active, started, since = [], 0, skew
    while active or started < n:
        if started < n and len(active) < lanes and since >= skew:
            active.append(chunk(started))
            started += 1
            since = 0
        since += 1
        for g in list(active):
            if next(g, "end") == "end":
                active.remove(g)


class Lane:

    def __init__(self, ln, xn, hh, xa, mx, pp, aa, m0, k, v, sr, kw, ea, eb, rr, d1, scr):
        self.ln, self.done = ln, None
        self.xn, self.hh, self.xa, self.mx, self.pp, self.aa, self.m0 = xn, hh, xa, mx, pp, aa, m0
        self.k, self.v, self.sr, self.kw, self.ea, self.eb, self.rr = k, v, sr, kw, ea, eb, rr
        self.d1, self.scr = d1, scr


def rwkv_stage(K, W):
    V, S, G, T, Q = K.V, K.S, K.G, K.T, K.Q
    X = K.X
    HID = 4 * D
    KH = HID // P
    NEG = -1e38
    M = Memory(K)
    K.start_combine(M)
    w = {n: M.sb("w_" + n, [P, DT, D]) for n in ("k", "v", "r", "cr")}
    for n in w:
        K.dma(Q, w[n][:], W[f"rwkv_W{n}_T"].rearrange("(k p) d -> p k d", p=P), "weights")
    w_ck = M.sb("w_ck", [P, DT, HID])
    w_cv = M.sb("w_cv", [P, KH, D])
    vec = M.sb("rwkv_vectors", [P, DT, 12])
    K.dma(Q, w_ck[:], W["rwkv_Wck_T"].rearrange("(k p) d -> p k d", p=P), "weights")
    K.dma(Q, w_cv[:], W["rwkv_Wcv_T"].rearrange("(k p) d -> p k d", p=P), "weights")
    loaded = K.dma(Q, vec[:], W["rwkv_vectors"], "weights")
    for e in (V, S, G, T):
        e.wait(loaded)
    WD, U, G1, B1, G2, B2 = 0, 1, 7, 8, 9, 10
    MIX = {"k": 2, "v": 3, "r": 4, "ck": 5, "cr": 6}
    omr = M.sb("one_minus_mix", [P, DT, 12])
    nu = M.sb("minus_u", [P, DT])
    V.did(V.e.tensor_scalar(omr[:], vec[:], -1.0, 1.0, ALU.mult, ALU.add))
    prep = V.did(V.e.tensor_scalar(nu[:], vec[:, :, U], -1.0, None, ALU.mult))
    for e in (V, S, G):
        e.wait(prep)

    def lane(i):
        shapes = {n: [P, TPC, D] for n in ("xn", "hh")}
        shapes.update({n: [P, DT, 1 + CH] for n in ("xa", "mx", "pp", "aa")})
        shapes.update({n: [P, DT, CH] for n in ("m0", "k", "v", "sr", "kw", "ea", "eb", "rr", "d1")})
        shapes["scr"] = [P, 2, D]
        ln = tuple(M.sb(f"l{i}_{n}", sh) for n, sh in (("st", [P, TPC, 6]), ("mv", [P, TPC, 2]),
                                                       ("ve", [P, TPC]), ("rs", [P, TPC])))
        return Lane(ln, **{n: M.sb(f"l{i}_{n}", sh) for n, sh in shapes.items()})

    lanes = [lane(i) for i in range(2)]
    kc, kc_free = M.sb("kc", [P, KH, CH]), [None]
    banks = [Bank(M.ps(f"bank{i}", [P, CH])) for i in range(8)]
    for_transposes, for_products, for_output = rotation(banks[0:2]), rotation(banks[2:6]), rotation(banks[6:8])

    def to_channels(src, dst, gain, bias, ready, free):
        marks = []
        for k in range(DT):
            f = for_transposes()
            T.wait(ready, f.free)
            for i in range(TPC):
                T.did(T.e.transpose(f.ap[:, i * P:(i + 1) * P], src[:, i, k * P:(k + 1) * P], K.ident[:]))
            f.free = do(S, lambda: S.e.activation(dst[:, k, 1:], f.ap[:], ACT.Identity,
                                                  bias=vec[:, k, bias:bias + 1], scale=vec[:, k, gain:gain + 1]),
                        T.own(), free)
            marks.append(f.free)
        return marks

    def mix_before(xa, dst, kind, ready, free):
        m = MIX[kind]
        for k in range(DT):
            mark = do(S, lambda: S.e.activation(dst[:, k, :], xa[:, k, 0:CH], ACT.Copy, scale=omr[:, k, m:m + 1]),
                      ready, free)
        return mark

    def mix_now(xa, dst, kind, ready):
        m = MIX[kind]
        for k in range(DT):
            mark = do(V, lambda: V.e.scalar_tensor_tensor(
                dst[:, k, :], xa[:, k, 1:], vec[:, k, m:m + 1], dst[:, k, :], ALU.mult, ALU.add), ready)
        return mark

    prev = {}
    carry = {n: [M.sb(f"carry_{n}{i}", [P, DT, 1]) for i in range(2)] for n in ("xa", "mx", "rr", "pp", "aa", "xb")}

    def start_column(name, buf, c, value, free=None):
        if c % CPB == 0:
            return do(V, lambda: V.e.memset(buf[:, :, 0:1], value), free)
        return do(V, lambda: V.e.tensor_copy(buf[:, :, 0:1], carry[name][(c - 1) % 2][:]), prev[name], free)

    def save_column(name, ap, c, ready):
        prev[name] = do(V, lambda: V.e.tensor_copy(carry[name][c % 2][:], ap), ready)

    def chunk(c):
        b = lanes[c % 2]
        x4 = X[:, TPC * c:TPC * (c + 1), :]
        first = c % CPB == 0
        for e in (V, S, G, T):
            e.wait(b.done)
        stats = layernorm_stats(K, b, x4, TPC, K.x_ready(c))
        yield
        xn_ready = layernorm_apply(K, b, x4, b.xn, TPC, stats)
        stats = layernorm_stats(K, b, b.xn, TPC, xn_ready)
        yield
        h_ready = layernorm_apply(K, b, b.xn, b.hh, TPC, stats)
        K.prefetch()
        yield
        col = start_column("xa", b.xa, c, 0.0)
        xa_ready = to_channels(b.hh, b.xa, G1, B1, h_ready, None)
        yield
        save_column("xa", b.xa[:, :, CH:], c, list(xa_ready))
        xa_ready.append(col)
        begun = {}
        for kind, to in (("k", b.m0), ("v", b.ea), ("r", b.eb)):
            begun[kind] = mix_before(b.xa, to, kind, xa_ready, None)
        yield
        mixes = {}
        for kind, to in (("k", b.m0), ("v", b.ea), ("r", b.eb)):
            mixes[kind] = mix_now(b.xa, to, kind, [begun[kind]] + xa_ready)
        K.prefetch()
        yield
        proj, made = {}, []
        for kind, m, dst in (("k", b.m0, b.k), ("v", b.ea, b.v), ("r", b.eb, b.sr)):
            proj[kind] = []
            for f, d, to, of, mark in made:
                f.free = do(S, lambda: S.e.activation(to[:, d, :], f.ap[:], ACT.Copy), mark)
                proj[of].append(f.free)
            made = []
            for d in range(DT):
                f = for_products()
                T.wait(mixes[kind], f.free)
                for k in range(DT):
                    T.did(T.e.matmul(f.ap[:], w[kind][:, k, d * P:(d + 1) * P], m[:, k, :],
                                     start=k == 0, stop=k == DT - 1))
                made.append((f, d, dst, kind, T.own()))
            yield
        read = T.own()
        for f, d, to, of, mark in made:
            f.free = do(S, lambda: S.e.activation(to[:, d, :], f.ap[:], ACT.Copy), mark)
            proj[of].append(f.free)
        K.prefetch(2)
        kw_ready = [do(V, lambda: V.e.tensor_scalar(b.kw[:, d, :], b.k[:, d, :], vec[:, d, WD:WD + 1], None, ALU.add),
                       proj["k"]) for d in range(DT)]
        col = start_column("mx", b.mx, c, NEG)
        for d in range(DT):
            mx = do(V, lambda: V.e.tensor_tensor_scan(
                b.mx[:, d, 1:], vec[:, d, WD:WD + 1].to_broadcast([P, CH]), b.kw[:, d, :],
                b.mx[:, d, 0:1], ALU.add, ALU.max), col, kw_ready)
        save_column("mx", b.mx[:, :, CH:], c, mx)
        d_a = do(V, lambda: V.e.tensor_tensor(b.ea[:], b.mx[:, :, 0:CH], b.mx[:, :, 1:], ALU.subtract), mx, read)
        d_b = do(V, lambda: V.e.tensor_tensor(b.eb[:], b.kw[:], b.mx[:, :, 1:], ALU.subtract), mx, read)
        yield
        for d in range(DT):
            e_a = do(S, lambda: S.e.activation(b.ea[:, d, :], b.ea[:, d, :], ACT.Exp, bias=vec[:, d, WD:WD + 1]), d_a)
        e_b = do(S, lambda: S.e.activation(b.eb[:], b.eb[:], ACT.Exp), d_b)
        yield
        for d in range(DT):
            r_ready = do(V, lambda: V.e.tensor_tensor_scan(
                b.rr[:, d, :], b.ea[:, d, :], b.eb[:, d, :],
                0.0 if first else carry["rr"][(c - 1) % 2][:, d, :], ALU.mult, ALU.add),
                e_a, e_b, prev.get("rr"))
        save_column("rr", b.rr[:, :, CH - 1:CH], c, r_ready)
        yield
        ln_r = do(S, lambda: S.e.activation(b.eb[:], b.rr[:], ACT.Ln), r_ready)
        yield
        col = start_column("pp", b.pp, c, NEG)
        pp = do(V, lambda: V.e.tensor_tensor(b.pp[:, :, 1:], b.eb[:], b.mx[:, :, 1:], ALU.add), ln_r, col)
        save_column("pp", b.pp[:, :, CH:], c, pp)
        d1 = do(V, lambda: V.e.tensor_tensor(b.d1[:], b.pp[:, :, 0:CH], b.k[:], ALU.subtract), pp)
        neg = do(V, lambda: V.e.tensor_scalar(b.ea[:], b.d1[:], 0.0, None, ALU.min), d1)
        pos = do(V, lambda: V.e.tensor_scalar(b.kw[:], b.d1[:], 0.0, None, ALU.max), d1)
        yield
        e1u = do(S, lambda: S.e.activation(b.ea[:], b.ea[:], ACT.Exp), neg)
        e2u = do(S, lambda: S.e.activation(b.kw[:], b.kw[:], ACT.Exp, scale=-1.0), pos)
        yield
        bv = do(G, lambda: G.e.tensor_tensor(b.kw[:], b.kw[:], b.v[:], ALU.mult), e2u, proj["v"])
        yield
        col = start_column("aa", b.aa, c, 0.0)
        for d in range(DT):
            aa = do(V, lambda: V.e.tensor_tensor_scan(
                b.aa[:, d, 1:], b.ea[:, d, :], b.kw[:, d, :], b.aa[:, d, 0:1], ALU.mult, ALU.add), e1u, bv, col)
        save_column("aa", b.aa[:, :, CH:], c, aa)
        yield
        for d in range(DT):
            S.wait(ln_r, d1)
            g1 = S.did(S.e.activation(b.eb[:, d, :], b.d1[:, d, :], ACT.Sigmoid, bias=nu[:, d:d + 1]))
            g2 = do(S, lambda: S.e.activation(b.rr[:, d, :], b.d1[:, d, :], ACT.Sigmoid,
                                              bias=vec[:, d, U:U + 1], scale=-1.0), prev["rr"])
        sr = do(S, lambda: S.e.activation(b.sr[:], b.sr[:], ACT.Sigmoid), proj["r"])
        yield
        ya = do(G, lambda: G.e.tensor_tensor(b.eb[:], b.eb[:], b.aa[:, :, 0:CH], ALU.mult), g1, aa)
        yb = do(V, lambda: V.e.tensor_tensor(b.rr[:], b.rr[:], b.v[:], ALU.mult), g2)
        yield
        y = do(V, lambda: V.e.tensor_tensor(b.rr[:], b.rr[:], b.eb[:], ALU.add), ya, yb)
        gated = do(V, lambda: V.e.tensor_tensor(b.rr[:], b.rr[:], b.sr[:], ALU.mult), y, sr)
        yield
        for i in range(0, TPC, 2):
            f = for_transposes()
            T.wait(gated, f.free)
            for j in range(2):
                for k in range(DT):
                    T.did(T.e.transpose(f.ap[:, j * D + k * P:j * D + (k + 1) * P],
                                        b.rr[:, k, (i + j) * P:(i + j + 1) * P], K.ident[:]))
            x1 = f.free = do(V, lambda: V.e.tensor_tensor(
                b.xn[:, i:i + 2, :], b.xn[:, i:i + 2, :], f.ap[:].rearrange("p (a c) -> p a c", a=2), ALU.add), T.own())
        yield
        grown = do(V, lambda: V.e.tensor_tensor(x4, x4, b.xn[:], ALU.add), x1)
        stats = layernorm_stats(K, b, b.xn, TPC, x1)
        yield
        h_ready = layernorm_apply(K, b, b.xn, b.hh, TPC, stats)
        yield
        mx_free = [pp, d_a, d_b, prev["mx"]]
        col = start_column("xb", b.mx, c, 0.0, mx_free)
        xb_ready = to_channels(b.hh, b.mx, G2, B2, h_ready, mx_free)
        yield
        save_column("xb", b.mx[:, :, CH:], c, list(xb_ready))
        xb_ready.append(col)
        begun_k = mix_before(b.mx, b.m0, "ck", xb_ready, read)
        begun_r = mix_before(b.mx, b.k, "cr", xb_ready, d1)
        yield
        mk = mix_now(b.mx, b.m0, "ck", [begun_k] + xb_ready)
        mr = mix_now(b.mx, b.k, "cr", [begun_r] + xb_ready)
        yield
        made, relu, sq = {}, {}, {}
        for h in range(KH + 2):
            if h >= 2:
                sq[h - 2] = do(V, lambda: V.e.tensor_tensor(kc[:, h - 2, :], kc[:, h - 2, :], kc[:, h - 2, :], ALU.mult),
                               relu[h - 2])
            if 1 <= h <= KH:
                f, mark = made[h - 1]
                relu[h - 1] = f.free = do(S, lambda: S.e.activation(kc[:, h - 1, :], f.ap[:], ACT.Relu), mark, kc_free[0])
            if h < KH:
                f = for_products()
                T.wait(mk, f.free)
                for k in range(DT):
                    T.did(T.e.matmul(f.ap[:], w_ck[:, k, h * P:(h + 1) * P], b.m0[:, k, :],
                                     start=k == 0, stop=k == DT - 1))
                made[h] = (f, T.own())
            yield
        scr_free, gate = [None, None], {}
        for i in range(TPC + 2):
            if i >= 2:
                f, scr = made[i - 2][0], b.scr[:, i % 2, :]
                prod = f.free = do(V, lambda: V.e.tensor_tensor(scr, scr, f.ap[:, D:2 * D], ALU.mult), gate[i - 2])
                scr_free[i % 2] = do(V, lambda: V.e.tensor_tensor(x4[:, i - 2, :], x4[:, i - 2, :], scr, ALU.add), prod, grown)
            if 1 <= i <= TPC:
                f, mark = made[i - 1]
                gate[i - 1] = do(S, lambda: S.e.activation(b.scr[:, (i - 1) % 2, :], f.ap[:, 0:D], ACT.Sigmoid),
                                 mark, scr_free[(i - 1) % 2])
            if i < TPC:
                f = for_output()
                T.wait(mr, sq[KH - 1], f.free)
                for k in range(DT):
                    T.did(T.e.matmul(f.ap[:, 0:D], b.k[:, k, i * P:(i + 1) * P], w["cr"][:, k, :],
                                     start=k == 0, stop=k == DT - 1))
                for h in range(KH):
                    T.did(T.e.matmul(f.ap[:, D:2 * D], kc[:, h, i * P:(i + 1) * P], w_cv[:, h, :],
                                     start=h == 0, stop=h == KH - 1))
                made[i] = (f, T.own())
                kc_free[0] = T.own()
            yield
        b.done = [V.own(), S.own(), G.own(), T.own()]

    run_lanes(chunk, NC, skew=17)
    K.x_is_ready()
    M.free()


def expert_tiles(K, M, R, E, F, w_gu, w_d, routed, scattered, rms=False):
    V, S, G, T, Q = K.V, K.S, K.G, K.T, K.Q
    FK = F // P
    n_tiles = 2 * NT + E
    wide = 2 * F > CH
    RING = 4
    rows = [M.sb(f"rows{i}", [P, D]) for i in range(RING)]
    xT = [M.sb(f"rowsT{i}", [P, DT, P]) for i in range(2)]
    act = [M.sb(f"act{i}", [P, F]) for i in range(2)]
    mid_ = [M.sb(f"mid{i}", [P, F]) for i in range(2)]
    midT = [M.sb(f"midT{i}", [P, FK, P]) for i in range(2)]
    out = [M.sb(f"result{i}", [P, D]) for i in range(RING)]
    sq = M.sb("squares", [P, F])
    ss = [M.sb(f"sum_squares{i}", [P, 1]) for i in range(4)]
    rs = [M.sb(f"inverse_rms{i}", [P, 1]) for i in range(4)]
    if wide:
        tb = [Bank(M.ps("transposed", [P, CH]))]
        gb = [Bank(M.ps(f"gate_up{i}", [P, 2 * CH])) for i in range(2)]
        hb = [Bank(M.ps("mid_transposed", [P, CH]))]
        ob = [Bank(M.ps("result_sum", [P, CH]))]
    else:
        tb, gb, hb, ob = ([Bank(M.ps(f"{n}{i}", [P, CH])) for i in range(n_b)]
                          for n, n_b in (("transposed", 1), ("gate_up", 2), ("mid_transposed", 1), ("result_sum", 1)))
    gu_flat = w_gu[:].rearrange("p e k f -> p (e k f)")
    d_flat = w_d[:].rearrange("p e k c -> p (e k c)")
    rows_here, rows_free = {}, [None] * RING
    xT_ready, xT_free, mid_ready, mid_free, midT_ready, midT_free = {}, [None] * 2, {}, [None] * 2, {}, [None] * 2
    rs_ready, stored, expert = {}, [None] * RING, {}
    Q.wait(scattered)
    T.wait(routed)

    def load(j):
        Q.wait(rows_free[j % RING])
        rows_here[j] = K.dma(Q, rows[j % RING][:], K.sorted_in[j * P:(j + 1) * P, :], f"rows{j % RING}")

    def transpose(j):
        b = tb[j % len(tb)]
        T.wait(rows_here[j], b.free)
        for k in range(DT):
            T.did(T.e.transpose(b.ap[:, k * P:(k + 1) * P], rows[j % RING][:, k * P:(k + 1) * P], K.ident[:]))
        rows_free[j % RING] = T.own()
        b.free = xT_ready[j] = do(S, lambda: S.e.activation(
            xT[j % 2][:], b.ap[:, 0:DT * P].rearrange("p (k q) -> p k q", k=DT), ACT.Copy), T.own(), xT_free[j % 2])

    def up(j):
        b = gb[j % len(gb)]
        expert[j] = T.e.value_load(R.tile_expert[0:1, j:j + 1], min_val=0, max_val=E - 1)
        T.wait(xT_ready[j], b.free)
        for at in range(0, 2 * F, CH):
            n = min(CH, 2 * F)
            for k in range(DT):
                T.did(T.e.matmul(b.ap[:, at:at + n], xT[j % 2][:, k, :],
                                 gu_flat[:, bass.ds(expert[j] * (DT * 2 * F) + (k * 2 * F + at), n)],
                                 start=k == 0, stop=k == DT - 1))
        xT_free[j % 2] = T.own()
        gate = do(S, lambda: S.e.activation(act[j % 2][:], b.ap[:, 0:F], ACT.Silu), T.own(), mid_ready.get(j - 2))
        b.free = mid_ready[j] = do(V, lambda: V.e.tensor_tensor(
            mid_[j % 2][:], act[j % 2][:], b.ap[:, F:2 * F], ALU.mult), gate, mid_free[j % 2], rs_ready.get(j - 2))
        if rms:
            s4 = ss[j % 4]
            sqd = do(S, lambda: S.e.activation(sq[:], mid_[j % 2][:], ACT.Square, accum_out=s4[:]),
                     mid_ready[j], rs_ready.get(j - 4), S.own())
            ve = do(V, lambda: V.e.tensor_scalar(s4[:], s4[:], 1.0 / F, 1e-6, ALU.mult, ALU.add), sqd)
            rs_ready[j] = do(G, lambda: G.e.tensor_tensor(rs[j % 4][:], s4[:], K.neghalf[:, 0:1], ALU.pow),
                             ve, stored_mark.get(j - 4))

    stored_mark = {}

    def turn(j):
        b = hb[j % len(hb)]
        T.wait(mid_ready[j], b.free)
        for k in range(FK):
            T.did(T.e.transpose(b.ap[:, k * P:(k + 1) * P], mid_[j % 2][:, k * P:(k + 1) * P], K.ident[:]))
        mid_free[j % 2] = T.own()
        b.free = midT_ready[j] = do(V, lambda: V.e.tensor_copy(
            midT[j % 2][:], b.ap[:, 0:F].rearrange("p (k q) -> p k q", k=FK)), T.own(), midT_free[j % 2])

    def down(j):
        b = ob[j % len(ob)]
        T.wait(midT_ready[j], b.free)
        for k in range(FK):
            T.did(T.e.matmul(b.ap[:, 0:D], midT[j % 2][:, k, :],
                             d_flat[:, bass.ds(expert[j] * (FK * D) + k * D, D)], start=k == 0, stop=k == FK - 1))
        midT_free[j % 2] = T.own()
        o = out[j % RING]
        if rms:
            b.free = do(S, lambda: S.e.activation(o[:], b.ap[:, 0:D], ACT.Copy, scale=rs[j % 4][:]),
                        T.own(), stored[j % RING], rs_ready[j])
        else:
            b.free = do(S, lambda: S.e.activation(o[:], b.ap[:, 0:D], ACT.Copy), T.own(), stored[j % RING])
        stored_mark[j] = b.free
        Q.wait(b.free)
        stored[j % RING] = K.dma(Q, K.sorted_out[j * P:(j + 1) * P, :], o[:], f"store{j % RING}")

    for j in range(RING - 1):
        load(j)
    for i in range(n_tiles + 3):
        if i < n_tiles:
            transpose(i)
        if 0 <= i - 1 < n_tiles:
            up(i - 1)
        if 0 <= i - 2 < n_tiles:
            turn(i - 2)
        if 0 <= i - 3 < n_tiles:
            down(i - 3)
        if i + RING - 1 < n_tiles:
            load(i + RING - 1)
    K.sorted_read = [rows_here[j] for j in range(n_tiles - RING, n_tiles)]
    return stored


def ssm1_stage(K, W):
    V, S, G, T, Q = K.V, K.S, K.G, K.T, K.Q
    X, E, F, NS = K.X, 4, 512, 16
    MY = Memory(K)
    y_rows = MY.sb("y_rows", [P, NT, D])
    norm_w = MY.sb("norm_w", [P, D])
    M = Memory(K)
    R = Routing(K, M, E)
    M0, M = M, Memory(K)
    K.start_combine(M)
    ln_buffers(M, TPC)
    w_delta = M.sb("w_delta", [P, DT, D])
    w_bc = M.sb("w_bc", [P, DT, 3, 2 * NS])
    w_router = M.sb("w_router", [P, DT, E])
    vec = M.sb("ssm_vectors", [P, DT, 2])
    A = M.sb("A", [P, DT, NS])
    sel = M.sb("selectors", [96, 32, P], BF16)
    K.dma(Q, w_delta[:], W["L1_attn_a_W_delta"].rearrange("(k p) e -> p k e", p=P), "weights")
    K.dma(Q, w_router[:], W["L1_attn_a_W_router"].rearrange("(k p) e -> p k e", p=P), "weights")
    for j in range(3):
        K.dma(Q, w_bc[:, :, j, 0:NS], W["L1_attn_a_W_B"].rearrange("(k p) e -> p k e", p=P), "weights")
        K.dma(Q, w_bc[:, :, j, NS:], W["L1_attn_a_W_C"].rearrange("(k p) e -> p k e", p=P), "weights")
    K.dma(Q, vec[:], W["ssm_vectors"], "weights")
    K.dma(Q, A[:], W["L1_attn_a_A_log"].rearrange("(k p) n -> p k n", p=P), "weights")
    K.dma(Q, norm_w[:], W["L1_norm_w"], "weights")
    loaded = K.dma(Q, sel[:], W["const_selectors"], "weights")
    S.wait(loaded)
    V.wait(S.did(S.e.activation(A[:], A[:], ACT.Exp)))
    a_ready = V.did(V.e.tensor_scalar(A[:], A[:], -1.0, None, ALU.mult))
    for e in (V, S, G, T):
        e.wait(loaded, a_ready)

    sc = Scan(K, M, DT, NS)
    xn = M.sb("xn", [P, TPC, D])
    xT = [M.sb(f"xT{i}", [P, DT, CH]) for i in range(2)]
    dt = [M.sb(f"dt{i}", [P, DT, CH]) for i in range(2)]
    dtu = [M.sb(f"dtu{i}", [P, DT, CH]) for i in range(2)]
    BC3 = [M.sb(f"BC3_{i}", [96, CH], BF16) for i in range(2)]
    y = [M.sb(f"y{i}", [P, DT, CH]) for i in range(2)]
    rest, ab = M.sb("bc_rest", [96, CH]), M.sb("softplus", [P, DT, CH])
    stat = M.sb("stat", [P, 4])
    small = M.sb("bound", [1, 8])
    flag = [M.sb(f"clip_flag{i}", [1, 1], I32) for i in range(2)]
    state = M.sb("clipped_state", [P, DT])
    pick = rotation([Bank(M.ps(f"front{i}", [P, CH])) for i in range(2)])
    st = {"ready": [None, None], "done": [None, None], "xn_free": None,
          "y_read": [None, None]}
    V.did(V.e.memset(stat[:], 0.0))
    V.did(V.e.memset(small[:], 0.0))
    V.wait(V.own())

    def front(c):
        r = c % 2
        V.wait(st["done"][r])
        x4 = X[:, TPC * c:TPC * (c + 1), :]
        yield
        stats = layernorm_stats(K, M, x4, TPC, K.x_ready(c))
        yield
        yield
        V.wait(st["xn_free"])
        normed = layernorm_apply(K, M, x4, xn, TPC, stats)
        yield
        for k in range(DT):
            f = pick()
            T.wait(normed, f.free)
            for i in range(TPC):
                T.did(T.e.transpose(f.ap[:, i * P:(i + 1) * P], xn[:, i, k * P:(k + 1) * P], K.ident[:]))
            st["xn_free"] = made = T.own()
            yield
            f.free = x_here = do(S, lambda: S.e.activation(xT[r][:, k, :], f.ap[:], ACT.Copy), made, st["done"][r])
            yield
        f = pick()
        T.wait(x_here, f.free)
        for k in range(DT):
            T.did(T.e.matmul(f.ap[0:96, :], w_bc[:, k, :, :].rearrange("p a b -> p (a b)"), xT[r][:, k, :],
                             start=k == 0, stop=k == DT - 1))
        made = T.own()
        yield
        max_b = do(V, lambda: V.e.tensor_reduce(stat[0:NS, 2:3], f.ap[0:NS, :], AX.X, ALU.max,
                                                apply_absolute_value=True), made, V.own(), st.get("stat_read"))
        f.free = split_done = split3(K, f.ap, BC3[r], rest, [made, st["done"][r], V.own()])
        yield
        for d in range(DT):
            f = pick()
            T.wait(f.free)
            for k in range(DT):
                T.did(T.e.matmul(f.ap[:], w_delta[:, k, d * P:(d + 1) * P], xT[r][:, k, :],
                                 start=k == 0, stop=k == DT - 1))
            made = T.own()
            yield
            K.prefetch(2)
            a1 = do(S, lambda: S.e.activation(ab[:, d, :], f.ap[:], ACT.Abs, bias=vec[:, d, 0:1]), made, st.get("ab_free"))
            f.free = do(V, lambda: V.e.tensor_scalar(dt[r][:, d, :], f.ap[:], vec[:, d, 0:1], 0.0, ALU.add, ALU.max), a1)
            yield
        e1 = do(S, lambda: S.e.activation(ab[:], ab[:], ACT.Exp, scale=-1.0), S.own())
        e2 = do(S, lambda: S.e.activation(ab[:], ab[:], ACT.Ln, bias=1.0), e1)
        yield
        yield
        made_dt = do(V, lambda: V.e.tensor_tensor(dt[r][:], dt[r][:], ab[:], ALU.add), e2, V.own())
        made_dtu = do(G, lambda: G.e.tensor_tensor(dtu[r][:], dt[r][:], xT[r][:], ALU.mult), made_dt)
        yield
        yield
        s1 = do(V, lambda: V.e.tensor_reduce(stat[:, 0:1], dt[r][:], AX.XY, ALU.max), made_dt, max_b)
        s2 = do(V, lambda: V.e.tensor_reduce(ab[:, :, 0], dtu[r][:], AX.X, ALU.add, apply_absolute_value=True), made_dtu)
        s3 = do(V, lambda: V.e.tensor_reduce(stat[:, 1:2], ab[:, :, 0], AX.X, ALU.max), s2)
        f = pick()
        T.wait(s1, s3, f.free)
        for j in range(3):
            T.did(T.e.matmul(f.ap[0:1, j * P:(j + 1) * P], stat[:, j:j + 1], K.ident[:], start=True, stop=True))
        st["ab_free"] = s3
        made = st["stat_read"] = T.own()
        yield

        def v(inst):
            V.wait(V.did(inst))
        V.wait(made)
        v(V.e.tensor_reduce(small[:, 0:3], f.ap[0:1, 0:3 * P].rearrange("p (a b) -> p a b", a=3), AX.X, ALU.max))
        f.free = V.own()
        v(V.e.tensor_tensor(small[:, 3:5], small[:, 0:2], small[:, 2:3].to_broadcast([1, 2]), ALU.mult))
        if c % CPB:
            v(V.e.tensor_tensor(small[:, 5:6], small[:, 5:6], small[:, 4:5], ALU.add))
        else:
            v(V.e.tensor_copy(small[:, 5:6], small[:, 4:5]))
        v(V.e.tensor_scalar(small[:, 6:7], small[:, 3:4], BAR_B_MAX * 0.99, None, ALU.is_gt))
        v(V.e.tensor_scalar(small[:, 7:8], small[:, 5:6], H_MAX * 0.99, None, ALU.is_gt))
        v(V.e.tensor_tensor(small[:, 6:7], small[:, 6:7], small[:, 7:8], ALU.add))
        flagged = do(V, lambda: V.e.tensor_copy(flag[r][:], small[:, 6:7]))
        st["ready"][r] = [made_dtu, made_dt, split_done]
        st["flag"] = flagged
        yield

    regs = {}

    def clipped(sc, r, n, c):
        if n == 0:
            V.wait(st["flag"])
            regs[c] = V.e.value_load(flag[c % 2][0:1, 0:1], min_val=0, max_val=2)
        q = c % 2
        with V.e.If(regs[c] > 0):
            V.e.drain()
            for d in range(DT):
                V.e.tensor_tensor(sc.dBu[r][:, d, :], dt[q][:, d, :], sc.Bb[r][:], ALU.mult)
            V.e.drain()
            V.e.tensor_scalar(sc.dBu[r][:], sc.dBu[r][:], BAR_B_MAX, -BAR_B_MAX, ALU.min, ALU.max)
            V.e.drain()
            V.e.tensor_tensor(sc.dBu[r][:], sc.dBu[r][:], xT[q][:], ALU.mult)
            if c % CPB:
                V.e.tensor_copy(state[:], sc.carry[:, n, :])
            else:
                V.e.memset(state[:], 0.0)
            with V.e.Fori(0, CH) as t:
                V.e.drain()
                V.e.tensor_tensor(state[:], state[:], sc.dA[r][:, :, bass.ds(t, 1)], ALU.mult)
                V.e.drain()
                V.e.tensor_tensor(state[:], state[:], sc.dBu[r][:, :, bass.ds(t, 1)], ALU.add)
                V.e.drain()
                V.e.tensor_scalar(state[:], state[:], H_MAX, -H_MAX, ALU.min, ALU.max)
                V.e.drain()
                V.e.tensor_copy(sc.dBu[r][:, :, bass.ds(t, 1)], state[:])
            V.e.drain()

    def take_y(c):
        r = c % 2
        V.wait(sc.summed[(c + 1) * NS - 1], st["y_read"][r])
        for d in range(DT):
            V.did(V.e.scalar_tensor_tensor(y[r][:, d, :], xT[r][:, d, :], vec[:, d, 1:2], sc.y[d][:],
                                           ALU.mult, ALU.add))
        sc.y_free = st["done"][r] = V.own()

    def back(c):
        r = c % 2
        y_made = st["done"][r]
        for i in range(0, TPC, 2):
            f = pick()
            T.wait(f.free, y_made)
            for j in range(2):
                for k in range(DT):
                    T.did(T.e.transpose(f.ap[:, j * D + k * P:j * D + (k + 1) * P],
                                        y[r][:, k, (i + j) * P:(i + j + 1) * P], K.ident[:]))
            made = T.own()
            yield
            f.free = do(S, lambda: S.e.activation(
                y_rows[:, TPC * c + i:TPC * c + i + 2, :], f.ap[:].rearrange("p (a c) -> p a c", a=2), ACT.Copy), made)
            yield
        for i in range(TPC):
            for k in range(DT):
                T.did(T.e.matmul(R.logit(TPC * c + i), y[r][:, k, i * P:(i + 1) * P], w_router[:, k, :],
                                 start=k == 0, stop=k == DT - 1))
        st["y_read"][r] = T.own()
        yield
        yield

    run_scan(sc, front, take_y, back, lambda c: (dt[c % 2], dtu[c % 2][:], BC3[c % 2][:], A, sel, st["ready"][c % 2]),
             clipped)
    M.free()
    M = M0
    w_gu = M.sb("w_gate_up", [P, E, DT, 2 * F])
    w_d = M.sb("w_down", [P, E, F // P, D])
    gain = M.sb("inner_gain", [P, E, F // P])
    K.dma(Q, gain[:], W["L1_inner_gain"], "weights")
    for e in range(E):
        for j, n in enumerate(("Wg", "Wu")):
            K.dma(Q, w_gu[:, e, :, j * F:(j + 1) * F], W["L1_attn_a_" + n][e].rearrange("(k p) f -> p k f", p=P), "weights")
        loaded = K.dma(Q, w_d[:, e, :, :], W["L1_attn_a_Wd"][e].rearrange("(k p) c -> p k c", p=P), "weights")
    routed = R.run(T.own(), normalise=True)
    scattered = R.scatter(y_rows, routed)
    V.wait(loaded)
    folded = V.did(V.e.tensor_tensor(w_d[:].rearrange("p e k c -> p (e k) c"), w_d[:].rearrange("p e k c -> p (e k) c"),
                                     last(gain[:].rearrange("p e k -> p (e k)"), D), ALU.mult))
    T.wait(loaded, folded)
    expert_tiles(K, M, R, E, F, w_gu, w_d, routed, scattered, rms=True)
    K.owed = lambda K, M, ring: NormedCombine(K, M, y_rows, norm_w, ring)
    K.x_is_ready()
    M.free()
    K.kept = (MY, y_rows)


def moe1_stage(K, W):
    V, S, G, T, Q = K.V, K.S, K.G, K.T, K.Q
    X, E, F, FS = K.X, 16, 128, 256
    M = Memory(K)
    R = Routing(K, M, E)
    lns = [Statistics(M, i) for i in range(2)]
    MY, xn = K.kept or (None, M.sb("xn", [P, NT, D]))
    K.kept = None
    K.start_combine(M)
    wr = M.sb("w_router", [P, DT, E])
    w_s = M.sb("w_shared_gate_up", [P, DT, 2 * FS])
    w_sd = M.sb("w_shared_down", [P, FS // P, D])
    w_gu = M.sb("w_gate_up", [P, E, DT, 2 * F])
    w_d = M.sb("w_down", [P, E, 1, D])
    rows_of = lambda n: W["L1_ffn_" + n].rearrange("(k p) e -> p k e", p=P)
    K.dma(Q, wr[:], rows_of("Wr"), "weights")
    K.dma(Q, w_s[:, :, 0:FS], rows_of("Sg"), "weights")
    K.dma(Q, w_s[:, :, FS:], rows_of("Su"), "weights")
    shared_here = K.dma(Q, w_sd[:], rows_of("Sd"), "weights")
    for j, n in enumerate(("Wg", "Wu")):
        for e in range(E):
            K.dma(Q, w_gu[:, e, :, j * F:(j + 1) * F], W["L1_ffn_" + n][e].rearrange("(k p) f -> p k f", p=P), "experts")
    experts_here = K.dma(Q, w_d[:, :, 0, :], W["L1_ffn_Wd"].rearrange("e p c -> p e c"), "experts")
    MS = Memory(K)
    xT = [MS.sb(f"xT{i}", [P, DT, CH]) for i in range(NC)]
    hs = [MS.sb(f"shared_act{i}", [P, FS // P, CH]) for i in range(2)]
    hm = [MS.sb(f"shared_mid{i}", [P, FS // P, CH]) for i in range(2)]
    copies = MS.sb("shared_copies", [P, 2, CH])
    sb_ = [Bank(MS.ps(f"shared{i}", [P, CH])) for i in range(4)]
    T.wait(shared_here)
    turn = rotation(sb_)
    stats = layernorm_stats(K, lns[0], X[:, 0:TPC, :], TPC, K.x_ready(0))
    for c in range(NC):
        r = c % 2
        tiles = slice(TPC * c, TPC * (c + 1))
        if c + 1 < NC:
            ahead = layernorm_stats(K, lns[1 - r], X[:, TPC * (c + 1):TPC * (c + 2), :], TPC, K.x_ready(c + 1))
        normed = layernorm_apply(K, lns[r], X[:, tiles, :], xn[:, tiles, :], TPC, stats)
        stats = ahead
        T.wait(channel_major(K, xn[:, tiles, :], xT[c], turn, normed, None))
        for i in range(TPC):
            for k in range(DT):
                T.did(T.e.matmul(R.logit(TPC * c + i), xT[c][:, k, i * P:(i + 1) * P], wr[:, k, :],
                                 start=k == 0, stop=k == DT - 1))
    logits_made = T.own()
    act_free, mid_free, copy_free = [None, None], [None, None], [None, None]

    def shared(c, E):
        r = c % 2

        def readable(bank, to, made):
            if E is V:
                return bank.ap[:], made
            bank.free = do(S, lambda: S.e.activation(copies[:, to, :], bank.ap[:], ACT.Copy), made, copy_free[to])
            return copies[:, to, :], bank.free

        for f in range(FS // P):
            made = []
            for j in range(2):
                b = turn()
                T.wait(b.free)
                for k in range(DT):
                    T.did(T.e.matmul(b.ap[:], w_s[:, k, j * FS + f * P:j * FS + (f + 1) * P], xT[c][:, k, :],
                                     start=k == 0, stop=k == DT - 1))
                made.append((b, T.own()))
            (gb, g_made), (ub, u_made) = made
            gb.free = gate = do(S, lambda: S.e.activation(hs[r][:, f, :], gb.ap[:], ACT.Silu), g_made, act_free[r])
            up, up_made = readable(ub, f, u_made)
            mid_made = do(E, lambda: E.e.tensor_tensor(hm[r][:, f, :], hs[r][:, f, :], up, ALU.mult),
                          gate, up_made, mid_free[r])
            if E is V:
                ub.free = mid_made
            copy_free[f] = mid_made
        act_free[r] = mid_made
        for i in range(0, TPC, 2):
            b = turn()
            T.wait(b.free, mid_made)
            for j in range(2):
                for f in range(FS // P):
                    T.did(T.e.matmul(b.ap[:, j * D:(j + 1) * D], hm[r][:, f, (i + j) * P:(i + j + 1) * P], w_sd[:, f, :],
                                     start=f == 0, stop=f == FS // P - 1))
            xt = X[:, TPC * c + i:TPC * c + i + 2, :]
            add, add_made = readable(b, i // 2, T.own())
            added = do(E, lambda: E.e.tensor_tensor(xt, xt, add.rearrange("p (a c) -> p a c", a=2), ALU.add), add_made)
            if E is V:
                b.free = added
            copy_free[i // 2] = added
        mid_free[r] = T.own()

    routed = R.run(logits_made, beside=[lambda: shared(0, G), lambda: shared(1, G)])
    scattered = R.scatter(xn, routed)
    for c in range(2, NC):
        shared(c, V)
    MS.free()
    T.wait(experts_here)
    expert_tiles(K, M, R, E, F, w_gu, w_d, routed, scattered)
    K.x_is_ready()
    K.owed = lambda K, M, ring: Combine(K, M, K.X, ring)
    M.free()
    if MY is not None:
        MY.free()


def attention_stage(K, W):
    V, S, G, T, Q = K.V, K.S, K.G, K.T, K.Q
    X = K.X
    HD, HU, DC = 16, 8, 64
    KT = L // P
    Q_PARTS, K_PARTS = (0, 0, 1, 0, 2, 1), (0, 1, 0, 2, 0, 1)
    ROWS = 6 * HD
    M = Memory(K)
    K.start_combine(M, ring=2)
    ln_buffers(M, TPC)
    w = {}
    for n, rows, c in (("wq", D, DC), ("wkv", D, DC), ("wqr", D, P), ("wqr_turned", D, P), ("wkr", D, P),
                       ("wkr_turned", D, P), ("wo", D, D)):
        w[n] = M.sb("w_" + n, [P, DT, c])
        K.dma(Q, w[n][:], W["attn_" + n].rearrange("(k p) c -> p k c", p=P), "weights")
    for n, c in (("wqc", P), ("wkc", P), ("wv", D)):
        w[n] = M.sb("w_" + n, [DC, c])
        K.dma(Q, w[n][:], W["attn_" + n], "weights")
    b64 = M.sb("latent_biases", [DC, 2])
    b128 = M.sb("biases", [P, 6])
    bv, bo = M.sb("bv", [P, D]), M.sb("bo", [P, D])
    cos, sin = M.sb("cos", [P, L]), M.sb("sin", [P, L])
    ident_bf = M.sb("ident_bf", [P, P], BF16)
    mask_qk, mask_kq = M.sb("mask_qk", [P, P], BF16), M.sb("mask_kq", [P, P], BF16)
    for to, n in ((b64, "attn_b64"), (b128, "attn_b128"), (bv, "attn_bv"), (bo, "attn_bo"), (cos, "const_cos"),
                  (sin, "const_sin"), (ident_bf, "const_ident_bf"), (mask_qk, "const_mask_qk"),
                  (mask_kq, "const_mask_kq")):
        loaded = K.dma(Q, to[:], W[n], "weights")
    for e in (V, S, G, T):
        e.wait(loaded)
    xT = M.sb("xT", [P, DT, L])
    latent = {"q": M.sb("latent_q", [DC, L]), "k": M.sb("latent_k", [DC, L])}
    pre = M.sb("pre_gelu", [P, L])
    full = M.sb("activated", [P, L])
    xn = full[:].rearrange("p (a c) -> p a c", a=TPC)
    parts = {n: M.sb("parts_" + n, [P, 3, L], BF16) for n in "qk"}
    QS = [M.sb(f"queries{i}", [ROWS + 3, HU, L], BF16) for i in range(2)]
    KS = [M.sb(f"keys{i}", [ROWS + 3, HU, L], BF16) for i in range(2)]
    V1 = [M.sb(f"values{i}", [P, KT, HU, 32]) for i in range(2)]
    mx = M.sb("maxima", [P, KT, HU, 2])
    mn = M.sb("minus_max", [P, KT * HU])
    mT = M.sb("max_rows", [KT * HU, P])
    mP = M.sb("max_parts", [KT * HU, 3, P], BF16)
    PT = [M.sb(f"weights_T{i}", [P, 4, CH]) for i in range(2)]
    oT = M.sb("out_T", [P, CH])
    rec = M.sb("reciprocal", [P, 4, 4])
    O = M.sb("out_rows", [P, KT, D])
    oTT, oTT_free = [M.sb(f"out_channels{i}", [P, DT, P]) for i in range(2)], [None, None]
    dram = {n: K.nc.dram_tensor(f"parts_of_{n}", [3, P, L], BF16, kind="Internal").ap() for n in "qk"}
    dram_m = K.nc.dram_tensor("parts_of_max", [3, HU, KT, P], BF16, kind="Internal").ap()
    st_ = [M.ps(f"scores_T{i}", [P, 2, CH]) for i in range(2)]
    sb2 = [Bank(M.ps(f"scores{i}", [P, CH])) for i in range(2)]
    ob, mb = Bank(M.ps("out_sum", [P, CH])), Bank(M.ps("misc", [P, CH]))
    for i in range(2):
        V.did(V.e.memset(V1[i][:], 0.0))
        ones_here = K.dma(Q, KS[i][ROWS:ROWS + 3, :, :], W["const_ones_rows"], "ones_rows")
    V.wait(V.own())
    for i in range(2):
        V.did(V.e.memset(V1[i][:, :, :, HD], 1.0))
    V.did(V.e.memset(mx[:], -1e38))
    V.wait(V.own())
    for e in (S, T, Q):
        e.wait(V.own(), ones_here)
    score_free, pt_free, pt_n = [None, None], [None, None], [0]
    o_read = [None]
    unit_done = [None, None]
    ready = {}
    st = {"staged": {"q": None, "k": None}, "mx": None, "m_stored": None, "part_free": None}

    def unit_a(u):
        b, ct, r = u // DT, u % DT, u % 2
        spare = [mb] + sb2
        turns = itertools.cycle(spare)
        if ct == 0:
            for c2 in range(CPB):
                c = b * CPB + c2
                stats = layernorm_stats(K, M, X[:, TPC * c:TPC * (c + 1), :], TPC, K.x_ready(c))
                yield
                V.wait(st.get("full_free"))
                normed = layernorm_apply(K, M, X[:, TPC * c:TPC * (c + 1), :], xn, TPC, stats)
                yield
                for k in range(DT):
                    f = next(turns)
                    T.wait(normed, f.free)
                    for i in range(TPC):
                        T.did(T.e.transpose(f.ap[:, i * P:(i + 1) * P], xn[:, i, k * P:(k + 1) * P], K.ident[:]))
                    st["full_free"] = T.own()
                    f.free = x_here = do(S, lambda: S.e.activation(xT[:, k, c2 * CH:(c2 + 1) * CH], f.ap[:], ACT.Copy),
                                         T.own(), st["part_free"])
                K.prefetch(2)
                yield
            for j, (n, wn) in enumerate((("q", "wq"), ("k", "wkv"))):
                for c2 in range(CPB):
                    f = next(turns)
                    T.wait(x_here, f.free)
                    for k in range(DT):
                        T.did(T.e.matmul(f.ap[0:DC, :], w[wn][:, k, :], xT[:, k, c2 * CH:(c2 + 1) * CH],
                                         start=k == 0, stop=k == DT - 1))
                    K.prefetch()
                    f.free = latent_here = do(S, lambda: S.e.activation(
                        latent[n][:, c2 * CH:(c2 + 1) * CH], f.ap[0:DC, :], ACT.Gelu, bias=b64[:, j:j + 1]),
                        T.own(), st["part_free"])
                yield
            T.wait(latent_here)
        for j, n in enumerate("qk"):
            if ct == 0:
                for c2 in range(CPB):
                    cs, f = slice(c2 * CH, (c2 + 1) * CH), next(turns)
                    T.wait(f.free)
                    T.did(T.e.matmul(f.ap[:], w["wqc" if n == "q" else "wkc"][:], latent[n][:, cs], start=True, stop=True))
                    f.free = made = do(S, lambda: S.e.activation(full[:, cs], f.ap[:], ACT.Gelu, bias=b128[:, j:j + 1]),
                                       T.own(), st.get("full_free"))
                yield
            else:
                for i, (wn, table, to) in enumerate((("r", cos, pre), ("r_turned", sin, full))):
                    for c2 in range(CPB):
                        cs, f = slice(c2 * CH, (c2 + 1) * CH), next(turns)
                        T.wait(f.free)
                        for k in range(DT):
                            T.did(T.e.matmul(f.ap[:], w["w" + n + wn][:, k, :], xT[:, k, cs],
                                             start=k == 0, stop=k == DT - 1))
                        bias = b128[:, 2 + 2 * j + i:3 + 2 * j + i]
                        f.free = do(V, lambda: V.e.scalar_tensor_tensor(to[:, cs], f.ap[:], bias, table[:, cs],
                                                                        ALU.add, ALU.mult), T.own(), st.get("pre_free"),
                                    st.get("full_free"))
                    yield
                summed = do(V, lambda: V.e.tensor_tensor(pre[:], pre[:], full[:], ALU.add), V.own())
                made = do(S, lambda: S.e.activation(full[:], pre[:], ACT.Gelu), summed, st.get("full_free"))
                st["pre_free"] = made
                yield
            pt = parts[n]
            p1 = do(V, lambda: V.e.tensor_copy(pt[:, 0, :], full[:]), made, st["staged"][n])
            r1 = do(V, lambda: V.e.tensor_tensor(full[:], full[:], pt[:, 0, :], ALU.subtract), p1)
            p2 = do(V, lambda: V.e.tensor_copy(pt[:, 1, :], full[:]), r1)
            r2 = do(V, lambda: V.e.tensor_tensor(full[:], full[:], pt[:, 1, :], ALU.subtract), p2)
            p3 = do(V, lambda: V.e.tensor_copy(pt[:, 2, :], full[:]), r2)
            st["full_free"] = p3
            yield
            Q.wait(p3, st.get("stacked_" + n))
            st["staged"][n] = K.dma(Q, dram[n].rearrange("a c t -> c a t"), pt[:], "stage_" + n)
            to, order = (QS[r], Q_PARTS) if n == "q" else (KS[r], K_PARTS)
            Q.wait(st["staged"][n], unit_done[r])
            for i, part in enumerate(order):
                here = K.dma(Q, to[i * HD:(i + 1) * HD, :, :], dram[n][part].rearrange("(h d) t -> d h t", d=HD),
                             f"stack_{n}{r}")
            st["stacked_" + n] = here
        for i in range(0, KT, 4):
            f = next(turns)
            T.wait(f.free)
            for j in range(4):
                T.did(T.e.matmul(f.ap[:, j * P:(j + 1) * P], latent["k"][:, (i + j) * P:(i + j + 1) * P],
                                 w["wv"][:, ct * P:(ct + 1) * P], start=True, stop=True))
            T_done = T.own()
            V.wait(T_done, unit_done[r])
            for j in range(4):
                f.free = v_ready = V.did(V.e.tensor_tensor(
                    V1[r][:, i + j, :, 0:HD], f.ap[:, j * P:(j + 1) * P].rearrange("p (h d) -> p h d", d=HD),
                    bv[:, ct * P:(ct + 1) * P].rearrange("p (h d) -> p h d", d=HD), ALU.add))
            yield
        st["part_free"] = T.own()
        for _ in range(5):
            yield
        T.wait(st["stacked_q"], st["stacked_k"])
        V.wait(st["mx"])
        all_scores = [Bank(st_[i][:, j, :]) for i in range(2) for j in range(2)] if u == 0 else []
        turns = itertools.cycle(sb2 + [mb] + all_scores)
        for h in range(HU):
            for qt in range(KT):
                for half in range(qt // 4 + 1):
                    f = next(turns)
                    n_keys = min(CH, (qt + 1) * P - half * CH)
                    diagonal = half == qt // 4
                    T.wait(f.free)
                    T.did(T.e.matmul(f.ap[:, 0:n_keys], QS[r][0:ROWS, h, qt * P:(qt + 1) * P],
                                     KS[r][0:ROWS, h, half * CH:half * CH + n_keys], start=True, stop=not diagonal))
                    if diagonal:
                        T.did(T.e.matmul(f.ap[:, n_keys - P:n_keys], ident_bf[:], mask_qk[:], start=False, stop=True))
                    f.free = do(V, lambda: V.e.tensor_reduce(mx[:, qt, h, half:half + 1], f.ap[:, 0:n_keys], AX.X, ALU.max),
                                T.own())
                    yield "short"
        neg = do(V, lambda: V.e.tensor_reduce(mn[:], mx[:], AX.X, ALU.max, negate=True), V.own(), st.get("mn_free"))
        st["mx"] = neg
        if u == 0:
            score_free[0] = score_free[1] = neg
        T.wait(neg, mb.free)
        st["mn_free"] = T.did(T.e.transpose(mb.ap[0:KT * HU, 0:P], mn[:], K.ident[:]))
        mb.free = c0 = do(V, lambda: V.e.tensor_copy(mT[:], mb.ap[0:KT * HU, 0:P]), T.own())
        m1 = do(V, lambda: V.e.tensor_copy(mP[:, 0, :], mT[:]), c0, st["m_stored"])
        r1 = do(V, lambda: V.e.tensor_tensor(mT[:], mT[:], mP[:, 0, :], ALU.subtract), m1)
        m2 = do(V, lambda: V.e.tensor_copy(mP[:, 1, :], mT[:]), r1)
        r2 = do(V, lambda: V.e.tensor_tensor(mT[:], mT[:], mP[:, 1, :], ALU.subtract), m2)
        m3 = do(V, lambda: V.e.tensor_copy(mP[:, 2, :], mT[:]), r2)
        Q.wait(m3, st.get("m_stacked"))
        for qt in range(KT):
            st["m_stored"] = K.dma(Q, dram_m[:, :, qt, :].rearrange("a h t -> h a t"),
                                   mP[qt * HU:(qt + 1) * HU, :, :], "stage_m")
        Q.wait(st["m_stored"])
        st["m_stacked"] = K.dma(Q, QS[r][ROWS:ROWS + 3, :, :], dram_m.rearrange("a h q t -> a h (q t)"), f"stack_m{r}")
        ready[u] = [v_ready, st["m_stacked"], st["stacked_q"], st["stacked_k"]]
        yield


    def unit_b(u):
        b, ct, r = u // DT, u % DT, u % 2
        T.wait(ready[u])
        steps = [(hg, qh, kt) for hg in range(2) for qh in range(2) for kt in range(4 * qh + 4)]
        later = []

        def product(hg, qh, kt, pt, slot, weighed):
            last_kt = 4 * qh + 3
            o = max(0, kt * P - qh * CH)
            T.wait(weighed, ob.free if kt == 0 else None)
            for j in range(4):
                T.did(T.e.matmul(ob.ap[32 * j:32 * j + 32, o:CH], V1[r][:, kt, hg * 4 + j, :],
                                 pt[:, j, o:CH], start=kt == 0, stop=kt == last_kt))
            pt_free[slot] = T.own()
            if kt == last_kt:
                ob.free = taken = do(S, lambda: S.e.activation(oT[:], ob.ap[:], ACT.Copy), T.own(), st.get("oT_free"))
                later.append(lambda: finish(hg, qh, taken))

        def finish(hg, qh, taken):
            T.wait(taken, mb.free)
            for t in range(4):
                T.did(T.e.transpose(mb.ap[:, t * P:(t + 1) * P], oT[:, t * P:(t + 1) * P], K.ident[:]))
            st["oT_free"] = T.own()
            v4 = mb.ap[:].rearrange("p (t h d) -> p t h d", t=4, h=4)
            rc = do(V, lambda: V.e.reciprocal(rec[:], v4[:, :, :, HD]), T.own(), st.get("rec_free"))
            h0 = (ct * HU + hg * 4) * HD
            V.wait(rc, o_read[0])
            for t in range(4):
                V.did(V.e.tensor_tensor(
                    O[:, qh * 4 + t, h0:h0 + 4 * HD].rearrange("p (h d) -> p h d", h=4), v4[:, t, :, 0:HD],
                    last(rec[:, t, :], HD), ALU.mult))
            mb.free = st["rec_free"] = V.own()

        for hg, qh, kt in steps:
            diagonal = kt * P >= qh * CH
            o = max(0, kt * P - qh * CH)
            slot = pt_n[0] % 2
            pt = PT[slot]
            pt_n[0] += 1
            for pair in range(2):
                T.wait(score_free[pair])
                for j in range(2):
                    h = hg * 4 + pair * 2 + j
                    T.did(T.e.matmul(st_[pair][:, j, o:CH], KS[r][:, h, kt * P:(kt + 1) * P],
                                     QS[r][:, h, qh * CH + o:(qh + 1) * CH], start=True, stop=not diagonal))
                    if diagonal:
                        T.did(T.e.matmul(st_[pair][:, j, o:o + P], ident_bf[:], mask_kq[:], start=False, stop=True))
                score_free[pair] = do(S, lambda: S.e.activation(
                    pt[:, 2 * pair:2 * pair + 2, o:CH], st_[pair][:, :, o:CH], ACT.Exp, scale=HD ** -0.5),
                    T.own(), pt_free[slot])
                if pair == 0:
                    yield
            weighed = S.own()
            due, later = later, []
            for issue in due:
                issue()
            later.append(lambda a=(hg, qh, kt, pt, slot, weighed): product(*a))
            yield
        while later:
            due, later = later, []
            for issue in due:
                issue()
            yield
        unit_done[r] = [T.own()]
        if ct == DT - 1:
            rows_ready, turned = V.own(), {}
            for t in range(KT + 1):
                if t < KT:
                    T.wait(mb.free, rows_ready)
                    for k in range(DT):
                        T.did(T.e.transpose(mb.ap[:, k * P:(k + 1) * P], O[:, t, k * P:(k + 1) * P], K.ident[:]))
                    o_read[0] = T.own()
                    turned[t] = mb.free = do(S, lambda: S.e.activation(
                        oTT[t % 2][:], mb.ap[:, 0:D].rearrange("p (k q) -> p k q", k=DT), ACT.Copy),
                        o_read[0], oTT_free[t % 2])
                if t:
                    q = (t - 1) % 2
                    T.wait(turned[t - 1], ob.free)
                    for k in range(DT):
                        T.did(T.e.matmul(ob.ap[:, q * D:(q + 1) * D], oTT[q][:, k, :], w["wo"][:, k, :],
                                         start=k == 0, stop=k == DT - 1))
                    oTT_free[q] = T.own()
                    xt = X[:, b * KT + t - 1, :]
                    ob.free = s1 = do(V, lambda: V.e.tensor_tensor(xt, xt, ob.ap[:, q * D:(q + 1) * D], ALU.add),
                                      T.own())
                    do(V, lambda: V.e.tensor_tensor(xt, xt, bo[:], ALU.add), s1)
                yield

    n_units = NB * DT
    SPARE = 10
    n_short = HU * sum(qt // 4 + 1 for qt in range(KT))
    b_steps = 2 * 2 * sum(4 * qh + 4 for qh in range(2)) + 2
    for _ in unit_a(0):
        pass
    for u in range(n_units):
        side = unit_a(u + 1) if u + 1 < n_units else iter(())
        step, short = None, n_short
        left = b_steps + (KT + 1 if u % DT == DT - 1 else 0)
        for _ in unit_b(u):
            take = max(1, -(-short // max(1, left - SPARE))) if step == "short" else 1
            left -= 1
            for _ in range(take):
                step = next(side, None)
            short -= take if step == "short" else 0
        for _ in side:
            pass
    K.x_is_ready()
    M.free()


STAGES = {"mamba": mamba_stage, "moe0a": moe0_stage, "moe0b": moe0_stage,
          "rwkv": rwkv_stage, "ssm1": ssm1_stage, "moe1a": moe1_stage, "moe1b": moe1_stage,
          "attn": attention_stage}
ORDER = ["mamba", "moe0a", "rwkv", "moe0b", "ssm1", "moe1a", "attn", "moe1b"]


def zero_rows(K, ready):
    K.Q.wait(ready, K.zeros_made)
    for s0 in range(0, SLOT_TILES, 8):
        for to in (K.sorted_in, K.sorted_out):
            K.dma(K.Q, to[s0 * P:(s0 + 8) * P, :].rearrange("(p a) (b c) -> p (a b) c", p=P, b=2),
                  mid(K.zeros[:], 16), "zeros")
    K.sorted_read = K.dma(K.Q, K.sorted_out[SLOTS:SLOTS + 1, :].rearrange("a (b c) -> (a b) c", b=2),
                          K.zeros[0:2, :], "zeros")


def build_program(nc, W, x_in, out, stages):
    with ExitStack() as stack:
        K = Core(nc, stack)
        K.X = stack.enter_context(nc.sbuf_tensor("residual", [P, NT, D], F32))
        K.ident = stack.enter_context(nc.sbuf_tensor("identity", [P, P], F32))
        K.neghalf = stack.enter_context(nc.sbuf_tensor("neghalf", [P, NT], F32))
        K.V.did(K.V.e.memset(K.neghalf[:], -0.5))
        half = K.V.own()
        K.dma(K.Q, K.ident[:], W["const_identity"], "x")
        x_tiles, out_tiles = (ap.rearrange("(t p) c -> p t c", p=P) for ap in (x_in, out))
        for c in range(NC):
            tiles = slice(TPC * c, TPC * (c + 1))
            queue, stream = (K.Q, "x") if c == 0 else (K.S, f"x{c}")
            K.chunk_marks[c] = K.dma(queue, K.X[:, tiles, :], x_tiles[:, tiles, :], stream)
        K.iota, K.before, K.ones_bf = (stack.enter_context(nc.sbuf_tensor(n, [P, P], t)) for n, t in
                                       (("iota", F32), ("before", BF16), ("ones_bf", BF16)))
        K.dma(K.Q, K.iota[:], W["const_iota"], "const")
        K.dma(K.Q, K.before[:], W["const_before"], "const")
        consts = K.dma(K.Q, K.ones_bf[:], W["const_ones"], "const")
        K.sorted_in = nc.dram_tensor("sorted_rows", [SLOTS, D], F32, kind="Internal").ap()
        K.sorted_out = nc.dram_tensor("sorted_results", [SLOTS + 1, D], F32, kind="Internal").ap()
        K.pick_weight, K.pick_row = ([stack.enter_context(nc.sbuf_tensor(f"{n}{i}", [P, NT], t)) for i in range(2)]
                                     for n, t in (("pick_weight", F32), ("pick_row", I32)))
        K.zeros = stack.enter_context(nc.sbuf_tensor("zeros", [P, D // 2], F32))
        K.zeros_made = K.V.did(K.V.e.memset(K.zeros[:], 0.0))
        if stages[0] != "mamba":
            zero_rows(K, None)
        for e in (K.V, K.S, K.G, K.T):
            e.wait(consts, half)
        for s in stages:
            STAGES[s](K, W)
        M = Memory(K)
        K.start_combine(M, ring=2 * TPC)
        for c in range(NC):
            tiles = slice(TPC * c, TPC * (c + 1))
            K.Q.wait(K.x_ready(c))
            K.prefetch(TPC)
            K.dma(K.Q, out_tiles[:, tiles, :], K.X[:, tiles, :], "out")
        M.free()


def prepare(inputs):
    bf16 = mybir.dt.np(BF16)
    a = {k: np.asarray(v) for k, v in inputs.items()}
    x = np.ascontiguousarray(a.pop("L0_attn_a_x").reshape(T_ALL, D))

    def cols(v):
        return v.reshape(-1, P).T

    W = {k: np.ascontiguousarray(a["L0_attn_a_" + k[10:]]) for k in
         ("L0_attn_a_W_in", "L0_attn_a_W_out", "L0_attn_a_W_dt", "L0_attn_a_W_xproj", "L0_attn_a_A_log")}
    conv = a["L0_attn_a_conv_w"][:, 0, :]
    W["mamba_vectors"] = np.ascontiguousarray(np.stack(
        [cols(conv[:, t]) for t in range(4)]
        + [cols(a["L0_attn_a_" + n]) for n in ("conv_b", "b_dt", "D", "D")], axis=-1))
    W["mamba_ln"] = np.ascontiguousarray(np.stack([cols(a["L0_attn_a_ln_g"]), cols(a["L0_attn_a_ln_b"])], axis=-1))
    W["const_identity"] = np.eye(P, dtype=np.float32)
    sel = np.zeros((96, 32, P), np.float32)
    for j in range(32):
        sel[[j, 32 + j, 64 + j], j, :] = 1
    W["const_selectors"] = sel.astype(bf16)
    iota = np.arange(P, dtype=np.float32)
    W["const_iota"] = np.tile(iota, (P, 1))
    W["const_before"] = (iota[:, None] < iota[None, :]).astype(bf16)
    W["const_ones_rows"] = np.ones((3, 8, L), bf16)
    W["const_ones"] = np.ones((P, P), bf16)
    W["L0_router_T"] = np.ascontiguousarray(a["L0_ffn_W_router"].T)
    W["L0_router_bias"] = np.ascontiguousarray(np.broadcast_to(a["L0_ffn_b_router"], (P, 8)))
    for k in ("k", "v", "r", "cr", "ck", "cv"):
        W[f"rwkv_W{k}_T"] = np.ascontiguousarray(a["L0_attn_b_W" + k].T)
    W["rwkv_vectors"] = np.ascontiguousarray(np.stack([cols(a["L0_attn_b_" + n]) for n in (
        "w", "u", "rk", "rv", "rr", "crk", "crr", "ln1_g", "ln1_b", "ln2_g", "ln2_b", "w")], axis=-1))
    W["ssm_vectors"] = np.ascontiguousarray(np.stack([cols(a["L1_attn_a_b_delta"]), cols(a["L1_attn_a_D_param"])], axis=-1))
    W["L1_norm_w"] = np.ascontiguousarray(np.broadcast_to(a["L1_attn_a_norm_w"], (P, D)))
    W["L1_inner_gain"] = np.ascontiguousarray(a["L1_attn_a_wn_exp"].reshape(4, 4, P).transpose(2, 0, 1))
    for k in ("W_delta", "W_router", "W_B", "W_C", "A_log", "Wg", "Wu", "Wd"):
        W["L1_attn_a_" + k] = a["L1_attn_a_" + k]
    for k in ("Wr", "Wg", "Wu", "Wd", "Sg", "Su", "Sd"):
        W["L1_ffn_" + k] = a["L1_ffn_" + k]
    at = {k[10:]: v for k, v in a.items() if k.startswith("L1_attn_b_")}
    for k in ("wq", "wkv", "wqr", "wkr", "wqc", "wkc", "wv", "wo"):
        W["attn_" + k] = at[k]
    turn = lambda v: np.concatenate([v[..., P // 2:], v[..., :P // 2]], axis=-1)
    W["attn_wqr_turned"], W["attn_wkr_turned"] = (np.ascontiguousarray(turn(at[k])) for k in ("wqr", "wkr"))
    W["attn_b64"] = np.ascontiguousarray(np.stack([at["bq"], at["bkv"]], axis=-1))
    W["attn_b128"] = np.ascontiguousarray(np.stack(
        [at["bqc"], at["bkc"], at["bqr"], turn(at["bqr"]), at["bkr"], turn(at["bkr"])], axis=-1))
    for k in ("bv", "bo"):
        W["attn_" + k] = np.ascontiguousarray(np.broadcast_to(at[k], (P, D)))
    inv_freq = (1.0 / np.float32(10000.0) ** (np.arange(0, P, 2, dtype=np.float32) / np.float32(P))).astype(np.float32)
    freqs = np.arange(L, dtype=np.float32)[:, None] * inv_freq[None, :]
    W["const_cos"] = np.ascontiguousarray(np.cos(np.concatenate([freqs, freqs], -1)).T.astype(np.float32))
    W["const_sin"] = np.ascontiguousarray(np.sin(np.concatenate([-freqs, freqs], -1)).T.astype(np.float32))
    W["const_ident_bf"] = np.eye(P).astype(bf16)
    above = iota[:, None] < iota[None, :]
    W["const_mask_qk"] = np.where(above, -1e30, 0).astype(bf16)
    W["const_mask_kq"] = np.where(above.T, -1e30, 0).astype(bf16)
    for k in ("L0_ffn_experts_inter", "L0_ffn_experts_out"):
        W[k] = a[k]
    return x, W


def kernel(**inputs):
    import concourse.bacc as _bacc
    from concourse.bass_utils import run_bass_kernel_spmd as _run

    nc = _bacc.Bacc("TRN2", target_bir_lowering=False, num_devices=1)
    x, W = prepare(inputs)
    arrays = {"in_x": x, **{"in_" + k: np.ascontiguousarray(v) for k, v in W.items()}}
    aps = {k: nc.dram_tensor(k, v.shape, mybir.dt.from_np(v.dtype), kind="ExternalInput").ap()
           for k, v in arrays.items()}
    out = nc.dram_tensor("out_x", (T_ALL, D), F32, kind="ExternalOutput").ap()
    build_program(nc, {k: aps["in_" + k] for k in W}, aps["in_x"], out, ORDER)
    r = _run(nc, [arrays], core_ids=[0])
    return r.results[0]["out_x"].reshape(NB, L, D)
```
